# Optimizing a Trainium2 kernel written in Bass

```python
import numpy as np
import jax
import jax.numpy as jnp

def _softmax(x, axis=-1):
    return jax.nn.softmax(x, axis=axis)

def _gelu(x):
    return jax.nn.gelu(x, approximate=True)

def _silu(x):
    return jax.nn.silu(x)

def _sigmoid(x):
    return jax.nn.sigmoid(x)

def _layernorm(x, axis=-1, eps=1e-05):
    m = jnp.mean(x, axis=axis, keepdims=True)
    v = jnp.var(x, axis=axis, keepdims=True)
    return (x - m) / jnp.sqrt(v + eps)

def _scatter_add(tgt, idx, src, axis=0):
    return tgt.at[idx].add(src)

def _segment_sum(src, seg, n):
    return jax.ops.segment_sum(src, seg, n)
kernel_name = 'mk_early_fusion_embed_d1_tok_img256_r4_089938'

def setup_inputs(seed: int=0):
    np.random.seed(seed)
    _w = jnp.asarray

    def _rec_inputs():
        import jax
        import jax.numpy as jnp
        _rk = jax.random.key(seed)
        x = 9.04603e-05 + 1.00016 * jax.random.normal(jax.random.fold_in(_rk, 1), (16, 1, 224, 224), jnp.float32)
        x_txt = jax.random.randint(jax.random.fold_in(_rk, 51), (16, 77), 0, 14, jnp.int32)
        return (x, x_txt)
    x, x_txt = _rec_inputs()

    def _L0_tok_setup():
        import jax, jax.numpy as jnp
        import numpy as np
        WS = 7
        H = W = 56
        C = 64
        NH = 8
        HD = C // NH
        SCALE = HD ** (-0.5)
        SHIFT = WS // 2
        N = WS * WS

        def _rel_pos_index():
            coords = np.stack(np.meshgrid(np.arange(WS), np.arange(WS), indexing='ij'))
            cf = coords.reshape(2, -1)
            rel = (cf[:, :, None] - cf[:, None, :]).transpose(1, 2, 0).copy()
            rel[..., 0] += WS - 1
            rel[..., 1] += WS - 1
            rel[..., 0] *= 2 * WS - 1
            return jnp.array(rel.sum(-1))

        def _attn_mask():
            img = np.zeros((H, W), np.int32)
            cnt = 0
            for h in (slice(0, -WS), slice(-WS, -SHIFT), slice(-SHIFT, None)):
                for w in (slice(0, -WS), slice(-WS, -SHIFT), slice(-SHIFT, None)):
                    cnt += 1
                    img[h, w] = cnt
            mw = img.reshape(H // WS, WS, W // WS, WS).transpose(0, 2, 1, 3).reshape(-1, N)
            diff = mw[:, None, :] - mw[:, :, None]
            return jnp.array(np.where(diff != 0, -100.0, 0.0).astype(np.float32))

        def _layernorm(x, g, b):
            m = x.mean(-1, keepdims=True)
            v = ((x - m) ** 2).mean(-1, keepdims=True)
            return (x - m) * jax.lax.rsqrt(v + 1e-05) * g + b

        def _window_partition(x):
            B = x.shape[0]
            x = x.reshape(B, H // WS, WS, W // WS, WS, C).transpose(0, 1, 3, 2, 4, 5)
            return x.reshape(-1, N, C)

        def _window_reverse(xw, B):
            x = xw.reshape(B, H // WS, W // WS, WS, WS, C).transpose(0, 1, 3, 2, 4, 5)
            return x.reshape(B, H, W, C)

        def _swin_block(x, p, shift, rpi, amask):
            B = x.shape[0]
            shortcut = x
            h = _layernorm(x, p['n1g'], p['n1b']).reshape(B, H, W, C)
            if shift > 0:
                h = jnp.roll(h, (-shift, -shift), axis=(1, 2))
            xw = _window_partition(h)
            B_ = xw.shape[0]
            qkv = (xw @ p['qkv_w'].T + p['qkv_b']).reshape(B_, N, 3, NH, HD).transpose(2, 0, 3, 1, 4)
            q, k, v = (qkv[0], qkv[1], qkv[2])
            attn = jnp.einsum('bhnd,bhmd->bhnm', q * SCALE, k)
            attn = attn + p['rpb'][rpi].transpose(2, 0, 1)[None]
            if shift > 0:
                nW = amask.shape[0]
                attn = attn.reshape(B_ // nW, nW, NH, N, N) + amask[None, :, None]
                attn = attn.reshape(B_, NH, N, N)
            attn = jax.nn.softmax(attn, axis=-1)
            o = jnp.einsum('bhnm,bhmd->bhnd', attn, v).transpose(0, 2, 1, 3).reshape(B_, N, C)
            o = o @ p['proj_w'].T + p['proj_b']
            h = _window_reverse(o, B)
            if shift > 0:
                h = jnp.roll(h, (shift, shift), axis=(1, 2))
            x = shortcut + h.reshape(B, H * W, C)
            y = _layernorm(x, p['n2g'], p['n2b'])
            y = jax.nn.gelu(y @ p['w1'].T + p['b1'], approximate=False)
            return x + y @ p['w2'].T + p['b2']
        key = jax.random.key(seed)
        ks = jax.random.split(key, 8)
        s = 0.02
        return {'x': jax.random.normal(ks[0], (16, 1, 224, 224), jnp.float32), 'pe_w': jax.random.normal(ks[1], (C, 1, 4, 4), jnp.float32) * s, 'pe_b': jnp.zeros((C,), jnp.float32), 'pe_ng': jnp.ones((C,), jnp.float32), 'pe_nb': jnp.zeros((C,), jnp.float32), 'n1g': jnp.ones((2, C), jnp.float32), 'n1b': jnp.zeros((2, C), jnp.float32), 'qkv_w': jax.random.normal(ks[2], (2, 3 * C, C), jnp.float32) * s, 'qkv_b': jnp.zeros((2, 3 * C), jnp.float32), 'rpb': jax.random.normal(ks[3], (2, (2 * WS - 1) ** 2, NH), jnp.float32) * s, 'proj_w': jax.random.normal(ks[4], (2, C, C), jnp.float32) * s, 'proj_b': jnp.zeros((2, C), jnp.float32), 'n2g': jnp.ones((2, C), jnp.float32), 'n2b': jnp.zeros((2, C), jnp.float32), 'w1': jax.random.normal(ks[5], (2, 4 * C, C), jnp.float32) * s, 'b1': jnp.zeros((2, 4 * C), jnp.float32), 'w2': jax.random.normal(ks[6], (2, C, 4 * C), jnp.float32) * s, 'b2': jnp.zeros((2, C), jnp.float32)}
    _L0_tok_all = _L0_tok_setup()
    _L0_tok_in = {k: v for k, v in _L0_tok_all.items() if k in ('pe_w', 'pe_b', 'pe_ng', 'pe_nb', 'n1g', 'n1b', 'qkv_w', 'qkv_b', 'rpb', 'proj_w', 'proj_b', 'n2g', 'n2b', 'w1', 'b1', 'w2', 'b2')}
    del _L0_tok_all

    def _L0_txt_setup():
        import jax, jax.numpy as jnp
        import numpy as np
        _PRIME = 31
        SIZES = tuple(range(3, 21))
        TBL = 1024
        MIXED = TBL
        NUM_SIZES_P1 = len(SIZES) + 1
        B, L, D = (8, 2048, 64)

        def _ngram_ids(byte_ids):
            dna_map = jnp.full((14,), -1, dtype=jnp.int32)
            dna_map = dna_map.at[jnp.array([1, 2, 3, 4])].set(jnp.array([0, 1, 2, 3], dtype=jnp.int32))
            dna_idx = dna_map[byte_ids]
            safe = jnp.maximum(dna_idx, 0)
            bad1 = dna_idx == -1
            h = safe
            bad = bad1
            ids = []
            for k in range(2, max(SIZES) + 1):
                h = (jnp.pad(h[:, :-1], ((0, 0), (1, 0))) * _PRIME + safe) % TBL
                bad = jnp.pad(bad[:, :-1], ((0, 0), (1, 0)), constant_values=True) | bad1
                if k in SIZES:
                    ids.append(jnp.where(bad, MIXED, h))
            return ids
        key = jax.random.key(seed)
        k1, k2 = jax.random.split(key)
        byte_ids = jax.random.randint(k1, (B, L), 0, 14, dtype=jnp.int32)
        tables = jax.random.normal(k2, (len(SIZES), TBL + 1, D), dtype=jnp.float32) * 0.02
        return {'byte_ids': byte_ids, 'tables': tables}
    _L0_txt_all = _L0_txt_setup()
    _L0_txt_in = {k: v for k, v in _L0_txt_all.items() if k in ('tables',)}
    del _L0_txt_all

    def _L0_attn_setup():
        import jax, jax.numpy as jnp
        import numpy as np
        B, T, C = (8, 1024, 64)
        N_LAYER, LAYER_ID = (12, 5)

        def _wkv(w, u, k, v):
            MIN_VALUE = -1e+38

            def step(carry, kv):
                p, q, o = carry
                kt, vt = kv
                no = jnp.maximum(o, u + kt)
                a = jnp.exp(o - no)
                b = jnp.exp(u + kt - no)
                y = (a * p + b * vt) / (a * q + b)
                no2 = jnp.maximum(w + o, kt)
                a2 = jnp.exp(w + o - no2)
                b2 = jnp.exp(kt - no2)
                return ((a2 * p + b2 * vt, a2 * q + b2, no2), y)
            p0 = jnp.zeros(k.shape[0:1] + k.shape[2:3], k.dtype)
            q0 = jnp.zeros_like(p0)
            o0 = jnp.full_like(p0, MIN_VALUE)
            kT = jnp.swapaxes(k, 0, 1)
            vT = jnp.swapaxes(v, 0, 1)
            _, yT = jax.lax.scan(step, (p0, q0, o0), (kT, vT))
            return jnp.swapaxes(yT, 0, 1)

        def _layernorm(x, w, b, eps=1e-05):
            mu = jnp.mean(x, axis=-1, keepdims=True)
            xc = x - mu
            var = jnp.mean(xc * xc, axis=-1, keepdims=True)
            return xc * jax.lax.rsqrt(var + eps) * w + b
        key = jax.random.key(seed)
        ks = jax.random.split(key, 5)
        x = jax.random.normal(ks[0], (B, T, C), dtype=jnp.float32)
        scale = 1.0 / np.sqrt(C)
        Wk = jax.random.normal(ks[1], (C, C), jnp.float32) * scale
        Wv = jax.random.normal(ks[2], (C, C), jnp.float32) * scale
        Wr = jax.random.normal(ks[3], (C, C), jnp.float32) * scale
        Wo = jax.random.normal(ks[4], (C, C), jnp.float32) * scale
        ratio_0_to_1 = LAYER_ID / (N_LAYER - 1)
        h = np.arange(C, dtype=np.float64)
        decay = -5.0 + 8.0 * (h / (C - 1)) ** (0.7 + 1.3 * ratio_0_to_1)
        zigzag = ((np.arange(C) + 1) % 3 - 1) * 0.5
        first = np.log(0.3) + zigzag
        return dict(x=x, Wk=Wk, Wv=Wv, Wr=Wr, Wo=Wo, spatial_decay=jnp.asarray(decay, jnp.float32), spatial_first=jnp.asarray(first, jnp.float32), ln_w=jnp.ones((C,), jnp.float32), ln_b=jnp.zeros((C,), jnp.float32))
    _L0_attn_all = _L0_attn_setup()
    _L0_attn_in = {k: v for k, v in _L0_attn_all.items() if k in ('Wk', 'Wv', 'Wr', 'Wo', 'spatial_decay', 'spatial_first', 'ln_w', 'ln_b')}
    del _L0_attn_all

    def _L0_ffn_setup():
        import jax, jax.numpy as jnp
        import numpy as np
        B, S, H, F, E, K = (8, 1024, 64, 128, 16, 2)
        EPS = 1e-05
        key = jax.random.key(seed)
        ks = jax.random.split(key, 9)
        sc = 0.02
        return {'x': jax.random.normal(ks[0], (B, S, H), dtype=jnp.float32), 'gate_w': jax.random.normal(ks[1], (H, E), dtype=jnp.float32) * sc, 'gate_b': jnp.zeros((E,), dtype=jnp.float32), 'w1': jax.random.normal(ks[2], (E, H, F), dtype=jnp.float32) * sc, 'b1': jnp.zeros((E, F), dtype=jnp.float32), 'w2': jax.random.normal(ks[3], (E, F, H), dtype=jnp.float32) * sc, 'b2': jnp.zeros((E, H), dtype=jnp.float32), 'gamma': jnp.ones((H,), dtype=jnp.float32), 'beta': jnp.zeros((H,), dtype=jnp.float32)}
    _L0_ffn_all = _L0_ffn_setup()
    _L0_ffn_in = {k: v for k, v in _L0_ffn_all.items() if k in ('gate_w', 'gate_b', 'w1', 'b1', 'w2', 'b2', 'gamma', 'beta')}
    del _L0_ffn_all
    return {'x': x, 'x_txt': x_txt, 'L0_tok_pe_w': _L0_tok_in['pe_w'], 'L0_tok_pe_b': _L0_tok_in['pe_b'], 'L0_tok_pe_ng': _L0_tok_in['pe_ng'], 'L0_tok_pe_nb': _L0_tok_in['pe_nb'], 'L0_tok_n1g': _L0_tok_in['n1g'], 'L0_tok_n1b': _L0_tok_in['n1b'], 'L0_tok_qkv_w': _L0_tok_in['qkv_w'], 'L0_tok_qkv_b': _L0_tok_in['qkv_b'], 'L0_tok_rpb': _L0_tok_in['rpb'], 'L0_tok_proj_w': _L0_tok_in['proj_w'], 'L0_tok_proj_b': _L0_tok_in['proj_b'], 'L0_tok_n2g': _L0_tok_in['n2g'], 'L0_tok_n2b': _L0_tok_in['n2b'], 'L0_tok_w1': _L0_tok_in['w1'], 'L0_tok_b1': _L0_tok_in['b1'], 'L0_tok_w2': _L0_tok_in['w2'], 'L0_tok_b2': _L0_tok_in['b2'], 'L0_txt_tables': _L0_txt_in['tables'], 'L0_attn_Wk': _L0_attn_in['Wk'], 'L0_attn_Wv': _L0_attn_in['Wv'], 'L0_attn_Wr': _L0_attn_in['Wr'], 'L0_attn_Wo': _L0_attn_in['Wo'], 'L0_attn_spatial_decay': _L0_attn_in['spatial_decay'], 'L0_attn_spatial_first': _L0_attn_in['spatial_first'], 'L0_attn_ln_w': _L0_attn_in['ln_w'], 'L0_attn_ln_b': _L0_attn_in['ln_b'], 'L0_ffn_gate_w': _L0_ffn_in['gate_w'], 'L0_ffn_gate_b': _L0_ffn_in['gate_b'], 'L0_ffn_w1': _L0_ffn_in['w1'], 'L0_ffn_b1': _L0_ffn_in['b1'], 'L0_ffn_w2': _L0_ffn_in['w2'], 'L0_ffn_b2': _L0_ffn_in['b2'], 'L0_ffn_gamma': _L0_ffn_in['gamma'], 'L0_ffn_beta': _L0_ffn_in['beta']}

def reference(x, x_txt, L0_tok_pe_w, L0_tok_pe_b, L0_tok_pe_ng, L0_tok_pe_nb, L0_tok_n1g, L0_tok_n1b, L0_tok_qkv_w, L0_tok_qkv_b, L0_tok_rpb, L0_tok_proj_w, L0_tok_proj_b, L0_tok_n2g, L0_tok_n2b, L0_tok_w1, L0_tok_b1, L0_tok_w2, L0_tok_b2, L0_txt_tables, L0_attn_Wk, L0_attn_Wv, L0_attn_Wr, L0_attn_Wo, L0_attn_spatial_decay, L0_attn_spatial_first, L0_attn_ln_w, L0_attn_ln_b, L0_ffn_gate_w, L0_ffn_gate_b, L0_ffn_w1, L0_ffn_b1, L0_ffn_w2, L0_ffn_b2, L0_ffn_gamma, L0_ffn_beta):
    import jax
    import jax.numpy as jnp

    def _L0_tok_ref(x, pe_w, pe_b, pe_ng, pe_nb, n1g, n1b, qkv_w, qkv_b, rpb, proj_w, proj_b, n2g, n2b, w1, b1, w2, b2):
        import jax, jax.numpy as jnp
        import numpy as np
        WS = 7
        H = W = 56
        C = 64
        NH = 8
        HD = C // NH
        SCALE = HD ** (-0.5)
        SHIFT = WS // 2
        N = WS * WS

        def _rel_pos_index():
            coords = np.stack(np.meshgrid(np.arange(WS), np.arange(WS), indexing='ij'))
            cf = coords.reshape(2, -1)
            rel = (cf[:, :, None] - cf[:, None, :]).transpose(1, 2, 0).copy()
            rel[..., 0] += WS - 1
            rel[..., 1] += WS - 1
            rel[..., 0] *= 2 * WS - 1
            return jnp.array(rel.sum(-1))

        def _attn_mask():
            img = np.zeros((H, W), np.int32)
            cnt = 0
            for h in (slice(0, -WS), slice(-WS, -SHIFT), slice(-SHIFT, None)):
                for w in (slice(0, -WS), slice(-WS, -SHIFT), slice(-SHIFT, None)):
                    cnt += 1
                    img[h, w] = cnt
            mw = img.reshape(H // WS, WS, W // WS, WS).transpose(0, 2, 1, 3).reshape(-1, N)
            diff = mw[:, None, :] - mw[:, :, None]
            return jnp.array(np.where(diff != 0, -100.0, 0.0).astype(np.float32))

        def _layernorm(x, g, b):
            m = x.mean(-1, keepdims=True)
            v = ((x - m) ** 2).mean(-1, keepdims=True)
            return (x - m) * jax.lax.rsqrt(v + 1e-05) * g + b

        def _window_partition(x):
            B = x.shape[0]
            x = x.reshape(B, H // WS, WS, W // WS, WS, C).transpose(0, 1, 3, 2, 4, 5)
            return x.reshape(-1, N, C)

        def _window_reverse(xw, B):
            x = xw.reshape(B, H // WS, W // WS, WS, WS, C).transpose(0, 1, 3, 2, 4, 5)
            return x.reshape(B, H, W, C)

        def _swin_block(x, p, shift, rpi, amask):
            B = x.shape[0]
            shortcut = x
            h = _layernorm(x, p['n1g'], p['n1b']).reshape(B, H, W, C)
            if shift > 0:
                h = jnp.roll(h, (-shift, -shift), axis=(1, 2))
            xw = _window_partition(h)
            B_ = xw.shape[0]
            qkv = (xw @ p['qkv_w'].T + p['qkv_b']).reshape(B_, N, 3, NH, HD).transpose(2, 0, 3, 1, 4)
            q, k, v = (qkv[0], qkv[1], qkv[2])
            attn = jnp.einsum('bhnd,bhmd->bhnm', q * SCALE, k)
            attn = attn + p['rpb'][rpi].transpose(2, 0, 1)[None]
            if shift > 0:
                nW = amask.shape[0]
                attn = attn.reshape(B_ // nW, nW, NH, N, N) + amask[None, :, None]
                attn = attn.reshape(B_, NH, N, N)
            attn = jax.nn.softmax(attn, axis=-1)
            o = jnp.einsum('bhnm,bhmd->bhnd', attn, v).transpose(0, 2, 1, 3).reshape(B_, N, C)
            o = o @ p['proj_w'].T + p['proj_b']
            h = _window_reverse(o, B)
            if shift > 0:
                h = jnp.roll(h, (shift, shift), axis=(1, 2))
            x = shortcut + h.reshape(B, H * W, C)
            y = _layernorm(x, p['n2g'], p['n2b'])
            y = jax.nn.gelu(y @ p['w1'].T + p['b1'], approximate=False)
            return x + y @ p['w2'].T + p['b2']
        B = x.shape[0]
        h = jax.lax.conv_general_dilated(x, pe_w, (4, 4), 'VALID', dimension_numbers=('NCHW', 'OIHW', 'NCHW'))
        h = h + pe_b[None, :, None, None]
        t = h.reshape(B, C, H * W).transpose(0, 2, 1)
        t = _layernorm(t, pe_ng, pe_nb)
        rpi = _rel_pos_index()
        amask = _attn_mask()
        for i, shift in enumerate((0, SHIFT)):
            p = {'n1g': n1g[i], 'n1b': n1b[i], 'qkv_w': qkv_w[i], 'qkv_b': qkv_b[i], 'rpb': rpb[i], 'proj_w': proj_w[i], 'proj_b': proj_b[i], 'n2g': n2g[i], 'n2b': n2b[i], 'w1': w1[i], 'b1': b1[i], 'w2': w2[i], 'b2': b2[i]}
            t = _swin_block(t, p, shift, rpi, amask)
        return t

    def _L0_txt_ref(byte_ids, tables):
        import jax, jax.numpy as jnp
        import numpy as np
        _PRIME = 31
        SIZES = tuple(range(3, 21))
        TBL = 1024
        MIXED = TBL
        NUM_SIZES_P1 = len(SIZES) + 1
        B, L, D = (8, 2048, 64)

        def _ngram_ids(byte_ids):
            dna_map = jnp.full((14,), -1, dtype=jnp.int32)
            dna_map = dna_map.at[jnp.array([1, 2, 3, 4])].set(jnp.array([0, 1, 2, 3], dtype=jnp.int32))
            dna_idx = dna_map[byte_ids]
            safe = jnp.maximum(dna_idx, 0)
            bad1 = dna_idx == -1
            h = safe
            bad = bad1
            ids = []
            for k in range(2, max(SIZES) + 1):
                h = (jnp.pad(h[:, :-1], ((0, 0), (1, 0))) * _PRIME + safe) % TBL
                bad = jnp.pad(bad[:, :-1], ((0, 0), (1, 0)), constant_values=True) | bad1
                if k in SIZES:
                    ids.append(jnp.where(bad, MIXED, h))
            return ids
        ids = _ngram_ids(byte_ids)
        total = jnp.zeros(byte_ids.shape + (tables.shape[-1],), dtype=tables.dtype)
        for t, id_n in enumerate(ids):
            total = total + tables[t][id_n]
        return total / NUM_SIZES_P1

    def _L0_attn_ref(x, Wk, Wv, Wr, Wo, spatial_decay, spatial_first, ln_w, ln_b):
        import jax, jax.numpy as jnp
        import numpy as np
        B, T, C = (8, 1024, 64)
        N_LAYER, LAYER_ID = (12, 5)

        def _wkv(w, u, k, v):
            MIN_VALUE = -1e+38

            def step(carry, kv):
                p, q, o = carry
                kt, vt = kv
                no = jnp.maximum(o, u + kt)
                a = jnp.exp(o - no)
                b = jnp.exp(u + kt - no)
                y = (a * p + b * vt) / (a * q + b)
                no2 = jnp.maximum(w + o, kt)
                a2 = jnp.exp(w + o - no2)
                b2 = jnp.exp(kt - no2)
                return ((a2 * p + b2 * vt, a2 * q + b2, no2), y)
            p0 = jnp.zeros(k.shape[0:1] + k.shape[2:3], k.dtype)
            q0 = jnp.zeros_like(p0)
            o0 = jnp.full_like(p0, MIN_VALUE)
            kT = jnp.swapaxes(k, 0, 1)
            vT = jnp.swapaxes(v, 0, 1)
            _, yT = jax.lax.scan(step, (p0, q0, o0), (kT, vT))
            return jnp.swapaxes(yT, 0, 1)

        def _layernorm(x, w, b, eps=1e-05):
            mu = jnp.mean(x, axis=-1, keepdims=True)
            xc = x - mu
            var = jnp.mean(xc * xc, axis=-1, keepdims=True)
            return xc * jax.lax.rsqrt(var + eps) * w + b
        t = x.shape[1]
        k = jnp.einsum('btc,dc->btd', x, Wk)
        v = jnp.einsum('btc,dc->btd', x, Wv)
        r = jnp.einsum('btc,dc->btd', x, Wr)
        sr = jax.nn.sigmoid(r)
        y = _wkv(spatial_decay / t, spatial_first / t, k, v)
        y = _layernorm(y, ln_w, ln_b)
        return jnp.einsum('btc,dc->btd', sr * y, Wo)

    def _L0_ffn_ref(x, gate_w, gate_b, w1, b1, w2, b2, gamma, beta):
        import jax, jax.numpy as jnp
        import numpy as np
        B, S, H, F, E, K = (8, 1024, 64, 128, 16, 2)
        EPS = 1e-05
        gate_logits = x @ gate_w + gate_b
        topk_vals, topk_idx = jax.lax.top_k(gate_logits, K)
        topk_w = jax.nn.softmax(topk_vals, axis=-1)
        h = jax.nn.relu(jnp.einsum('bsh,ehf->bsef', x, w1) + b1)
        expert_out = jnp.einsum('bsef,efh->bseh', h, w2) + b2
        sel = jnp.take_along_axis(expert_out, topk_idx[:, :, :, None], axis=2)
        moe = jnp.sum(topk_w[..., None] * sel, axis=2)
        y = x + moe
        mu = jnp.mean(y, axis=-1, keepdims=True)
        var = jnp.var(y, axis=-1, keepdims=True)
        return (y - mu) / jnp.sqrt(var + EPS) * gamma + beta
    h = _L0_tok_ref(x, L0_tok_pe_w, L0_tok_pe_b, L0_tok_pe_ng, L0_tok_pe_nb, L0_tok_n1g, L0_tok_n1b, L0_tok_qkv_w, L0_tok_qkv_b, L0_tok_rpb, L0_tok_proj_w, L0_tok_proj_b, L0_tok_n2g, L0_tok_n2b, L0_tok_w1, L0_tok_b1, L0_tok_w2, L0_tok_b2)
    h = jnp.concatenate([h, _L0_txt_ref(x_txt, L0_txt_tables)], axis=1)
    h = h + _L0_attn_ref(_layernorm(h, axis=-1), L0_attn_Wk, L0_attn_Wv, L0_attn_Wr, L0_attn_Wo, L0_attn_spatial_decay, L0_attn_spatial_first, L0_attn_ln_w, L0_attn_ln_b)
    h = h + _L0_ffn_ref(_layernorm(h, axis=-1), L0_ffn_gate_w, L0_ffn_gate_b, L0_ffn_w1, L0_ffn_b1, L0_ffn_w2, L0_ffn_b2, L0_ffn_gamma, L0_ffn_beta)
    return h

_drawn_inputs = setup_inputs


def setup_inputs(seed=0):
    import zlib

    import numpy as np

    out = dict(_drawn_inputs(seed))
    spreads = {'L0_tok_pe_b': (0.0, 0.1),
     'L0_tok_pe_ng': (1.0, 0.2),
     'L0_tok_pe_nb': (0.0, 0.1),
     'L0_tok_n1g': (1.0, 0.6),
     'L0_tok_n1b': (0.0, 0.8),
     'L0_tok_qkv_b': (0.0, 0.401),
     'L0_tok_proj_b': (0.0, 0.1),
     'L0_tok_n2g': (1.0, 0.6),
     'L0_tok_n2b': (0.0, 0.8),
     'L0_tok_b1': (0.0, 0.396),
     'L0_tok_b2': (0.0, 0.1),
     'L0_attn_ln_w': (1.0, 0.2),
     'L0_attn_ln_b': (0.0, 0.1),
     'L0_ffn_gate_b': (0.0, 0.284),
     'L0_ffn_b1': (0.0, 0.8),
     'L0_ffn_b2': (0.0, 0.294),
     'L0_ffn_gamma': (1.0, 0.2),
     'L0_ffn_beta': (0.0, 0.1)}
    factors = {'L0_tok_rpb': 200.0,
     'L0_attn_spatial_decay': 5.861,
     'L0_attn_spatial_first': 200.0,
     'L0_ffn_w1': 8.0,
     'L0_ffn_w2': 5.854}
    for name, (base, spread) in spreads.items():
        noise = np.random.default_rng([zlib.crc32(name.encode()), seed]).standard_normal(out[name].shape)
        drawn = base * np.exp(spread * noise) if base else spread * noise
        out[name] = jnp.asarray(drawn.astype(out[name].dtype))
    for name, factor in factors.items():
        out[name] = (out[name] * factor).astype(out[name].dtype)
    return out
```

```python
from contextlib import ExitStack, contextmanager

import numpy as np

import concourse.bass as bass
from concourse import mybir

F32 = mybir.dt.float32
I32 = mybir.dt.int32
U32 = mybir.dt.uint32
ALU = mybir.AluOpType
ACT = mybir.ActivationFunctionType
AX_X = mybir.AxisListType.X

P = 128
B = 16
PAIRS = B // 2
C = 64
SIDE = 56
NIMG = SIDE * SIDE
NTXT = 77
T = NIMG + NTXT
WS = 7
WIN = WS * WS
NWIN = SIDE // WS
STRIP = WS * SIDE
STRIPS = NIMG // STRIP
NH = 8
HD = C // NH
SHIFT = WS // 2
QPAD = 64
GROUPS = NH // 2
VA = 2 * HD + 2
EPS = 1e-5
LN_EXP = "natural_log_exp_and_others"
SIZES = 18
TBL = 1024
HIST = 20
TXT_P = 112
TXT_COLS = B * NTXT // TXT_P
E = 16
FF = 128
BLK = 126
NBLK = 4
CHUNK = BLK * NBLK
CHUNKS = PAIRS * T // CHUNK
TCH = 459
TCHS = T // TCH
assert CHUNKS * CHUNK == PAIRS * T and TCHS * TCH == T and TXT_P * TXT_COLS == B * NTXT

COLS = ["pe_b", "pe_ng", "pe_nb"]
for _l in (0, 1):
    COLS += [f"{n}{_l}" for n in ("n1g", "n1b", "bq", "bk", "bv", "bp", "n2g", "n2b", "b2", "b1lo", "b1hi")]
COLS += ["decay", "first", "ln_w", "ln_b", "eps"]
CI = {n: i for i, n in enumerate(COLS)}


def at(turn, per, k):
    return turn * per + max(k, 0) + 1


def open_all(eng, *sems):
    for s in sems:
        eng.sem_inc(s, 1)


class Kit:

    def __init__(self, nc, ctx, d):
        self.nc, self.d, self.used = nc, d, []
        sb = lambda name, shape, dt=F32: ctx.enter_context(nc.sbuf_tensor(name, shape, dt))
        self.stream = sb("stream", [P, PAIRS, T])
        self.cols = sb("cols", [P, len(COLS)])
        self.center = sb("center", [P, P])
        self.average = sb("average", [P, P])
        self.ident = sb("ident", [P, P])
        self.gathered = [ctx.enter_context(nc.semaphore(f"gathered{i}")) for i in (0, 1)]

    @contextmanager
    def semaphore(self, name):
        with self.nc.semaphore(name) as sem:
            self.used.append(sem)
            yield sem

    def clear(self):
        with self.nc.Block() as block:
            @block.gpsimd
            def _(gp):
                for sem in self.used:
                    gp.sem_clear(sem)
        self.used = []

    def col(self, name):
        return self.cols[:, CI[name]:CI[name] + 1]


def setup(kit):
    nc = kit.nc
    with kit.semaphore("consts_in") as consts_in, nc.Block() as block:
        @block.sync
        def _(sp):
            for dst, name in ((kit.cols, "cols"), (kit.center, "center"), (kit.average, "average"),
                              (kit.ident, "ident")):
                sp.dma_start(dst[:, :], kit.d[name]).then_inc(consts_in, 16)
            sp.wait_ge(consts_in, 64)


def embed(kit):
    nc = kit.nc
    N, K = STRIP, STRIPS
    with ExitStack() as ctx:
        sb = lambda name, shape, dt=F32: ctx.enter_context(nc.sbuf_tensor(name, shape, dt))
        ps = lambda name: ctx.enter_context(nc.psum_tensor(name, [P, 2, 512], F32))
        sem = lambda name: ctx.enter_context(kit.semaphore(name))
        w = sb("pe_w", [32, P])
        patches = sb("patches", [32, NIMG])
        conv = sb("pe_conv", [P, 2, N])
        sq = sb("pe_sq", [P, 2, N])
        logv = sb("pe_logv", [P, 2, N])
        rstd = sb("pe_rstd", [P, 2, N])
        normed = sb("pe_normed", [P, 2, N])
        pconv, pcen, pvar = ps("pconv"), ps("pcen"), ps("pvar")
        w_in, patches_in = sem("w_in"), sem("patches_in")
        conv_mm, conv_out, cen_mm, sq_out, var_mm = (sem(n) for n in (
            "conv_mm", "conv_out", "cen_mm", "sq_out", "var_mm"))
        logv_out, rstd_out, normed_out, stream_out = (sem(n) for n in (
            "logv_out", "rstd_out", "normed_out", "stream_out"))
        block = ctx.enter_context(nc.Block())

        @block.sync
        def _(sp):
            sp.dma_start(w[:, :], kit.d["pe_w"]).then_inc(w_in, 16)
            with sp.Fori(0, PAIRS) as p:
                sp.wait_ge(conv_mm, at(p, K, 0))
                sp.dma_start(patches[:, :], kit.d["patches"][:, bass.ds(p * NIMG, NIMG)]).then_inc(patches_in, 16)

        @block.tensor
        def _(pe):
            open_all(pe, conv_mm, cen_mm, var_mm)
            pe.wait_ge(w_in, 16)
            with pe.Fori(0, PAIRS) as p:
                pe.wait_ge(patches_in, p * 16 + 16)
                for s in range(K + 2):
                    if s < K:
                        pe.wait_ge(conv_out, at(p, K, s - 1))
                        nc.tensor.matmul(pconv[:, s % 2, 0:N], w[:, :], patches[:, s * N:(s + 1) * N],
                                         start=True, stop=True).then_inc(conv_mm, 1)
                    c = s - 1
                    if 0 <= c < K:
                        pe.wait_ge(conv_out, at(p, K, c + 1))
                        pe.wait_ge(normed_out, at(p, K, c - 1))
                        nc.tensor.matmul(pcen[:, c % 2, 0:N], kit.center[:, :], conv[:, c % 2, :],
                                         start=True, stop=True).then_inc(cen_mm, 1)
                    c = s - 2
                    if 0 <= c < K:
                        pe.wait_ge(sq_out, at(p, K, c + 1))
                        pe.wait_ge(logv_out, at(p, K, c - 1))
                        nc.tensor.matmul(pvar[:, c % 2, 0:N], kit.average[:, :], sq[:, c % 2, :],
                                         start=True, stop=True).then_inc(var_mm, 1)

        @block.scalar
        def _(act):
            open_all(act, conv_out, sq_out, logv_out, rstd_out, stream_out)
            act.preload_act_table_set(LN_EXP)
            with act.Fori(0, PAIRS) as p:
                for s in range(K + 3):
                    if s < K:
                        act.wait_ge(conv_mm, at(p, K, s + 1))
                        act.wait_ge(cen_mm, at(p, K, s - 1))
                        nc.scalar.activation(conv[:, s % 2, :], pconv[:, s % 2, 0:N], ACT.Identity,
                                             bias=kit.col("pe_b")).then_inc(conv_out, 1)
                    c = s - 1
                    if 0 <= c < K:
                        act.wait_ge(cen_mm, at(p, K, c + 1))
                        act.wait_ge(var_mm, at(p, K, c - 1))
                        nc.scalar.activation(sq[:, c % 2, :], pcen[:, c % 2, 0:N], ACT.Square).then_inc(sq_out, 1)
                    c = s - 2
                    if 0 <= c < K:
                        act.wait_ge(var_mm, at(p, K, c + 1))
                        act.wait_ge(rstd_out, at(p, K, c - 1))
                        nc.scalar.activation(logv[:, c % 2, :], pvar[:, c % 2, 0:N], ACT.Ln,
                                             bias=kit.col("eps")).then_inc(logv_out, 1)
                        act.wait_ge(logv_out, at(p, K, c + 1))
                        act.wait_ge(normed_out, at(p, K, c - 1))
                        nc.scalar.activation(rstd[:, c % 2, :], logv[:, c % 2, :], ACT.Exp,
                                             scale=-0.5).then_inc(rstd_out, 1)
                    c = s - 3
                    if 0 <= c < K:
                        act.wait_ge(normed_out, at(p, K, c + 1))
                        nc.scalar.activation(kit.stream[:, bass.ds(p, 1), c * N:(c + 1) * N], normed[:, c % 2, :].unsqueeze(1),
                                             ACT.Identity, bias=kit.col("pe_nb"),
                                             scale=kit.col("pe_ng")).then_inc(stream_out, 1)

        @block.vector
        def _(dve):
            open_all(dve, normed_out)
            with dve.Fori(0, PAIRS) as p:
                for c in range(K):
                    dve.wait_ge(rstd_out, at(p, K, c + 1))
                    dve.wait_ge(stream_out, at(p, K, c - 1))
                    nc.vector.tensor_tensor(normed[:, c % 2, :], pcen[:, c % 2, 0:N], rstd[:, c % 2, :],
                                            ALU.mult).then_inc(normed_out, 1)


def image_rows(kit, pair, row, rows):
    flat = kit.stream[:, :, :].rearrange("p n t -> p (n t)")
    return flat[:, bass.ds(pair * T + row * SIDE, rows * SIDE)].rearrange("p (r c) -> p r c", c=SIDE)


def strip_pieces(kit, strip, pair, row, last, shift):
    if not shift:
        return [(strip[:, :, :], image_rows(kit, pair, row * WS, WS))]
    parts = [(0, WS, row * WS + shift)]
    if last:
        parts = [(0, WS - shift, SIDE - (WS - shift)), (WS - shift, shift, 0)]
    out = []
    for r0, rows, at_row in parts:
        img = image_rows(kit, pair, at_row, rows)
        out.append((strip[:, r0:r0 + rows, 0:SIDE - shift], img[:, :, shift:SIDE]))
        out.append((strip[:, r0:r0 + rows, SIDE - shift:SIDE], img[:, :, 0:shift]))
    return out


def window_attention(kit, layer):
    nc = kit.nc
    shift = SHIFT if layer else 0
    N, W = STRIP, NWIN
    scale = HD ** -0.5
    with ExitStack() as ctx:
        sb = lambda name, shape, dt=F32: ctx.enter_context(nc.sbuf_tensor(f"{name}{layer}", shape, dt))
        ps = lambda name, *shape: ctx.enter_context(nc.psum_tensor(f"{name}{layer}", [P, *shape], F32))
        sem = lambda name: ctx.enter_context(kit.semaphore(f"{name}{layer}"))
        sems = lambda names: [sem(n) for n in names.split()]
        weights = sb("attn_w", [P, 4, P])
        tables = sb("score_bias", [P, 4, NH * WIN])
        relbias = sb("relbias", [P, NH * WIN])
        headmask, fold = sb("headmask", [P, NH]), sb("fold", [P, WIN])
        vmask = sb("vmask", [2 * WIN, 4 * P])
        vones = sb("vones", [2 * WIN, 4 * GROUPS])
        bq_scaled = sb("bq_scaled", [P, 1])
        src, res = sb("src", [P, WS, SIDE]), sb("res", [P, WS, SIDE])
        sq, logv, rstd, normed = (sb(n, [P, N]) for n in ("sq", "logv", "rstd", "normed"))
        hn = sb("hn", [P, W, 2, WIN])
        qbd = sb("qbd", [P, W, P])
        keys = sb("keys", [P, N])
        kx = sb("kx", [P, W, NH, WIN])
        va = sb("va", [2 * WIN, W, 2 * GROUPS, VA])
        scores, probs = sb("scores", [P, 2, NH, WIN]), sb("probs", [P, 2, NH * WIN])
        rmax = sb("rmax", [P, 2, NH])
        pt = sb("pt", [2 * WIN, 2, GROUPS, P])
        rsum = sb("rsum", [P, 2, NH])
        obd = sb("obd", [P, W, P])
        ofm = sb("ofm", [P, N])
        pa, pb, pv, pt_ps, po, pf = (ps(n, 512) for n in ("pa", "pb", "pv", "pt_ps", "po", "pf"))
        pscore = ps("pscore", 2, 512)
        weights_in, cleared, tables_out, passed = sems("weights_in cleared tables_out passed")
        src_in, twice_out, kx_pool, stream_out = sems("src_in twice_out kx_pool stream_out")
        cen_mm, var_mm, q_mm, k_mm, v_mm, score_mm, turn_mm, av_mm, fold_mm, proj_mm = sems(
            "cen_mm var_mm q_mm k_mm v_mm score_mm turn_mm av_mm fold_mm proj_mm")
        sq_out, logv_out, rstd_out, hn_out, q_out, keys_out, probs_out, pt_out, ofm_out, res_out = sems(
            "sq_out logv_out rstd_out hn_out q_out keys_out probs_out pt_out ofm_out res_out")
        normed_out, kx_dve, va_out, biased_out, max_out, shifted_out, rsum_out, o_out = sems(
            "normed_out kx_dve va_out biased_out max_out shifted_out rsum_out o_out")
        POOL_HEADS = 3
        block = ctx.enter_context(nc.Block())

        def turns(eng, body):
            with eng.Fori(0, PAIRS) as pair:
                if shift:
                    with eng.Fori(0, W - 1) as row:
                        body(pair * W + row, pair, row, False)
                    body(pair * W + (W - 1), pair, W - 1, True)
                else:
                    with eng.Fori(0, W) as row:
                        body(pair * W + row, pair, row, False)

        @block.sync
        def _(sp):
            for dst, name in ((weights[:, :, :].rearrange("p a b -> p (a b)"), f"attn_w{layer}"),
                              (tables[:, :, :].rearrange("p a b -> p (a b)"), "amask"),
                              (relbias[:, :], f"relbias{layer}"), (headmask[:, :], "headmask"),
                              (fold[:, :], "fold"), (vmask[:, :], "vmask"), (vones[:, :], "vones")):
                sp.dma_start(dst, kit.d[name]).then_inc(weights_in, 16)

        @block.gpsimd
        def _(gp):
            open_all(gp, src_in, twice_out, kx_pool, stream_out)
            nc.gpsimd.memset(qbd[:, :, :], 0.0).then_inc(cleared, 1)
            nc.gpsimd.memset(obd[:, :, :], 0.0).then_inc(cleared, 1)

            gp.wait_ge(weights_in, 7 * 16)

            def settled():
                gp.sem_inc(passed, 1)

            def body(turn, pair, row, last):
                gp.wait_ge(stream_out, at(turn, 1, 0))
                settled()
                for buf, img in strip_pieces(kit, src, pair, row, last, shift):
                    done = nc.gpsimd.tensor_copy(buf, img)
                done.then_inc(src_in, 1)
                gp.wait_ge(hn_out, at(turn, 1, 1))
                settled()
                nc.gpsimd.tensor_copy(hn[:, :, 1, :], hn[:, :, 0, :]).then_inc(twice_out, 1)
                gp.wait_ge(keys_out, at(turn, 1, 1))
                settled()
                for h in range(POOL_HEADS):
                    nc.gpsimd.tensor_scalar(kx[:, :, h, :], keys[:, :].rearrange("p (w k) -> p w k", w=W),
                                            headmask[:, h:h + 1], None, ALU.mult).then_inc(kx_pool, 1)
                gp.wait_ge(res_out, at(turn, 1, 1))
                settled()
                for (old, img), (new, _) in zip(strip_pieces(kit, src, pair, row, last, shift),
                                                strip_pieces(kit, res, pair, row, last, shift)):
                    done = nc.gpsimd.tensor_tensor(img, new, old, ALU.add)
                done.then_inc(stream_out, 1)

            turns(gp, body)

        @block.tensor
        def _(pe):
            open_all(pe, cen_mm, var_mm, q_mm, k_mm, v_mm, score_mm, turn_mm, av_mm, fold_mm, proj_mm)
            pe.wait_ge(weights_in, 7 * 16)
            pe.wait_ge(cleared, 2)

            def body(turn, pair, row, last):
                pe.wait_ge(src_in, at(turn, 1, 1))
                nc.tensor.matmul(pa[:, 0:N], kit.center[:, :], src[:, :, :].rearrange("p r c -> p (r c)"),
                                 start=True, stop=True).then_inc(cen_mm, 1)
                pe.wait_ge(sq_out, at(turn, 1, 1))
                nc.tensor.matmul(pb[:, 0:N], kit.average[:, :], sq[:, :], start=True, stop=True).then_inc(var_mm, 1)
                pe.wait_ge(hn_out, at(turn, 1, 1))
                flat = hn[:, :, 0, :]
                nc.tensor.matmul(pb[:, 0:N], weights[:, 1, :], flat, start=True, stop=True).then_inc(k_mm, 1)
                nc.tensor.matmul(pa[:, 0:N], weights[:, 0, :], flat, start=True, stop=True).then_inc(q_mm, 1)

                def fold_group(g):
                    pe.wait_ge(o_out, at(turn, W, 2 * g + 2))
                    for w in (2 * g, 2 * g + 1):
                        nc.tensor.matmul(pf[:, w * WIN:(w + 1) * WIN], obd[:, w, :], fold[:, :],
                                         start=True, stop=True).then_inc(fold_mm, 1)

                def values(g):
                    pe.wait_ge(va_out, at(turn, 2, g))
                    for w in range(4 * g, 4 * g + 4):
                        nc.tensor.matmul(pv[0:2 * WIN, w % 4 * P:w % 4 * P + P],
                                         hn[:, w, :, :].rearrange("p a k -> p (a k)"), weights[:, 2, :],
                                         start=True, stop=True).then_inc(v_mm, 1)

                pe.wait_ge(twice_out, at(turn, 1, 1))
                values(0)
                pe.wait_ge(q_out, at(turn, 2, 2))
                pe.wait_ge(kx_pool, at(turn, POOL_HEADS, POOL_HEADS))
                pe.wait_ge(kx_dve, at(turn, NH - POOL_HEADS, NH - POOL_HEADS))
                for step in range(W + 2):
                    w = step
                    if w < W:
                        pe.wait_ge(biased_out, at(turn, W, w - 1))
                        nc.tensor.matmul(pscore[:, w % 2, 0:NH * WIN], qbd[:, w, :],
                                         kx[:, w, :, :].rearrange("p h k -> p (h k)"),
                                         start=True, stop=True).then_inc(score_mm, 1)
                    if step == 1:
                        values(1)
                    w = step - 1
                    if 0 <= w < W:
                        pe.wait_ge(probs_out, at(turn, W, w + 1))
                        pe.wait_ge(pt_out, at(turn, W, w))
                        for g in range(GROUPS):
                            done = nc.tensor.transpose(pt_ps[0:2 * WIN, g * P:(g + 1) * P],
                                                       probs[:, w % 2, g * 2 * WIN:(g + 1) * 2 * WIN],
                                                       kit.ident[:, :])
                        done.then_inc(turn_mm, 1)
                    w = step - 2
                    if 0 <= w < W:
                        pe.wait_ge(pt_out, at(turn, W, w + 1))
                        pe.wait_ge(va_out, at(turn, 2, w // 4 + 1))
                        if w % 2 == 0:
                            pe.wait_ge(o_out, at(turn, W, w))
                        for b in (0, 1):
                            for g in range(GROUPS):
                                o = (w % 2 * GROUPS + g) * VA
                                done = nc.tensor.matmul(po[QPAD * b:QPAD * b + QPAD, o:o + VA],
                                                        pt[:, w % 2, g, QPAD * b:QPAD * b + QPAD],
                                                        va[:, w, b * GROUPS + g, :], start=True, stop=True)
                        done.then_inc(av_mm, 1)
                        if w % 2 == 1 and w > 1:
                            fold_group(w // 2 - 1)
                fold_group(W // 2 - 1)
                pe.wait_ge(ofm_out, at(turn, 1, 1))
                nc.tensor.matmul(pa[:, 0:N], weights[:, 3, :], ofm[:, :], start=True, stop=True).then_inc(proj_mm, 1)

            turns(pe, body)

        @block.scalar
        def _(act):
            open_all(act, sq_out, logv_out, rstd_out, hn_out, q_out, keys_out, probs_out, pt_out, ofm_out, res_out)
            act.preload_act_table_set(LN_EXP)
            act.wait_ge(tables_out, 1)

            def body(turn, pair, row, last):
                act.wait_ge(cen_mm, at(turn, 1, 1))
                nc.scalar.activation(sq[:, :], pa[:, 0:N], ACT.Square).then_inc(sq_out, 1)
                act.wait_ge(var_mm, at(turn, 1, 1))
                nc.scalar.activation(logv[:, :], pb[:, 0:N], ACT.Ln, bias=kit.col("eps")).then_inc(logv_out, 1)
                act.wait_ge(logv_out, at(turn, 1, 1))
                nc.scalar.activation(rstd[:, :], logv[:, :], ACT.Exp, scale=-0.5).then_inc(rstd_out, 1)
                act.wait_ge(normed_out, at(turn, 1, 1))
                nc.scalar.activation(hn[:, :, 0, :].rearrange("p w (r c) -> p r w c", c=WS),
                                     normed[:, :].rearrange("p (r w c) -> p r w c", r=WS, w=W), ACT.Identity,
                                     bias=kit.col(f"n1b{layer}"), scale=kit.col(f"n1g{layer}")).then_inc(hn_out, 1)
                act.wait_ge(k_mm, at(turn, 1, 1))
                nc.scalar.activation(keys[:, :], pb[:, 0:N], ACT.Identity,
                                     bias=kit.col(f"bk{layer}")).then_inc(keys_out, 1)
                act.wait_ge(q_mm, at(turn, 1, 1))
                for b in (0, 1):
                    half = slice(C * b, C * b + C)
                    nc.scalar.activation(qbd[half, :, QPAD * b:QPAD * b + WIN],
                                         pa[half, 0:N].rearrange("p (w k) -> p w k", w=W), ACT.Identity,
                                         bias=bq_scaled[half, :], scale=scale).then_inc(q_out, 1)
                for step in range(W + 1):
                    w = step
                    if w < W:
                        act.wait_ge(shifted_out, at(turn, W, w + 1))
                        act.wait_ge(turn_mm, at(turn, W, w - 1))
                        nc.scalar.activation(probs[:, w % 2, :],
                                             scores[:, w % 2, :, :].rearrange("p h k -> p (h k)"),
                                             ACT.Exp).then_inc(probs_out, 1)
                    w = step - 1
                    if 0 <= w < W:
                        act.wait_ge(turn_mm, at(turn, W, w + 1))
                        act.wait_ge(av_mm, at(turn, W, w - 1))
                        nc.scalar.activation(pt[:, w % 2, :, :].rearrange("p g q -> p (g q)"),
                                             pt_ps[0:2 * WIN, :], ACT.Copy).then_inc(pt_out, 1)
                act.wait_ge(fold_mm, at(turn, W, W))
                nc.scalar.activation(ofm[:, :], pf[:, 0:N], ACT.Identity,
                                     bias=kit.col(f"bv{layer}")).then_inc(ofm_out, 1)
                act.wait_ge(proj_mm, at(turn, 1, 1))
                act.wait_ge(stream_out, at(turn, 1, 0))
                nc.scalar.activation(res[:, :, :].rearrange("p r (w c) -> p r w c", w=W),
                                     pa[:, 0:N].rearrange("p (w r c) -> p r w c", w=W, r=WS), ACT.Identity,
                                     bias=kit.col(f"bp{layer}")).then_inc(res_out, 1)

            turns(act, body)

        @block.vector
        def _(dve):
            open_all(dve, normed_out, kx_dve, va_out, biased_out, max_out, shifted_out, rsum_out, o_out)
            dve.wait_ge(weights_in, 7 * 16)
            nc.vector.tensor_scalar(bq_scaled[:, :], kit.col(f"bq{layer}"), scale, None, ALU.mult).then_inc(tables_out, 1)
            nc.vector.tensor_tensor(tables[:, :, :], tables[:, :, :],
                                    relbias[:, :].unsqueeze(1).broadcast_to([P, 4, NH * WIN]),
                                    ALU.add).then_inc(tables_out, 1)
            for s in range(W):
                nc.vector.tensor_copy(va[:, s, :, 2 * HD:VA],
                                      vones[:, :].rearrange("p (g o) -> p g o", o=2)).then_inc(tables_out, 1)
            dve.wait_ge(tables_out, 2 + W)

            def body(turn, pair, row, last):
                dve.wait_ge(rstd_out, at(turn, 1, 1))
                nc.vector.tensor_tensor(normed[:, :], pa[:, 0:N], rstd[:, :], ALU.mult).then_inc(normed_out, 1)
                dve.wait_ge(keys_out, at(turn, 1, 1))
                for h in range(POOL_HEADS, NH):
                    nc.vector.tensor_scalar(kx[:, :, h, :], keys[:, :].rearrange("p (w k) -> p w k", w=W),
                                            headmask[:, h:h + 1], None, ALU.mult).then_inc(kx_dve, 1)

                def outputs(g):
                    dve.wait_ge(av_mm, at(turn, W, 2 * g + 2))
                    o = po[:, 0:2 * GROUPS * VA].rearrange("p (w g v) -> p w g v", w=2, g=GROUPS)
                    nc.vector.reciprocal(rsum[:, :, :].rearrange("p w (g o) -> p w g o", o=2),
                                         o[:, :, :, 2 * HD:VA]).then_inc(rsum_out, 1)
                    dve.wait_ge(rsum_out, at(turn, W // 2, g + 1))
                    for b in (0, 1):
                        half = slice(QPAD * b, QPAD * b + QPAD)
                        for k in (0, 1):
                            dst = obd[half, 2 * g + k, C * b:C * b + C].rearrange("p (g o d) -> p g o d", o=2, d=HD)
                            val = o[half, k, :, 0:2 * HD].rearrange("p g (o d) -> p g o d", o=2)
                            rs = rsum[half, k, :].rearrange("p (g o) -> p g o", o=2).unsqueeze(3)
                            done = nc.vector.tensor_tensor(dst, val, rs.broadcast_to([QPAD, GROUPS, 2, HD]), ALU.mult)
                            if b == 1:
                                done.then_inc(o_out, 1)

                def values(g):
                    dve.wait_ge(v_mm, at(turn, W, 4 * g + 4))
                    nc.vector.tensor_tensor(
                        va[:, 4 * g:4 * g + 4, :, 0:2 * HD].rearrange("p w g v -> p (w g) v"),
                        pv[0:2 * WIN, :].rearrange("p (g v) -> p g v", v=2 * HD),
                        vmask[:, :].rearrange("p (g v) -> p g v", v=2 * HD), ALU.mult).then_inc(va_out, 1)

                for step in range(W + 2):
                    w = step
                    if w in (1, 3):
                        values(w // 2)
                    if w < W:
                        dve.wait_ge(score_mm, at(turn, W, w + 1))
                        dve.wait_ge(probs_out, at(turn, W, w - 1))
                        flat = scores[:, w % 2, :, :].rearrange("p h k -> p (h k)")
                        kind = (2 * last + (w == W - 1)) if shift else 0
                        nc.vector.tensor_tensor(flat, pscore[:, w % 2, 0:NH * WIN], tables[:, kind, :],
                                                ALU.add).then_inc(biased_out, 1)
                        dve.wait_ge(biased_out, at(turn, W, w + 1))
                        nc.vector.tensor_reduce(rmax[:, w % 2, :], scores[:, w % 2, :, :], AX_X,
                                                ALU.max).then_inc(max_out, 1)
                        dve.wait_ge(max_out, at(turn, W, w + 1))
                        nc.vector.tensor_tensor(scores[:, w % 2, :, :], scores[:, w % 2, :, :],
                                                rmax[:, w % 2, :].unsqueeze(2).broadcast_to([P, NH, WIN]),
                                                ALU.subtract).then_inc(shifted_out, 1)
                    w = step - 2
                    if 0 <= w < W and w % 2 == 1:
                        outputs(w // 2)

            turns(dve, body)


def mlp(kit, layer):
    nc = kit.nc
    N, K = STRIP, STRIPS
    with ExitStack() as ctx:
        sb = lambda name, shape, dt=F32: ctx.enter_context(nc.sbuf_tensor(f"{name}_m{layer}", shape, dt))
        ps = lambda name, *shape: ctx.enter_context(nc.psum_tensor(f"{name}_m{layer}", [P, *shape], F32))
        sem = lambda name: ctx.enter_context(kit.semaphore(f"{name}_m{layer}"))
        sems = lambda names: [sem(n) for n in names.split()]
        up = sb("up", [P, 4 * C])
        down = sb("down", [P, 2, 2, P])
        sq, logv, rstd, normed = (sb(n, [P, 2, N]) for n in ("sq", "logv", "rstd", "normed"))
        hn = sb("hn", [P, K, N])
        gel = sb("gel", [P, 2, 4, N])
        pcen, pvar, pup, pdown = ps("pcen", 2, 512), ps("pvar", 512), ps("pup", 4, 512), ps("pdown", 512)
        weights_in, cen_mm, var_mm, up_mm, down_mm = sems("weights_in cen_mm var_mm up_mm down_mm")
        sq_out, logv_out, rstd_out, hn_out, gelu_out = sems("sq_out logv_out rstd_out hn_out gelu_out")
        normed_out, stream_out = sems("normed_out stream_out")
        block = ctx.enter_context(nc.Block())

        @block.sync
        def _(sp):
            sp.dma_start(up[:, :], kit.d[f"up{layer}"]).then_inc(weights_in, 16)
            sp.dma_start(down[:, :, :, :].rearrange("p h b m -> p (h b m)"), kit.d[f"down{layer}"]).then_inc(weights_in, 16)

        @block.tensor
        def _(pe):
            open_all(pe, cen_mm, var_mm, up_mm, down_mm)
            pe.wait_ge(weights_in, 32)
            with pe.Fori(0, PAIRS) as p:
                pe.wait_ge(stream_out, at(p, K, 0))
                for s in range(K + 1):
                    if s < K:
                        pe.wait_ge(normed_out, at(p, K, s - 1))
                        nc.tensor.matmul(pcen[:, s % 2, 0:N], kit.center[:, :],
                                         kit.stream[:, bass.ds(p, 1), s * N:(s + 1) * N].rearrange("p a n -> p (a n)"),
                                         start=True, stop=True).then_inc(cen_mm, 1)
                    c = s - 1
                    if 0 <= c:
                        pe.wait_ge(sq_out, at(p, K, c + 1))
                        pe.wait_ge(logv_out, at(p, K, c))
                        nc.tensor.matmul(pvar[:, 0:N], kit.average[:, :], sq[:, c % 2, :],
                                         start=True, stop=True).then_inc(var_mm, 1)
                for s in range(K + 1):
                    if s < K:
                        pe.wait_ge(hn_out, at(p, K, s + 1))
                        for b in (0, 1):
                            for half in (0, 1):
                                pe.wait_ge(gelu_out, at(p, 4 * K, 4 * (s - 1) + 2 * b + half + 1))
                                nc.tensor.matmul(pup[:, 2 * b + half, 0:N], up[C * b:C * b + C, P * half:P * half + P],
                                                 hn[C * b:C * b + C, s, :], start=True, stop=True).then_inc(up_mm, 1)
                    c = s - 1
                    if 0 <= c:
                        pe.wait_ge(stream_out, at(p, K, c))
                        for i in range(4):
                            pe.wait_ge(gelu_out, at(p, 4 * K, 4 * c + i + 1))
                            done = nc.tensor.matmul(pdown[:, 0:N], down[:, i % 2, i // 2, :], gel[:, c % 2, i, :],
                                                    start=(i == 0), stop=(i == 3))
                        done.then_inc(down_mm, 1)

        @block.scalar
        def _(act):
            open_all(act, sq_out, logv_out, rstd_out, hn_out, gelu_out)
            with act.Fori(0, PAIRS) as p:
                act.preload_act_table_set(LN_EXP)
                for s in range(K + 2):
                    if s < K:
                        act.wait_ge(cen_mm, at(p, K, s + 1))
                        act.wait_ge(var_mm, at(p, K, s - 1))
                        nc.scalar.activation(sq[:, s % 2, :], pcen[:, s % 2, 0:N], ACT.Square).then_inc(sq_out, 1)
                    c = s - 1
                    if 0 <= c < K:
                        act.wait_ge(var_mm, at(p, K, c + 1))
                        act.wait_ge(rstd_out, at(p, K, c - 1))
                        nc.scalar.activation(logv[:, c % 2, :], pvar[:, 0:N], ACT.Ln,
                                             bias=kit.col("eps")).then_inc(logv_out, 1)
                        act.wait_ge(logv_out, at(p, K, c + 1))
                        act.wait_ge(normed_out, at(p, K, c - 1))
                        nc.scalar.activation(rstd[:, c % 2, :], logv[:, c % 2, :], ACT.Exp,
                                             scale=-0.5).then_inc(rstd_out, 1)
                    c = s - 2
                    if 0 <= c < K:
                        act.wait_ge(normed_out, at(p, K, c + 1))
                        act.wait_ge(up_mm, at(p, 4 * K, 0))
                        nc.scalar.activation(hn[:, c, :], normed[:, c % 2, :], ACT.Identity,
                                             bias=kit.col(f"n2b{layer}"), scale=kit.col(f"n2g{layer}")).then_inc(hn_out, 1)
                for c in range(K):
                    act.wait_ge(down_mm, at(p, K, c - 1))
                    for i in range(4):
                        act.wait_ge(up_mm, at(p, 4 * K, 4 * c + i + 1))
                        nc.scalar.activation(gel[:, c % 2, i, :], pup[:, i, 0:N], ACT.Gelu,
                                             bias=kit.col(f"b1{('lo', 'hi')[i % 2]}{layer}")).then_inc(gelu_out, 1)

        @block.vector
        def _(dve):
            open_all(dve, normed_out, stream_out)
            with dve.Fori(0, PAIRS) as p:
                for c in range(K):
                    dve.wait_ge(rstd_out, at(p, K, c + 1))
                    dve.wait_ge(hn_out, at(p, K, c - 1))
                    nc.vector.tensor_tensor(normed[:, c % 2, :], pcen[:, c % 2, 0:N], rstd[:, c % 2, :],
                                            ALU.mult).then_inc(normed_out, 1)
                for c in range(K):
                    x = kit.stream[:, bass.ds(p, 1), c * N:(c + 1) * N].rearrange("p a n -> p (a n)")
                    dve.wait_ge(down_mm, at(p, K, c + 1))
                    nc.vector.scalar_tensor_tensor(out=x, in0=pdown[:, 0:N], scalar=kit.col(f"b2{layer}"), in1=x,
                                                   op0=ALU.add, op1=ALU.add).then_inc(stream_out, 1)


def text(kit):
    nc = kit.nc
    NC = TXT_COLS
    with ExitStack() as ctx:
        sb = lambda name, shape, dt=F32: ctx.enter_context(nc.sbuf_tensor(f"txt_{name}", shape, dt))
        sem = lambda name: ctx.enter_context(kit.semaphore(f"txt_{name}"))
        sems = lambda names: [sem(n) for n in names.split()]
        history = sb("history", [TXT_P, NC * HIST], I32)
        powers, fresh = sb("powers", [TXT_P, NC * HIST]), sb("fresh", [TXT_P, NC * HIST])
        base = sb("base", [TXT_P, NC * SIZES])
        byte, low, ok, bad, safe, term, total, anybad = (
            sb(n, [TXT_P, NC * HIST]) for n in "byte low ok bad safe term total anybad".split())
        whole, masked = sb("whole", [TXT_P, NC, HIST], I32), sb("masked", [TXT_P, NC, HIST], I32)
        hashed, good, kept, row = (sb(n, [TXT_P, NC, HIST]) for n in "hashed good kept row".split())
        ids = sb("ids", [TXT_P, NC, SIZES], U32)
        now = sb("now", [TXT_P, 2, SIZES], U32)
        rows = sb("rows", [TXT_P, 2, SIZES, C])
        total_rows = sb("total_rows", [TXT_P, C])
        twice = sb("twice", [TXT_P, 2, C])
        turned = sb("turned", [P, B * NTXT])
        pt = ctx.enter_context(nc.psum_tensor("txt_pt", [P, 512], F32))
        inputs_in, steps, now_out, sum_out, twice_out, turn_mm, turned_out, stream_out = sems(
            "inputs_in steps now_out sum_out twice_out turn_mm turned_out stream_out")
        gathered = kit.gathered
        block = ctx.enter_context(nc.Block())

        @block.sync
        def _(sp):
            for dst, name in ((history, "history"), (powers, "hashes"), (fresh, "fresh"), (base, "tablebase")):
                sp.dma_start(dst[:, :], kit.d[name]).then_inc(inputs_in, 16)

        @block.vector
        def _(dve):
            open_all(dve, now_out, sum_out, twice_out)
            dve.wait_ge(inputs_in, 64)
            count = [0]

            def then(ins):
                count[0] += 1
                ins.then_inc(steps, 1)
                dve.wait_ge(steps, count[0])

            then(nc.vector.tensor_copy(byte[:, :], history[:, :]))
            then(nc.vector.tensor_scalar(low[:, :], byte[:, :], 1.0, None, ALU.is_ge))
            then(nc.vector.scalar_tensor_tensor(out=ok[:, :], in0=byte[:, :], scalar=4.0, in1=low[:, :],
                                                op0=ALU.is_le, op1=ALU.mult))
            then(nc.vector.tensor_scalar(bad[:, :], ok[:, :], -1.0, 1.0, ALU.mult, ALU.add))
            then(nc.vector.scalar_tensor_tensor(out=safe[:, :], in0=byte[:, :], scalar=-1.0, in1=ok[:, :],
                                                op0=ALU.add, op1=ALU.mult))
            then(nc.vector.tensor_tensor(term[:, :], safe[:, :], powers[:, :], ALU.mult))
            then(nc.vector.tensor_tensor_scan(total[:, :], fresh[:, :], term[:, :], 0.0, ALU.mult, ALU.add))
            then(nc.vector.tensor_tensor_scan(anybad[:, :], fresh[:, :], bad[:, :], 0.0, ALU.mult, ALU.max))
            flat = lambda t: t[:, :, :].rearrange("p n h -> p (n h)")
            then(nc.vector.tensor_copy(flat(whole), total[:, :]))
            then(nc.vector.tensor_scalar(flat(masked), flat(whole), TBL - 1, None, ALU.bitwise_and))
            then(nc.vector.tensor_copy(flat(hashed), flat(masked)))
            then(nc.vector.tensor_scalar(flat(good), anybad[:, :], -1.0, 1.0, ALU.mult, ALU.add))
            then(nc.vector.tensor_tensor(flat(kept), flat(hashed), flat(good), ALU.mult))
            then(nc.vector.scalar_tensor_tensor(out=flat(row), in0=anybad[:, :], scalar=float(TBL), in1=flat(kept),
                                                op0=ALU.mult, op1=ALU.add))
            then(nc.vector.tensor_tensor(ids[:, :, :], row[:, :, HIST - SIZES:HIST],
                                         base[:, :].rearrange("p (n s) -> p n s", n=NC), ALU.add))
            for n in range(NC + 1):
                if n < NC:
                    if n >= 2:
                        dve.wait_ge(gathered[n % 2], 16 * SIZES * (n // 2))
                    nc.vector.tensor_copy(now[:, n % 2, :], ids[:, n, :]).then_inc(now_out, 1)
                if n >= 1:
                    m = n - 1
                    dve.wait_ge(gathered[m % 2], 16 * SIZES * (m // 2 + 1))
                    dve.wait_ge(twice_out, at(m, 1, 0))
                    nc.vector.tensor_reduce(total_rows[:, :], rows[:, m % 2, :, :].rearrange("p s c -> p c s"),
                                            AX_X, ALU.add).then_inc(sum_out, 1)
                    dve.wait_ge(sum_out, at(m, 1, 1))
                    dve.wait_ge(turn_mm, at(m, 1, 0))
                    nc.vector.tensor_scalar(twice[:, :, :], total_rows[:, :].unsqueeze(1).broadcast_to([TXT_P, 2, C]),
                                            1.0 / (SIZES + 1), None, ALU.mult).then_inc(twice_out, 1)

        @block.gpsimd
        def _(gp):
            for n in range(NC):
                gp.wait_ge(now_out, at(n, 1, 1))
                if n >= 2:
                    gp.wait_ge(sum_out, at(n - 2, 1, 1))
                for s in range(SIZES):
                    gp.indirect_dma_start(out=rows[:, n % 2, s, :], out_offset=None, in_=kit.d["tables"],
                                          in_offset=bass.IndirectOffsetOnAxis(ap=now[:, n % 2, s:s + 1], axis=0),
                                          ).then_inc(gathered[n % 2], 16)

        @block.tensor
        def _(pe):
            open_all(pe, turn_mm)
            for n in range(NC):
                pe.wait_ge(twice_out, at(n, 1, 1))
                pe.wait_ge(turned_out, at(n, 1, 0))
                nc.tensor.transpose(pt[:, 0:TXT_P], twice[:, :, :].rearrange("p a c -> p (a c)"),
                                    kit.ident[0:TXT_P, 0:TXT_P]).then_inc(turn_mm, 1)

        @block.scalar
        def _(act):
            open_all(act, turned_out)
            for n in range(NC):
                act.wait_ge(turn_mm, at(n, 1, 1))
                nc.scalar.activation(turned[:, n * TXT_P:(n + 1) * TXT_P], pt[:, 0:TXT_P],
                                     ACT.Copy).then_inc(turned_out, 1)
            act.wait_ge(turned_out, at(NC, 1, 0))
            for b in (0, 1):
                half = slice(C * b, C * b + C)
                nc.scalar.activation(kit.stream[half, :, NIMG:T],
                                     turned[half, :].rearrange("p (n b t) -> p b n t", b=2, t=NTXT)[:, b],
                                     ACT.Copy).then_inc(stream_out, 1)


def time_mix(kit):
    nc = kit.nc
    N, K = TCH, TCHS
    with ExitStack() as ctx:
        sb = lambda name, shape, dt=F32: ctx.enter_context(nc.sbuf_tensor(f"mix_{name}", shape, dt))
        sem = lambda name: ctx.enter_context(kit.semaphore(f"mix_{name}"))
        sems = lambda names: [sem(n) for n in names.split()]
        weights = sb("w", [P, 4, P])
        rates = sb("rates", [P, 2])
        decay, first = rates[:, 0:1], rates[:, 1:2]
        sq, logv, rstd, h, sq2, logv2, rstd2, yn, ya, gated, sr, bv, na, nb, da, best, numer, denom, recip = (
            sb(n, [P, N]) for n in ("sq logv rstd h sq2 logv2 rstd2 yn ya gated sr bv na nb da best "
                                    "numer denom recip").split())
        key, val, gate, y = sb("key", [P, 2, N]), sb("val", [P, 3, N]), sb("gate", [P, 4, N]), sb("y", [P, 2, N])
        top, num, den = (sb(n, [P, 2, N + 1]) for n in ("top", "num", "den"))
        ex = sb("ex", [P, 2, 4, N])
        pcen, pvar, pk, pv, pr, pcen2, pvar2, pout = (
            ctx.enter_context(nc.psum_tensor(f"mix_{n}", [P, 512], F32)) for n in
            "pcen pvar pk pv pr pcen2 pvar2 pout".split())
        weights_in, rates_out, passed = sems("weights_in rates_out passed")
        cen_mm, var_mm, k_mm, v_mm, r_mm, cen2_mm, var2_mm, out_mm = sems(
            "cen_mm var_mm k_mm v_mm r_mm cen2_mm var2_mm out_mm")
        sq_out, logv_out, rstd_out, key_out, val_out, er_out, gate_out, a2_out, b2_out, a1_out, b1_out = sems(
            "sq_out logv_out rstd_out key_out val_out er_out gate_out a2_out b2_out a1_out b1_out")
        sq2_out, logv2_out, rstd2_out, ya_out = sems("sq2_out logv2_out rstd2_out ya_out")
        h_out, topc_out, top_out, e2_out, best_out, numc_out, num_out, denc_out, den_out = sems(
            "h_out topc_out top_out e2_out best_out numc_out num_out denc_out den_out")
        numer_out, denom_out, recip_out, y_out, yn_out, sr_out, stream_out = sems(
            "numer_out denom_out recip_out y_out yn_out sr_out stream_out")
        d2_out, d1_out, e1_out, bv_out, na_out, nb_out, da_out, gated_out = sems(
            "d2_out d1_out e1_out bv_out na_out nb_out da_out gated_out")
        block = ctx.enter_context(nc.Block())

        def steps(eng, *stages):
            with eng.Fori(0, PAIRS) as p:
                def ready(sem, c):
                    eng.wait_ge(sem, at(p, K, c + 1))

                def free(sem, c, buffers):
                    eng.wait_ge(sem, at(p, K, c - buffers + 1))

                for s in range(K + 4):
                    for lag, stage in enumerate(stages):
                        if stage and 0 <= s - lag < K:
                            stage(p, s - lag, ready, free)

        def tokens(p, c):
            return kit.stream[:, bass.ds(p, 1), c * N:(c + 1) * N].rearrange("p a n -> p (a n)")

        @block.sync
        def _(sp):
            sp.dma_start(weights[:, :, :].rearrange("p a b -> p (a b)"), kit.d["mix_w"]).then_inc(weights_in, 16)

        @block.tensor
        def _(pe):
            open_all(pe, cen_mm, var_mm, k_mm, v_mm, r_mm, cen2_mm, var2_mm, out_mm)
            pe.wait_ge(weights_in, 16)

            def project(p, c, ready, free):
                free(h_out, c, 1)
                nc.tensor.matmul(pcen[:, 0:N], kit.center[:, :], tokens(p, c), start=True, stop=True).then_inc(cen_mm, 1)
                ready(sq_out, c)
                free(logv_out, c, 1)
                nc.tensor.matmul(pvar[:, 0:N], kit.average[:, :], sq[:, :], start=True, stop=True).then_inc(var_mm, 1)
                ready(h_out, c)
                for i, (bank, used, done) in enumerate(((pk, key_out, k_mm), (pv, val_out, v_mm), (pr, er_out, r_mm))):
                    free(used, c, 1)
                    nc.tensor.matmul(bank[:, 0:N], weights[:, i, :], h[:, :], start=True, stop=True).then_inc(done, 1)

            def norm(p, c, ready, free):
                ready(y_out, c)
                free(yn_out, c, 1)
                nc.tensor.matmul(pcen2[:, 0:N], kit.center[:, :], y[:, c % 2, :], start=True, stop=True).then_inc(cen2_mm, 1)
                ready(sq2_out, c)
                free(logv2_out, c, 1)
                nc.tensor.matmul(pvar2[:, 0:N], kit.average[:, :], sq2[:, :], start=True, stop=True).then_inc(var2_mm, 1)

            def output(p, c, ready, free):
                ready(gated_out, c)
                free(stream_out, c, 1)
                nc.tensor.matmul(pout[:, 0:N], weights[:, 3, :], gated[:, :], start=True, stop=True).then_inc(out_mm, 1)

            steps(pe, project, None, None, norm, output)

        @block.scalar
        def _(act):
            open_all(act, sq_out, logv_out, rstd_out, key_out, val_out, er_out, gate_out, a2_out, b2_out, a1_out,
                     b1_out, sq2_out, logv2_out, rstd2_out, ya_out)
            act.preload_act_table_set(LN_EXP)
            act.wait_ge(rates_out, 2)

            def project(p, c, ready, free):
                ready(cen_mm, c)
                free(var_mm, c, 1)
                nc.scalar.activation(sq[:, :], pcen[:, 0:N], ACT.Square).then_inc(sq_out, 1)
                ready(var_mm, c)
                free(rstd_out, c, 1)
                nc.scalar.activation(logv[:, :], pvar[:, 0:N], ACT.Ln, bias=kit.col("eps")).then_inc(logv_out, 1)
                ready(logv_out, c)
                free(h_out, c, 1)
                nc.scalar.activation(rstd[:, :], logv[:, :], ACT.Exp, scale=-0.5).then_inc(rstd_out, 1)
                ready(k_mm, c)
                free(e1_out, c, 2)
                nc.scalar.activation(key[:, c % 2, :], pk[:, 0:N], ACT.Copy).then_inc(key_out, 1)
                ready(v_mm, c)
                free(nb_out, c, 3)
                nc.scalar.activation(val[:, c % 3, :], pv[:, 0:N], ACT.Copy).then_inc(val_out, 1)
                ready(r_mm, c)
                free(sr_out, c, 4)
                nc.scalar.activation(gate[:, c % 4, :], pr[:, 0:N], ACT.Exp, scale=-1.0).then_inc(er_out, 1)
                ready(er_out, c)
                nc.scalar.activation(gate[:, c % 4, :], gate[:, c % 4, :], ACT.Copy, bias=1.0).then_inc(gate_out, 1)

            def exponentials(p, c, ready, free):
                e = ex[:, c % 2, :, :]
                ready(d2_out, c)
                nc.scalar.activation(e[:, 0, :], e[:, 0, :], ACT.Exp, bias=decay).then_inc(a2_out, 1)
                ready(e2_out, c)
                nc.scalar.activation(e[:, 1, :], e[:, 1, :], ACT.Exp).then_inc(b2_out, 1)
                ready(d1_out, c)
                nc.scalar.activation(e[:, 2, :], e[:, 2, :], ACT.Exp).then_inc(a1_out, 1)
                ready(e1_out, c)
                nc.scalar.activation(e[:, 3, :], e[:, 3, :], ACT.Exp, bias=first).then_inc(b1_out, 1)

            def norm(p, c, ready, free):
                ready(cen2_mm, c)
                free(var2_mm, c, 1)
                nc.scalar.activation(sq2[:, :], pcen2[:, 0:N], ACT.Square).then_inc(sq2_out, 1)
                ready(var2_mm, c)
                free(rstd2_out, c, 1)
                nc.scalar.activation(logv2[:, :], pvar2[:, 0:N], ACT.Ln, bias=kit.col("eps")).then_inc(logv2_out, 1)
                ready(logv2_out, c)
                free(yn_out, c, 1)
                nc.scalar.activation(rstd2[:, :], logv2[:, :], ACT.Exp, scale=-0.5).then_inc(rstd2_out, 1)
                ready(yn_out, c)
                free(gated_out, c, 1)
                nc.scalar.activation(ya[:, :], yn[:, :], ACT.Identity, bias=kit.col("ln_b"),
                                     scale=kit.col("ln_w")).then_inc(ya_out, 1)

            steps(act, project, exponentials, None, norm)

        @block.vector
        def _(dve):
            open_all(dve, h_out, topc_out, top_out, e2_out, best_out, numc_out, num_out, denc_out, den_out,
                     numer_out, denom_out, recip_out, y_out, yn_out, sr_out, stream_out)
            for i, name in enumerate(("decay", "first")):
                nc.vector.tensor_scalar(rates[:, i:i + 1], kit.col(name), 1.0 / T, None, ALU.mult).then_inc(rates_out, 1)
            dve.wait_ge(rates_out, 2)

            def carry(state, c, start, done):
                if c == 0:
                    nc.vector.memset(state[:, 0, 0:1], start).then_inc(done, 1)
                else:
                    nc.vector.tensor_copy(state[:, c % 2, 0:1], state[:, (c - 1) % 2, N:N + 1]).then_inc(done, 1)

            def project(p, c, ready, free):
                ready(rstd_out, c)
                free(r_mm, c, 1)
                nc.vector.tensor_tensor(h[:, :], pcen[:, 0:N], rstd[:, :], ALU.mult).then_inc(h_out, 1)

            def maxima(p, c, ready, free):
                free(d1_out, c, 2)
                free(e2_out, c, 1)
                carry(top, c, -1e38, topc_out)
                ready(topc_out, c)
                ready(key_out, c)
                nc.vector.tensor_tensor_scan(top[:, c % 2, 1:N + 1], decay.broadcast_to([P, N]), key[:, c % 2, :],
                                             top[:, c % 2, 0:1], ALU.add, ALU.max).then_inc(top_out, 1)
                ready(top_out, c)
                free(e1_out, c, 1)
                nc.vector.scalar_tensor_tensor(out=best[:, :], in0=key[:, c % 2, :], scalar=first,
                                               in1=top[:, c % 2, 0:N], op0=ALU.add, op1=ALU.max).then_inc(best_out, 1)
                free(y_out, c, 2)
                nc.vector.tensor_tensor(ex[:, c % 2, 1, :], key[:, c % 2, :], top[:, c % 2, 1:N + 1],
                                        ALU.subtract).then_inc(e2_out, 1)

            def states(p, c, ready, free):
                e = ex[:, c % 2, :, :]
                free(y_out, c, 1)
                carry(den, c, 0.0, denc_out)
                carry(num, c, 0.0, numc_out)
                ready(denc_out, c)
                ready(a2_out, c)
                ready(b2_out, c)
                nc.vector.tensor_tensor_scan(den[:, c % 2, 1:N + 1], e[:, 0, :], e[:, 1, :], den[:, c % 2, 0:1],
                                             ALU.mult, ALU.add).then_inc(den_out, 1)
                ready(numc_out, c)
                ready(bv_out, c)
                nc.vector.tensor_tensor_scan(num[:, c % 2, 1:N + 1], e[:, 0, :], bv[:, :], num[:, c % 2, 0:1],
                                             ALU.mult, ALU.add).then_inc(num_out, 1)
                ready(da_out, c)
                ready(b1_out, c)
                nc.vector.tensor_tensor(denom[:, :], da[:, :], e[:, 3, :], ALU.add).then_inc(denom_out, 1)
                ready(denom_out, c)
                nc.vector.reciprocal(recip[:, :], denom[:, :]).then_inc(recip_out, 1)
                ready(na_out, c)
                ready(nb_out, c)
                nc.vector.tensor_tensor(numer[:, :], na[:, :], nb[:, :], ALU.add).then_inc(numer_out, 1)
                ready(numer_out, c)
                ready(recip_out, c)
                free(cen2_mm, c, 2)
                nc.vector.tensor_tensor(y[:, c % 2, :], numer[:, :], recip[:, :], ALU.mult).then_inc(y_out, 1)

            def norm(p, c, ready, free):
                ready(gate_out, c)
                free(gated_out, c, 1)
                nc.vector.reciprocal(sr[:, :], gate[:, c % 4, :]).then_inc(sr_out, 1)
                ready(rstd2_out, c)
                free(ya_out, c, 1)
                nc.vector.tensor_tensor(yn[:, :], pcen2[:, 0:N], rstd2[:, :], ALU.mult).then_inc(yn_out, 1)

            def output(p, c, ready, free):
                ready(out_mm, c)
                nc.vector.tensor_tensor(tokens(p, c), pout[:, 0:N], tokens(p, c), ALU.add).then_inc(stream_out, 1)

            steps(dve, project, maxima, states, norm, output)

        @block.gpsimd
        def _(gp):
            open_all(gp, d2_out, d1_out, e1_out, bv_out, na_out, nb_out, da_out, gated_out)

            def then(out, in0, in1, op, done):
                gp.sem_inc(passed, 1)
                nc.gpsimd.tensor_tensor(out, in0, in1, op).then_inc(done, 1)

            def exponents(p, c, ready, free):
                old, new = top[:, c % 2, 0:N], top[:, c % 2, 1:N + 1]
                ready(top_out, c)
                free(y_out, c, 2)
                then(ex[:, c % 2, 0, :], old, new, ALU.subtract, d2_out)
                ready(best_out, c)
                then(ex[:, c % 2, 2, :], old, best[:, :], ALU.subtract, d1_out)
                then(ex[:, c % 2, 3, :], key[:, c % 2, :], best[:, :], ALU.subtract, e1_out)

            def states(p, c, ready, free):
                e = ex[:, c % 2, :, :]
                ready(b2_out, c)
                ready(val_out, c)
                free(num_out, c, 1)
                then(bv[:, :], e[:, 1, :], val[:, c % 3, :], ALU.mult, bv_out)
                ready(b1_out, c)
                free(numer_out, c, 1)
                then(nb[:, :], e[:, 3, :], val[:, c % 3, :], ALU.mult, nb_out)
                ready(den_out, c)
                ready(a1_out, c)
                free(denom_out, c, 1)
                then(da[:, :], e[:, 2, :], den[:, c % 2, 0:N], ALU.mult, da_out)
                ready(num_out, c)
                then(na[:, :], e[:, 2, :], num[:, c % 2, 0:N], ALU.mult, na_out)

            def norm(p, c, ready, free):
                ready(ya_out, c)
                ready(sr_out, c)
                free(out_mm, c, 1)
                then(gated[:, :], ya[:, :], sr[:, :], ALU.mult, gated_out)

            steps(gp, None, exponents, states, norm)


def experts(kit):
    nc = kit.nc
    N, G = CHUNK, 2 * NBLK
    with ExitStack() as ctx:
        sb = lambda name, shape, dt=F32: ctx.enter_context(nc.sbuf_tensor(f"moe_{name}", shape, dt))
        sem = lambda name: ctx.enter_context(kit.semaphore(f"moe_{name}"))
        sems = lambda names: [sem(n) for n in names.split()]
        w1, b1, w2 = sb("w1", [P, E, FF]), sb("b1", [P, E]), sb("w2", [P, E, C])
        w2b, gate_w, gate_b = sb("w2b", [2 * E, P]), sb("gate_w", [P, 2 * E]), sb("gate_b", [P, G * E])
        gamma, beta, iota = sb("gamma", [P, C]), sb("beta", [P, C]), sb("iota", [P, E])
        xs, sq, logv, rstd = (sb(n, [P, N]) for n in ("xs", "sq", "logv", "rstd"))
        h = sb("h", [P, 2, N])
        xt, acc = sb("xt", [BLK, 2, G, C]), sb("acc", [BLK, 2, G, C])
        logits = sb("logits", [BLK, G, E])
        best, place = sb("best", [BLK, G, 8]), sb("place", [BLK, G, 8], U32)
        placef = sb("placef", [BLK, G, 2])
        gap, egap, denom, wbest, wnext = (sb(n, [BLK, G]) for n in "gap egap denom wbest wnext".split())
        is_best, is_next, part_best, part_next = (sb(n, [BLK, G, E]) for n in "is_best is_next part_best part_next".split())
        wt = sb("wt", [BLK, 2, G, E])
        wtt = sb("wtt", [2 * E, N])
        hidden = sb("hidden", [P, 2, 2, N])
        scaled = sb("scaled", [BLK, 2, G, C])
        total, mean, sqsum, flogv, frstd = (sb(n, [BLK, G]) for n in "total mean sqsum flogv frstd".split())
        dev, devsq, fnorm, fgain, fshift = (sb(n, [BLK, G, C]) for n in "dev devsq fnorm fgain fshift".split())
        result = sb("result", [BLK, 2, G, C])
        ps = lambda name, *shape: ctx.enter_context(nc.psum_tensor(f"moe_{name}", [P, *shape], F32))
        pcen, pvar, pturn, phid, pout = ps("pcen", 512), ps("pvar", 512), ps("pturn", 512), ps("phid", 3, 512), ps("pout", 2, 512)
        weights_in, passed = sems("weights_in passed")
        cen_mm, var_mm, xt_mm, logit_mm, wtt_mm, h_mm, up_mm, down_mm = sems(
            "cen_mm var_mm xt_mm logit_mm wtt_mm h_mm up_mm down_mm")
        sq_out, logv_out, rstd_out, xt_out, egap_out, wtt_out, acc_in, hidden_act, devsq_out, flogv_out, frstd_out = sems(
            "sq_out logv_out rstd_out xt_out egap_out wtt_out acc_in hidden_act devsq_out flogv_out frstd_out")
        h_out, logits_out, best_out, place_out, placef_out, gap_out, denom_out, wbest_out, wnext_out = sems(
            "h_out logits_out best_out place_out placef_out gap_out denom_out wbest_out wnext_out")
        is_out, part_out, wt_out, hidden_dve, scaled_out, total_out, mean_out, sqsum_out, fnorm_out = sems(
            "is_out part_out wt_out hidden_dve scaled_out total_out mean_out sqsum_out fnorm_out")
        xs_in, acc_out, dev_out, fgain_out, fshift_out, result_out = sems(
            "xs_in acc_out dev_out fgain_out fshift_out result_out")
        stored = sems("stored0 stored1")
        block = ctx.enter_context(nc.Block())
        WEIGHTS = (("w1", w1), ("b1", b1), ("w2", w2), ("w2b", w2b), ("gate_w", gate_w), ("gate_b", gate_b),
                   ("gamma", gamma), ("beta", beta), ("iota", iota))

        def at(chunk, per, k):
            value = chunk * per + k
            return max(value, 0) + 1 if isinstance(value, int) else value + 1

        def turns(eng, body):
            body(0, 0, True, False, 0)
            with eng.Fori(0, (CHUNKS - 3) // 2) as t:
                body(2 * t + 1, 1, False, False, t)
                body(2 * t + 2, 0, False, False, t)
            body(CHUNKS - 2, 1, False, False, (CHUNKS - 3) // 2)
            body(CHUNKS - 1, 0, False, True, (CHUNKS - 3) // 2)

        @block.sync
        def _(sp):
            for sem in stored:
                sp.sem_inc(sem, 16)
            for name, t in WEIGHTS:
                dst = t[:, :] if len(t.shape) == 2 else t[:, :, :].rearrange("p a b -> p (a b)")
                sp.dma_start(dst, kit.d[name]).then_inc(weights_in, 16)

            def body(j, buf, first, last, stores):
                sp.wait_ge(result_out, at(j, 1, 1))
                sp.dma_start(kit.out[bass.ds(j, 1), :, :].rearrange("a t c -> (a t) c"),
                             result[:, buf, :, :].rearrange("p g c -> p (g c)")).then_inc(stored[buf], 16)

            turns(sp, body)
            sp.wait_ge(stored[0], 16 * ((CHUNKS + 1) // 2) + 16)
            sp.wait_ge(stored[1], 16 * (CHUNKS // 2) + 16)

        @block.tensor
        def _(pe):
            open_all(pe, cen_mm, var_mm, xt_mm, logit_mm, wtt_mm, h_mm, up_mm, down_mm)
            pe.wait_ge(weights_in, 16 * len(WEIGHTS))
            blocks = [slice(k * BLK, (k + 1) * BLK) for k in range(NBLK)]

            def center(j):
                pe.wait_ge(xs_in, at(j, 1, 1))
                pe.wait_ge(h_out, at(j, 1, 0))
                nc.tensor.matmul(pcen[:, 0:N], kit.center[:, :], xs[:, :], start=True, stop=True).then_inc(cen_mm, 1)
                pe.wait_ge(acc_in, at(j, 1, 0))
                for k, b in enumerate(blocks):
                    done = nc.tensor.transpose(pturn[0:BLK, k * P:(k + 1) * P], xs[:, b], kit.ident[:, :])
                done.then_inc(xt_mm, 1)

            def variance(j):
                pe.wait_ge(sq_out, at(j, 1, 1))
                pe.wait_ge(wtt_out, at(j, 1, 0))
                nc.tensor.matmul(pvar[:, 0:N], kit.average[:, :], sq[:, :], start=True, stop=True).then_inc(var_mm, 1)

            def gate(j, buf):
                pe.wait_ge(h_out, at(j, 1, 1))
                pe.wait_ge(logv_out, at(j, 1, 1))
                for k, b in enumerate(blocks):
                    done = nc.tensor.matmul(pvar[0:BLK, k * 2 * E:(k + 1) * 2 * E], h[:, buf, b], gate_w[:, :],
                                            start=True, stop=True)
                done.then_inc(logit_mm, 1)

            def turn_weights(j, buf):
                pe.wait_ge(wt_out, at(j, 1, 1))
                pe.wait_ge(logits_out, at(j, 1, 1))
                for k, b in enumerate(blocks):
                    done = nc.tensor.transpose(pvar[0:2 * E, b], wt[:, buf, 2 * k:2 * k + 2, :].rearrange("p g e -> p (g e)"),
                                               kit.ident[0:BLK, 0:BLK])
                done.then_inc(wtt_mm, 1)

            def start_sum(j, buf):
                pe.wait_ge(wtt_out, at(j, 1, 1))
                pe.wait_ge(xt_out, at(j, 1, 1))
                for k, b in enumerate(blocks):
                    dst = pturn[0:BLK, k * P:(k + 1) * P]
                    nc.tensor.matmul(dst, h[:, buf, b], kit.ident[:, :], start=True, stop=False)
                    done = nc.tensor.matmul(dst, wtt[:, b], w2b[:, :], start=False, stop=True)
                done.then_inc(h_mm, 1)

            def up(j, buf, e):
                for b in (0, 1):
                    i = 2 * e + b
                    half = slice(C * b, C * b + C)
                    if i < 3:
                        pe.wait_ge(hidden_act, at(j, E, 0))
                        pe.wait_ge(hidden_dve, at(j, E, 0))
                    else:
                        pe.wait_ge((hidden_act, hidden_dve)[(i - 3) % 2], at(j, E, (i - 3) // 2 + 1))
                    nc.tensor.matmul(phid[:, i % 3, 0:N], w1[half, e, :], h[half, buf, :],
                                     start=True, stop=True).then_inc(up_mm, 1)

            def down(j, e):
                pe.wait_ge(scaled_out, at(j, E, e - 1))
                for b in (0, 1):
                    pe.wait_ge((hidden_act, hidden_dve)[b], at(j, E, e + 1))
                    for k, blk in enumerate(blocks):
                        g = 2 * k + b
                        done = nc.tensor.matmul(pout[0:BLK, e % 2, g * C:(g + 1) * C], hidden[:, e % 2, b, blk],
                                                w2[:, e, :], start=True, stop=True)
                done.then_inc(down_mm, 1)

            def ahead(e, j, buf):
                if e == 0:
                    center(j)
                if e == 1:
                    variance(j)
                if e == 3:
                    gate(j, buf)
                if e == 11:
                    turn_weights(j, buf)
                if e == 14:
                    start_sum(j, buf)

            for e in range(E):
                ahead(e, 0, 0)

            def body(j, buf, first, last, stores):
                for e in range(E + 1):
                    if e < E:
                        up(j, buf, e)
                        if not last:
                            ahead(e, j + 1, 1 - buf)
                    if e > 0:
                        down(j, e - 1)

            turns(pe, body)

        @block.scalar
        def _(act):
            open_all(act, sq_out, logv_out, rstd_out, xt_out, egap_out, wtt_out, acc_in, hidden_act, devsq_out,
                     flogv_out, frstd_out)
            act.preload_act_table_set(LN_EXP)
            act.wait_ge(weights_in, 16 * len(WEIGHTS))

            def ahead(e, j, buf):
                if e == 0:
                    act.wait_ge(cen_mm, at(j, 1, 1))
                    act.wait_ge(var_mm, at(j, 1, 0))
                    nc.scalar.activation(sq[:, :], pcen[:, 0:N], ACT.Square).then_inc(sq_out, 1)
                if e == 2:
                    act.wait_ge(var_mm, at(j, 1, 1))
                    act.wait_ge(rstd_out, at(j, 1, 0))
                    nc.scalar.activation(logv[:, :], pvar[:, 0:N], ACT.Ln, bias=kit.col("eps")).then_inc(logv_out, 1)
                    act.wait_ge(logv_out, at(j, 1, 1))
                    act.wait_ge(h_out, at(j, 1, 0))
                    nc.scalar.activation(rstd[:, :], logv[:, :], ACT.Exp, scale=-0.5).then_inc(rstd_out, 1)
                if e == 9:
                    act.wait_ge(gap_out, at(j, 1, 1))
                    act.wait_ge(wnext_out, at(j, 1, 0))
                    nc.scalar.activation(egap[:, :], gap[:, :], ACT.Exp).then_inc(egap_out, 1)
                if e == 12:
                    act.wait_ge(xt_mm, at(j, 1, 1))
                    act.wait_ge(result_out, at(j, 1, -1))
                    nc.scalar.activation(xt[:, buf, :, :].rearrange("p g c -> p (g c)"), pturn[0:BLK, :],
                                         ACT.Copy).then_inc(xt_out, 1)
                    act.wait_ge(wtt_mm, at(j, 1, 1))
                    act.wait_ge(h_mm, at(j, 1, 0))
                    nc.scalar.activation(wtt[:, :], pvar[0:2 * E, 0:N], ACT.Copy).then_inc(wtt_out, 1)
                if e == 15:
                    act.wait_ge(h_mm, at(j, 1, 1))
                    act.wait_ge(dev_out, at(j, 1, -1))
                    nc.scalar.activation(acc[:, buf, :, :].rearrange("p g c -> p (g c)"), pturn[0:BLK, :],
                                         ACT.Copy).then_inc(acc_in, 1)

            def finish(e, j):
                if e == 4:
                    act.wait_ge(dev_out, at(j, 1, 1))
                    act.wait_ge(sqsum_out, at(j, 1, 0))
                    nc.scalar.activation(devsq[:, :, :], dev[:, :, :], ACT.Square).then_inc(devsq_out, 1)
                if e == 6:
                    act.wait_ge(sqsum_out, at(j, 1, 1))
                    act.wait_ge(frstd_out, at(j, 1, 0))
                    nc.scalar.activation(flogv[:, :], sqsum[:, :], ACT.Ln, bias=kit.cols[0:BLK, CI["eps"]:CI["eps"] + 1],
                                         scale=1.0 / C).then_inc(flogv_out, 1)
                    act.wait_ge(flogv_out, at(j, 1, 1))
                    act.wait_ge(fnorm_out, at(j, 1, 0))
                    nc.scalar.activation(frstd[:, :], flogv[:, :], ACT.Exp, scale=-0.5).then_inc(frstd_out, 1)

            for e in range(E):
                ahead(e, 0, 0)

            def body(j, buf, first, last, stores):
                for e in range(E):
                    i = 2 * e
                    act.wait_ge(up_mm, at(j, 2 * E, i + 1))
                    act.wait_ge(down_mm, at(j, E, e - 1))
                    nc.scalar.activation(hidden[:, e % 2, 0, :], phid[:, i % 3, 0:N], ACT.Relu,
                                         bias=b1[:, e:e + 1]).then_inc(hidden_act, 1)
                    if not last:
                        ahead(e, j + 1, 1 - buf)
                    if not first:
                        finish(e, j - 1)

            turns(act, body)
            for e in range(E):
                finish(e, CHUNKS - 1)

        @block.vector
        def _(dve):
            open_all(dve, h_out, logits_out, best_out, place_out, placef_out, gap_out, denom_out, wbest_out, wnext_out,
                     is_out, part_out, wt_out, hidden_dve, scaled_out, total_out, mean_out, sqsum_out, fnorm_out)
            dve.wait_ge(weights_in, 16 * len(WEIGHTS))
            wide = lambda t: t.unsqueeze(2).broadcast_to([BLK, G, E])

            def settled():
                dve.sem_inc(passed, 1)

            def ahead(e, j, buf):
                if e == 2:
                    dve.wait_ge(rstd_out, at(j, 1, 1))
                    dve.wait_ge(h_mm, at(j, 1, -1))
                    dve.wait_ge(up_mm, at(j, 2 * E, -2 * E))
                    nc.vector.tensor_tensor(h[:, buf, :], pcen[:, 0:N], rstd[:, :], ALU.mult).then_inc(h_out, 1)
                if e == 4:
                    dve.wait_ge(logit_mm, at(j, 1, 1))
                    dve.wait_ge(place_out, at(j, G, 0))
                    nc.vector.tensor_tensor(logits[:, :, :].rearrange("p g e -> p (g e)"), pvar[0:BLK, 0:G * E],
                                            gate_b[0:BLK, :], ALU.add).then_inc(logits_out, 1)
                    dve.wait_ge(logits_out, at(j, 1, 1))
                    dve.wait_ge(gap_out, at(j, 1, 0))
                    settled()
                    for g in range(G):
                        nc.vector.max(best[:, g, :], logits[:, g, :]).then_inc(best_out, 1)
                if e == 5:
                    dve.wait_ge(best_out, at(j, G, G))
                    dve.wait_ge(placef_out, at(j, 1, 0))
                    settled()
                    for g in range(G):
                        nc.vector.max_index(place[:, g, :], best[:, g, :], logits[:, g, :]).then_inc(place_out, 1)
                if e == 6:
                    dve.wait_ge(egap_out, at(j, 1, 0))
                    nc.vector.tensor_tensor(gap[:, :], best[:, :, 1], best[:, :, 0], ALU.subtract).then_inc(gap_out, 1)
                    dve.wait_ge(place_out, at(j, G, G))
                    dve.wait_ge(is_out, at(j, 2, 0))
                    nc.vector.tensor_copy(placef[:, :, :], place[:, :, 0:2]).then_inc(placef_out, 1)
                if e == 7:
                    dve.wait_ge(placef_out, at(j, 1, 1))
                    dve.wait_ge(part_out, at(j, 2, 0))
                    for which, t in enumerate((is_best, is_next)):
                        nc.vector.tensor_tensor(t[:, :, :], iota[0:BLK, :].unsqueeze(1).broadcast_to([BLK, G, E]),
                                                wide(placef[:, :, which]), ALU.is_equal).then_inc(is_out, 1)
                if e == 9:
                    dve.wait_ge(egap_out, at(j, 1, 1))
                    dve.wait_ge(wbest_out, at(j, 1, 0))
                    nc.vector.tensor_scalar(denom[:, :], egap[:, :], 1.0, None, ALU.add).then_inc(denom_out, 1)
                    dve.wait_ge(denom_out, at(j, 1, 1))
                    dve.wait_ge(part_out, at(j, 2, 0))
                    nc.vector.reciprocal(wbest[:, :], denom[:, :]).then_inc(wbest_out, 1)
                    dve.wait_ge(wbest_out, at(j, 1, 1))
                    nc.vector.tensor_tensor(wnext[:, :], egap[:, :], wbest[:, :], ALU.mult).then_inc(wnext_out, 1)
                if e == 10:
                    dve.wait_ge(wnext_out, at(j, 1, 1))
                    dve.wait_ge(is_out, at(j, 2, 2))
                    dve.wait_ge(wt_out, at(j, 1, 0))
                    nc.vector.tensor_tensor(part_best[:, :, :], is_best[:, :, :], wide(wbest[:, :]), ALU.mult).then_inc(part_out, 1)
                    nc.vector.tensor_tensor(part_next[:, :, :], is_next[:, :, :], wide(wnext[:, :]), ALU.mult).then_inc(part_out, 1)
                    dve.wait_ge(part_out, at(j, 2, 2))
                    dve.wait_ge(scaled_out, at(j, E, -E))
                    dve.wait_ge(wtt_mm, at(j, 1, -1))
                    nc.vector.tensor_tensor(wt[:, buf, :, :], part_best[:, :, :], part_next[:, :, :], ALU.add).then_inc(wt_out, 1)

            def finish(e, j, buf):
                if e == 1:
                    dve.wait_ge(acc_out, at(j, E, E))
                    dve.wait_ge(mean_out, at(j, 1, 0))
                    nc.vector.tensor_reduce(total[:, :], acc[:, buf, :, :], AX_X, ALU.add).then_inc(total_out, 1)
                    dve.wait_ge(total_out, at(j, 1, 1))
                    dve.wait_ge(dev_out, at(j, 1, 0))
                    nc.vector.tensor_scalar(mean[:, :], total[:, :], 1.0 / C, None, ALU.mult).then_inc(mean_out, 1)
                if e == 5:
                    dve.wait_ge(devsq_out, at(j, 1, 1))
                    dve.wait_ge(flogv_out, at(j, 1, 0))
                    nc.vector.tensor_reduce(sqsum[:, :], devsq[:, :, :], AX_X, ALU.add).then_inc(sqsum_out, 1)
                if e == 7:
                    dve.wait_ge(frstd_out, at(j, 1, 1))
                    dve.wait_ge(fgain_out, at(j, 1, 0))
                    nc.vector.tensor_tensor(fnorm[:, :, :], dev[:, :, :],
                                            frstd[:, :].unsqueeze(2).broadcast_to([BLK, G, C]), ALU.mult).then_inc(fnorm_out, 1)

            for e in range(E):
                ahead(e, 0, 0)

            def body(j, buf, first, last, stores):
                for e in range(E + 1):
                    if e < E:
                        i = 2 * e + 1
                        dve.wait_ge(up_mm, at(j, 2 * E, i + 1))
                        dve.wait_ge(down_mm, at(j, E, e - 1))
                        nc.vector.tensor_scalar(hidden[:, e % 2, 1, :], phid[:, i % 3, 0:N], b1[:, e:e + 1], 0.0,
                                                ALU.add, ALU.max).then_inc(hidden_dve, 1)
                    if e > 0:
                        f = e - 1
                        dve.wait_ge(down_mm, at(j, E, f + 1))
                        dve.wait_ge(acc_out, at(j, E, f - 1))
                        nc.vector.tensor_tensor(scaled[:, f % 2, :, :], pout[0:BLK, f % 2, :].rearrange("p (g c) -> p g c", c=C),
                                                wt[:, buf, :, f].unsqueeze(2).broadcast_to([BLK, G, C]),
                                                ALU.mult).then_inc(scaled_out, 1)
                    if e < E and not last:
                        ahead(e, j + 1, 1 - buf)
                    if e < E and not first:
                        finish(e, j - 1, 1 - buf)

            turns(dve, body)
            for e in range(E):
                finish(e, CHUNKS - 1, 0)

        @block.gpsimd
        def _(gp):
            open_all(gp, xs_in, acc_out, dev_out, fgain_out, fshift_out, result_out)
            gp.wait_ge(weights_in, 16 * len(WEIGHTS))
            flat = kit.stream[:, :, :].rearrange("p n t -> p (n t)")

            def settled():
                gp.sem_inc(passed, 1)

            def ahead(e, j):
                if e == 0:
                    gp.wait_ge(xt_mm, at(j, 1, 0))
                    settled()
                    nc.gpsimd.tensor_copy(xs[:, :], flat[:, bass.ds(j * N, N)]).then_inc(xs_in, 1)

            def finish(e, j, buf, stores):
                if e == 1:
                    gp.wait_ge(mean_out, at(j, 1, 1))
                    gp.wait_ge(fnorm_out, at(j, 1, 0))
                    settled()
                    nc.gpsimd.tensor_tensor(dev[:, :, :], acc[:, buf, :, :],
                                            mean[:, :].unsqueeze(2).broadcast_to([BLK, G, C]), ALU.subtract).then_inc(dev_out, 1)
                if e == 8:
                    gp.wait_ge(fnorm_out, at(j, 1, 1))
                    gp.wait_ge(fshift_out, at(j, 1, 0))
                    settled()
                    nc.gpsimd.tensor_tensor(fgain[:, :, :], fnorm[:, :, :],
                                            gamma[0:BLK, :].unsqueeze(1).broadcast_to([BLK, G, C]), ALU.mult).then_inc(fgain_out, 1)
                if e == 9:
                    gp.wait_ge(fgain_out, at(j, 1, 1))
                    gp.wait_ge(result_out, at(j, 1, 0))
                    settled()
                    nc.gpsimd.tensor_tensor(fshift[:, :, :], fgain[:, :, :],
                                            beta[0:BLK, :].unsqueeze(1).broadcast_to([BLK, G, C]), ALU.add).then_inc(fshift_out, 1)
                if e == 10:
                    gp.wait_ge(fshift_out, at(j, 1, 1))
                    gp.wait_ge(stored[buf], 16 * stores + 16)
                    settled()
                    nc.gpsimd.tensor_tensor(result[:, buf, :, :], fshift[:, :, :], xt[:, buf, :, :], ALU.add).then_inc(result_out, 1)

            ahead(0, 0)

            def body(j, buf, first, last, stores):
                for e in range(E):
                    if not last:
                        ahead(e, j + 1)
                    gp.wait_ge(scaled_out, at(j, E, e + 1))
                    gp.wait_ge(acc_out, at(j, E, e))
                    if e == 0:
                        gp.wait_ge(acc_in, at(j, 1, 1))
                    settled()
                    nc.gpsimd.tensor_tensor(acc[:, buf, :, :], acc[:, buf, :, :], scaled[:, e % 2, :, :],
                                            ALU.add).then_inc(acc_out, 1)
                    if not first:
                        finish(e, j - 1, 1 - buf, stores)

            turns(gp, body)
            for e in range(E):
                finish(e, CHUNKS - 1, 0, CHUNKS // 2)


STAGES = [(embed,), (text,), (window_attention, 0), (mlp, 0), (window_attention, 1), (mlp, 1), (time_mix,), (experts,)]


def build(nc, d, out):
    with ExitStack() as ctx:
        kit = Kit(nc, ctx, d)
        kit.out = out
        setup(kit)
        kit.clear()
        for stage, *args in STAGES:
            stage(kit, *args)
            kit.clear()

def block_diag(m):
    z = np.zeros((2 * m.shape[0], 2 * m.shape[1]), m.dtype)
    z[:m.shape[0], :m.shape[1]] = m
    z[m.shape[0]:, m.shape[1]:] = m
    return z


def stack2(m):
    return np.concatenate([m, m], axis=0)


def shape_constants():
    f = np.float32
    average = block_diag(np.full((C, C), 1.0 / C, f))
    center = np.eye(P, dtype=f) - average
    row = np.arange(P)[:, None]
    fold = ((row % QPAD) == np.arange(WIN)[None, :]).astype(f)
    headmask = ((row % C) // HD == np.arange(NH)[None, :]).astype(f)
    dup = (np.arange(2 * WIN) // WIN)[:, None]
    vmask = (dup == (np.arange(4 * P)[None, :] // HD) % 2).astype(f)
    vones = np.tile((dup == np.arange(2)[None, :]).astype(f), (1, 2 * GROUPS))
    img = np.zeros((SIDE, SIDE), np.int32)
    n = 0
    for h in (slice(0, -WS), slice(-WS, -SHIFT), slice(-SHIFT, None)):
        for w in (slice(0, -WS), slice(-WS, -SHIFT), slice(-SHIFT, None)):
            n += 1
            img[h, w] = n
    mw = img.reshape(NWIN, WS, NWIN, WS).transpose(0, 2, 1, 3).reshape(NWIN, NWIN, WIN)
    amask = np.zeros((P, 4, NH, WIN), f)
    for kind in range(4):
        m = mw[NWIN - 1 if kind // 2 else 0, NWIN - 1 if kind % 2 else 0]
        a = np.where(m[None, :] != m[:, None], -100.0, 0.0).astype(f)
        for b in (0, 1):
            amask[QPAD * b:QPAD * b + WIN, kind] = a[:, None, :]
    iota = np.broadcast_to(np.arange(E, dtype=f), (P, E)).copy()
    power = np.array([pow(31, j, TBL) for j in range(HIST)], f)
    return dict(average=average, center=center, ident=np.eye(P, dtype=f), fold=fold, headmask=headmask,
                vmask=vmask, vones=vones, amask=amask.reshape(P, -1), iota=iota,
                hashes=np.broadcast_to(np.tile(power, TXT_COLS), (TXT_P, TXT_COLS * HIST)).copy(),
                fresh=np.broadcast_to(np.tile((np.arange(HIST) > 0).astype(f), TXT_COLS),
                                      (TXT_P, TXT_COLS * HIST)).copy(),
                tablebase=np.broadcast_to(np.tile(np.arange(SIZES, dtype=f) * (TBL + 1), TXT_COLS),
                                          (TXT_P, TXT_COLS * SIZES)).copy())


def lay_out(i):
    a = {k.replace("L0_", ""): np.asarray(v) for k, v in i.items()}
    f = np.float32
    d = shape_constants()
    d["patches"] = a["x"].reshape(PAIRS, 2, SIDE, 4, SIDE, 4).transpose(1, 3, 5, 0, 2, 4).reshape(32, PAIRS * NIMG)
    d["pe_w"] = block_diag(a["tok_pe_w"].reshape(C, 16).T)
    cols = {"pe_b": a["tok_pe_b"], "pe_ng": a["tok_pe_ng"], "pe_nb": a["tok_pe_nb"],
            "decay": a["attn_spatial_decay"], "first": a["attn_spatial_first"],
            "eps": np.full(C, EPS, f), "ln_w": a["attn_ln_w"], "ln_b": a["attn_ln_b"]}
    coords = np.stack(np.meshgrid(np.arange(WS), np.arange(WS), indexing="ij")).reshape(2, -1)
    rel = (coords[:, :, None] - coords[:, None, :]) + WS - 1
    rpi = rel[0] * (2 * WS - 1) + rel[1]
    for l in (0, 1):
        for n in ("n1g", "n1b", "n2g", "n2b", "b2"):
            cols[f"{n}{l}"] = a[f"tok_{n}"][l]
        qkvb = a["tok_qkv_b"][l].reshape(3, C)
        cols[f"bq{l}"], cols[f"bk{l}"], cols[f"bv{l}"] = qkvb
        cols[f"bp{l}"] = a["tok_proj_b"][l]
        cols[f"b1lo{l}"], cols[f"b1hi{l}"] = a["tok_b1"][l].reshape(2, P)
        qkvw = a["tok_qkv_w"][l].reshape(3, C, C)
        d[f"attn_w{l}"] = np.concatenate([block_diag(m.T) for m in (*qkvw, a["tok_proj_w"][l])], axis=1)
        bias = np.zeros((P, NH, WIN), f)
        table = a["tok_rpb"][l][rpi].transpose(0, 2, 1)
        for b in (0, 1):
            bias[QPAD * b:QPAD * b + WIN] = table
        d[f"relbias{l}"] = bias.reshape(P, -1)
        d[f"up{l}"] = stack2(a["tok_w1"][l].T)
        down = np.zeros((P, 2, 2, P), f)
        for half in (0, 1):
            for b in (0, 1):
                down[:, half, b, C * b:C * b + C] = a["tok_w2"][l][:, P * half:P * half + P].T
        d[f"down{l}"] = down.reshape(P, -1)
    d["cols"] = np.stack([v if v.shape[0] == P else np.concatenate([v, v]) for v in (cols[n] for n in COLS)], axis=1)
    d["mix_w"] = np.concatenate([block_diag(a[f"attn_W{n}"].T) for n in "kvro"], axis=1)
    d["gate_w"] = block_diag(a["ffn_gate_w"])
    d["gate_b"] = np.broadcast_to(np.tile(a["ffn_gate_b"], 2 * NBLK), (P, 2 * NBLK * E)).copy()
    d["w1"] = stack2(a["ffn_w1"].transpose(1, 0, 2).reshape(C, E * FF))
    d["b1"] = a["ffn_b1"].T
    d["w2"] = a["ffn_w2"].transpose(1, 0, 2).reshape(FF, E * C)
    d["w2b"] = block_diag(a["ffn_b2"])
    d["gamma"] = np.broadcast_to(a["ffn_gamma"], (P, C)).copy()
    d["beta"] = np.broadcast_to(a["ffn_beta"], (P, C)).copy()
    txt = a["x_txt"]
    padded = np.concatenate([np.zeros((B, HIST - 1), txt.dtype), txt], axis=1)
    history = np.stack([padded[:, HIST - 1 - j:HIST - 1 - j + NTXT] for j in range(HIST)], axis=2)
    d["history"] = history.reshape(TXT_COLS, TXT_P, HIST).transpose(1, 0, 2).reshape(TXT_P, TXT_COLS * HIST)
    d["tables"] = a["txt_tables"].reshape(SIZES * (TBL + 1), C)
    return {k: np.ascontiguousarray(v) for k, v in d.items()}


def kernel(**inputs):
    import concourse.bacc as bacc
    from concourse.bass_utils import run_bass_kernel_spmd

    data = lay_out(inputs)
    nc = bacc.Bacc("TRN2", target_bir_lowering=False, num_devices=1)
    d = {k: nc.dram_tensor("in_" + k, data[k].shape, mybir.dt.from_np(data[k].dtype), kind="ExternalInput").ap() for k in data}
    out = nc.dram_tensor("fused_out", [CHUNKS, BLK, NBLK * P], F32, kind="ExternalOutput").ap()
    build(nc, d, out)
    got = run_bass_kernel_spmd(nc, [{"in_" + k: data[k] for k in data}], core_ids=[0]).results[0]["fused_out"]
    y = got.reshape(CHUNKS, BLK, NBLK, 2, C).transpose(3, 0, 2, 1, 4).reshape(2, PAIRS, T, C)
    return np.ascontiguousarray(y.transpose(1, 0, 2, 3).reshape(B, T, C))
```

```python
from contextlib import ExitStack, contextmanager

import numpy as np

import concourse.bass as bass
from concourse import mybir

F32 = mybir.dt.float32
I32 = mybir.dt.int32
U32 = mybir.dt.uint32
F32R = mybir.dt.float32r
ALU = mybir.AluOpType
ACT = mybir.ActivationFunctionType
AX_X = mybir.AxisListType.X

P = 128
B = 16
PAIRS = B // 2
C = 64
SIDE = 56
NIMG = SIDE * SIDE
NTXT = 77
T = NIMG + NTXT
WS = 7
WIN = WS * WS
NWIN = SIDE // WS
STRIP = WS * SIDE
STRIPS = NIMG // STRIP
NH = 8
HD = C // NH
SHIFT = WS // 2
QPAD = 64
GROUPS = NH // 2
VA = 2 * HD + 2
EPS = 1e-5
OPEN = 64
LN_EXP = "natural_log_exp_and_others"
SIZES = 18
TBL = 1024
HIST = 20
TXT_P = 112
TXT_COLS = B * NTXT // TXT_P
E = 16
FF = 128
BLK = 126
NBLK = 4
CHUNK = BLK * NBLK
CHUNKS = PAIRS * T // CHUNK
TCH = 459
TCHS = T // TCH
assert CHUNKS * CHUNK == PAIRS * T and TCHS * TCH == T and TXT_P * TXT_COLS == B * NTXT

COLS = ["pe_b", "pe_ng", "pe_nb"]
for _l in (0, 1):
    COLS += [f"{n}{_l}" for n in ("n1g", "n1b", "bq", "bk", "bv", "bp", "n2g", "n2b", "b2", "b1lo", "b1hi")]
COLS += ["decay", "first", "ln_w", "ln_b", "eps"]
CI = {n: i for i, n in enumerate(COLS)}


def at(turn, per, k):
    return turn * per + k + OPEN


def open_all(eng, *sems):
    for s in sems:
        eng.sem_inc(s, OPEN)


class Kit:

    def __init__(self, nc, ctx, d):
        self.nc, self.d, self.used = nc, d, []
        sb = lambda name, shape, dt=F32: ctx.enter_context(nc.sbuf_tensor(name, shape, dt))
        self.stream = sb("stream", [P, PAIRS, T])
        self.cols = sb("cols", [P, len(COLS)])
        self.center = sb("center", [P, P])
        self.average = sb("average", [P, P])
        self.ident = sb("ident", [P, P])
        self.gathered = [ctx.enter_context(nc.semaphore(f"gathered{i}")) for i in range(TXT_COLS)]

    @contextmanager
    def semaphore(self, name):
        with self.nc.semaphore(name) as sem:
            self.used.append(sem)
            yield sem

    def clear(self):
        with self.nc.Block() as block:
            @block.gpsimd
            def _(gp):
                for sem in self.used:
                    gp.sem_clear(sem)
        self.used = []

    def col(self, name):
        return self.cols[:, CI[name]:CI[name] + 1]


def setup(kit):
    nc = kit.nc
    with kit.semaphore("consts_in") as consts_in, nc.Block() as block:
        @block.sync
        def _(sp):
            for dst, name in ((kit.cols, "cols"), (kit.center, "center"), (kit.average, "average"),
                              (kit.ident, "ident")):
                sp.dma_start(dst[:, :], kit.d[name]).then_inc(consts_in, 16)
            sp.wait_ge(consts_in, 64)


def hash_text(kit, ids):
    nc = kit.nc
    NC = TXT_COLS
    with ExitStack() as ctx:
        sb = lambda name, shape, dt=F32: ctx.enter_context(nc.sbuf_tensor(f"txt_{name}", shape, dt))
        history = sb("history", [TXT_P, NC * HIST], I32)
        powers, fresh = sb("powers", [TXT_P, NC * HIST]), sb("fresh", [TXT_P, NC * HIST])
        base = sb("base", [TXT_P, NC * SIZES])
        byte, low, ok, bad, safe, term, total, anybad = (
            sb(n, [TXT_P, NC * HIST]) for n in "byte low ok bad safe term total anybad".split())
        whole, masked = sb("whole", [TXT_P, NC, HIST], I32), sb("masked", [TXT_P, NC, HIST], I32)
        hashed, good, kept, row = (sb(n, [TXT_P, NC, HIST]) for n in "hashed good kept row".split())
        inputs_in = ctx.enter_context(kit.semaphore("txt_inputs_in"))
        steps = ctx.enter_context(kit.semaphore("txt_steps"))
        block = ctx.enter_context(nc.Block())

        @block.sync
        def _(sp):
            for dst, name in ((history, "history"), (powers, "hashes"), (fresh, "fresh"), (base, "tablebase")):
                sp.dma_start(dst[:, :], kit.d[name]).then_inc(inputs_in, 16)

        @block.vector
        def _(dve):
            dve.wait_ge(inputs_in, 64)
            count = [0]

            def then(ins):
                count[0] += 1
                ins.then_inc(steps, 1)
                dve.wait_ge(steps, count[0])

            then(nc.vector.tensor_copy(byte[:, :], history[:, :]))
            then(nc.vector.tensor_scalar(low[:, :], byte[:, :], 1.0, None, ALU.is_ge))
            then(nc.vector.scalar_tensor_tensor(out=ok[:, :], in0=byte[:, :], scalar=4.0, in1=low[:, :],
                                                op0=ALU.is_le, op1=ALU.mult))
            then(nc.vector.tensor_scalar(bad[:, :], ok[:, :], -1.0, 1.0, ALU.mult, ALU.add))
            then(nc.vector.scalar_tensor_tensor(out=safe[:, :], in0=byte[:, :], scalar=-1.0, in1=ok[:, :],
                                                op0=ALU.add, op1=ALU.mult))
            then(nc.vector.tensor_tensor(term[:, :], safe[:, :], powers[:, :], ALU.mult))
            then(nc.vector.tensor_tensor_scan(total[:, :], fresh[:, :], term[:, :], 0.0, ALU.mult, ALU.add))
            then(nc.vector.tensor_tensor_scan(anybad[:, :], fresh[:, :], bad[:, :], 0.0, ALU.mult, ALU.max))
            flat = lambda t: t[:, :, :].rearrange("p n h -> p (n h)")
            then(nc.vector.tensor_copy(flat(whole), total[:, :]))
            then(nc.vector.tensor_scalar(flat(masked), flat(whole), TBL - 1, None, ALU.bitwise_and))
            then(nc.vector.tensor_copy(flat(hashed), flat(masked)))
            then(nc.vector.tensor_scalar(flat(good), anybad[:, :], -1.0, 1.0, ALU.mult, ALU.add))
            then(nc.vector.tensor_tensor(flat(kept), flat(hashed), flat(good), ALU.mult))
            then(nc.vector.scalar_tensor_tensor(out=flat(row), in0=anybad[:, :], scalar=float(TBL), in1=flat(kept),
                                                op0=ALU.mult, op1=ALU.add))
            then(nc.vector.tensor_tensor(ids[:, :, :], row[:, :, HIST - SIZES:HIST],
                                         base[:, :].rearrange("p (n s) -> p n s", n=NC), ALU.add))
    kit.clear()


def embed(kit):
    nc = kit.nc
    with nc.sbuf_tensor("txt_ids", [TXT_P, TXT_COLS, SIZES], U32) as ids:
        hash_text(kit, ids)
        embed_all(kit, ids)


def embed_all(kit, ids):
    nc = kit.nc
    N, K, NC = STRIP, STRIPS, TXT_COLS
    HALF = K // 2
    with ExitStack() as ctx:
        sb = lambda name, shape, dt=F32: ctx.enter_context(nc.sbuf_tensor(name, shape, dt))
        ps = lambda name, *shape: ctx.enter_context(nc.psum_tensor(name, [P, *shape], F32))
        sem = lambda name: ctx.enter_context(kit.semaphore(name))
        sems = lambda names: [sem(n) for n in names.split()]
        w = sb("pe_w", [32, P])
        patches = sb("patches", [32, 2, HALF * N])
        conv, sq, logv, rstd, normed = (sb("pe_" + n, [P, 2, N]) for n in "conv sq logv rstd normed".split())
        rows = sb("txt_rows", [TXT_P, NC, SIZES, C])
        total_rows = sb("txt_total_rows", [TXT_P, C])
        twice = sb("txt_twice", [TXT_P, 2, C])
        turned = sb("txt_turned", [P, B * NTXT])
        pconv, pcen, pvar, pt = ps("pconv", 512), ps("pcen", 4, 512), ps("pvar", 2, 512), ps("txt_pt", 512)
        w_in = sem("w_in")
        patches_in = sems("patches_in0 patches_in1")
        conv_mm, cen_mm, var_mm, conv_out, sq_out, logv_out, rstd_out, normed_out, stream_out = sems(
            "conv_mm cen_mm var_mm conv_out sq_out logv_out rstd_out normed_out stream_out")
        sum_out, twice_out, turn_mm, turned_out, text_out = sems("sum_out twice_out turn_mm turned_out text_out")
        gathered = kit.gathered
        block = ctx.enter_context(nc.Block())

        @block.sync
        def _(sp):
            sp.dma_start(w[:, :], kit.d["pe_w"]).then_inc(w_in, 16)
            with sp.Fori(0, PAIRS) as p:
                for h in (0, 1):
                    sp.wait_ge(conv_mm, at(p, K, h * HALF + HALF - K))
                    sp.dma_start(patches[:, h, :], kit.d["patches"][:, bass.ds(p * NIMG + h * HALF * N, HALF * N)]
                                 ).then_inc(patches_in[h], 16)

        @block.gpsimd
        def _(gp):
            for n in range(NC):
                for s in range(SIZES):
                    gp.indirect_dma_start(out=rows[:, n, s, :], out_offset=None, in_=kit.d["tables"],
                                          in_offset=bass.IndirectOffsetOnAxis(ap=ids[:, n, s:s + 1], axis=0),
                                          ).then_inc(gathered[n], 16)

        @block.tensor
        def _(pe):
            open_all(pe, conv_mm, cen_mm, var_mm, turn_mm)
            pe.wait_ge(w_in, 16)
            with pe.Fori(0, PAIRS) as p:
                for s in range(K + 2):
                    if s < K:
                        if s % HALF == 0:
                            pe.wait_ge(patches_in[s // HALF], p * 16 + 16)
                        pe.wait_ge(conv_out, at(p, K, s))
                        nc.tensor.matmul(pconv[:, 0:N], w[:, :], patches[:, s // HALF, (s % HALF) * N:(s % HALF + 1) * N],
                                         start=True, stop=True).then_inc(conv_mm, 1)
                    c = s - 1
                    if 0 <= c < K:
                        pe.wait_ge(conv_out, at(p, K, c + 1))
                        pe.wait_ge(normed_out, at(p, K, c - 3))
                        nc.tensor.matmul(pcen[:, c % 4, 0:N], kit.center[:, :], conv[:, c % 2, :],
                                         start=True, stop=True).then_inc(cen_mm, 1)
                    c = s - 2
                    if 0 <= c < K:
                        pe.wait_ge(sq_out, at(p, K, c + 1))
                        pe.wait_ge(logv_out, at(p, K, c - 1))
                        nc.tensor.matmul(pvar[:, c % 2, 0:N], kit.average[:, :], sq[:, c % 2, :],
                                         start=True, stop=True).then_inc(var_mm, 1)
            for n in range(NC):
                pe.wait_ge(twice_out, at(n, 1, 1))
                pe.wait_ge(turned_out, at(n, 1, 0))
                nc.tensor.transpose(pt[:, 0:TXT_P], twice[:, :, :].rearrange("p a c -> p (a c)"),
                                    kit.ident[0:TXT_P, 0:TXT_P]).then_inc(turn_mm, 1)

        @block.scalar
        def _(act):
            open_all(act, sq_out, logv_out, rstd_out, stream_out, turned_out)
            act.preload_act_table_set(LN_EXP)
            with act.Fori(0, PAIRS) as p:
                for s in range(K + 3):
                    if s < K:
                        act.wait_ge(cen_mm, at(p, K, s + 1))
                        act.wait_ge(var_mm, at(p, K, s - 1))
                        nc.scalar.activation(sq[:, s % 2, :], pcen[:, s % 4, 0:N], ACT.Square).then_inc(sq_out, 1)
                    c = s - 2
                    if 0 <= c < K:
                        act.wait_ge(var_mm, at(p, K, c + 1))
                        act.wait_ge(rstd_out, at(p, K, c - 1))
                        nc.scalar.activation(logv[:, c % 2, :], pvar[:, c % 2, 0:N], ACT.Ln,
                                             bias=kit.col("eps")).then_inc(logv_out, 1)
                        act.wait_ge(logv_out, at(p, K, c + 1))
                        act.wait_ge(normed_out, at(p, K, c - 1))
                        nc.scalar.activation(rstd[:, c % 2, :], logv[:, c % 2, :], ACT.Exp,
                                             scale=-0.5).then_inc(rstd_out, 1)
                    c = s - 3
                    if 0 <= c < K:
                        act.wait_ge(normed_out, at(p, K, c + 1))
                        nc.scalar.activation(kit.stream[:, bass.ds(p, 1), c * N:(c + 1) * N], normed[:, c % 2, :].unsqueeze(1),
                                             ACT.Identity, bias=kit.col("pe_nb"),
                                             scale=kit.col("pe_ng")).then_inc(stream_out, 1)
            for n in range(NC):
                act.wait_ge(turn_mm, at(n, 1, 1))
                nc.scalar.activation(turned[:, n * TXT_P:(n + 1) * TXT_P], pt[:, 0:TXT_P],
                                     ACT.Copy).then_inc(turned_out, 1)
            act.wait_ge(turned_out, at(NC, 1, 0))
            for b in (0, 1):
                half = slice(C * b, C * b + C)
                nc.scalar.activation(kit.stream[half, :, NIMG:T],
                                     turned[half, :].rearrange("p (n b t) -> p b n t", b=2, t=NTXT)[:, b],
                                     ACT.Copy).then_inc(text_out, 1)

        @block.vector
        def _(dve):
            open_all(dve, conv_out, normed_out, sum_out, twice_out)
            with dve.Fori(0, PAIRS) as p:
                for s in range(K + 3):
                    if s < K:
                        dve.wait_ge(conv_mm, at(p, K, s + 1))
                        dve.wait_ge(cen_mm, at(p, K, s - 1))
                        nc.vector.tensor_scalar(conv[:, s % 2, :], pconv[:, 0:N], kit.col("pe_b"), None,
                                                ALU.add).then_inc(conv_out, 1)
                    c = s - 3
                    if 0 <= c:
                        dve.wait_ge(rstd_out, at(p, K, c + 1))
                        dve.wait_ge(stream_out, at(p, K, c - 1))
                        nc.vector.tensor_tensor(normed[:, c % 2, :], pcen[:, c % 4, 0:N], rstd[:, c % 2, :],
                                                ALU.mult).then_inc(normed_out, 1)
            for n in range(NC):
                dve.wait_ge(gathered[n], 16 * SIZES)
                dve.wait_ge(twice_out, at(n, 1, 0))
                nc.vector.tensor_reduce(total_rows[:, :], rows[:, n, :, :].rearrange("p s c -> p c s"),
                                        AX_X, ALU.add).then_inc(sum_out, 1)
                dve.wait_ge(sum_out, at(n, 1, 1))
                dve.wait_ge(turn_mm, at(n, 1, 0))
                nc.vector.tensor_scalar(twice[:, :, :], total_rows[:, :].unsqueeze(1).broadcast_to([TXT_P, 2, C]),
                                        1.0 / (SIZES + 1), None, ALU.mult).then_inc(twice_out, 1)


def image_rows(kit, pair, row, rows):
    flat = kit.stream[:, :, :].rearrange("p n t -> p (n t)")
    return flat[:, bass.ds(pair * T + row * SIDE, rows * SIDE)].rearrange("p (r c) -> p r c", c=SIDE)


def strip_pieces(kit, strip, pair, row, last, shift):
    if not shift:
        return [(strip[:, :, :], image_rows(kit, pair, row * WS, WS))]
    parts = [(0, WS, row * WS + shift)]
    if last:
        parts = [(0, WS - shift, SIDE - (WS - shift)), (WS - shift, shift, 0)]
    out = []
    for r0, rows, at_row in parts:
        img = image_rows(kit, pair, at_row, rows)
        out.append((strip[:, r0:r0 + rows, 0:SIDE - shift], img[:, :, shift:SIDE]))
        out.append((strip[:, r0:r0 + rows, SIDE - shift:SIDE], img[:, :, 0:shift]))
    return out


def window_attention(kit, layer):
    nc = kit.nc
    shift = SHIFT if layer else 0
    N, W = STRIP, NWIN
    scale = HD ** -0.5
    ACT_HEADS = 3
    EXP_LAG, TURN_LAG, AV_LAG, OUT_LAG, FOLD_LAG = 1, 2, 3, 4, 6
    with ExitStack() as ctx:
        sb = lambda name, shape, dt=F32: ctx.enter_context(nc.sbuf_tensor(f"{name}{layer}", shape, dt))
        ps = lambda name, *shape: ctx.enter_context(nc.psum_tensor(f"{name}{layer}", [P, *shape], F32))
        sem = lambda name: ctx.enter_context(kit.semaphore(f"{name}{layer}"))
        sems = lambda names: [sem(n) for n in names.split()]
        weights = sb("attn_w", [P, 4, P])
        tables = sb("score_bias", [P, 4, NH * WIN])
        headmask, fold = sb("headmask", [P, NH]), sb("fold", [P, WIN])
        vmask = sb("vmask", [2 * WIN, 4 * P])
        vones = sb("vones", [2 * WIN, 4 * GROUPS])
        bq_scaled = sb("bq_scaled", [P, 1])
        src, res = sb("src", [P, WS, SIDE]), sb("res", [P, WS, SIDE])
        sq, logv, rstd, normed = (sb(n, [P, N]) for n in ("sq", "logv", "rstd", "normed"))
        hn = sb("hn", [P, W, 2, WIN])
        keys = sb("keys", [P, N])
        qbd = sb("qbd", [P, 2, W, P])
        kx = sb("kx", [P, 2, W, NH, WIN])
        va = sb("va", [2 * WIN, 2, W, 2 * GROUPS, VA])
        scores = sb("scores", [P, 4, NH, WIN])
        relbias = scores[:, 0, :, :].rearrange("p h k -> p (h k)")
        rmax = sb("rmax", [P, 4, NH])
        pt = sb("pt", [2 * WIN, 2, GROUPS, P])
        rsum = sb("rsum", [P, 2, GROUPS, 2])
        obd = sb("obd", [P, W, P])
        ofm = sb("ofm", [P, N])
        pa, pb, pv, pt_ps, po, pf = (ps(n, 512) for n in ("pa", "pb", "pv", "pt_ps", "po", "pf"))
        pscore = ps("pscore", 2, 512)
        weights_in, cleared, tables_out, passed = sems("weights_in cleared tables_out passed")
        src_in, twice_out, shifted_pool, stream_out = sems("src_in twice_out shifted_pool stream_out")
        cen_mm, var_mm, q_mm, k_mm, v_mm, score_mm, turn_mm, av_mm, fold_mm, proj_mm = sems(
            "cen_mm var_mm q_mm k_mm v_mm score_mm turn_mm av_mm fold_mm proj_mm")
        sq_out, logv_out, rstd_out, hn_out, q_out, keys_out, kx_act, probs_out, pt_out, ofm_out, res_out = sems(
            "sq_out logv_out rstd_out hn_out q_out keys_out kx_act probs_out pt_out ofm_out res_out")
        normed_out, kx_dve, va_out, biased_out, max_out, shifted_dve, rsum_out, o_out = sems(
            "normed_out kx_dve va_out biased_out max_out shifted_dve rsum_out o_out")
        block = ctx.enter_context(nc.Block())
        D = W // 2

        def shifted(w):
            return (shifted_dve, W // 4, w // 4 + 1) if w % 4 == 0 else (shifted_pool, W - W // 4, w - w // 4)

        def lagged(n, buf, w, lag):
            return (n, buf, w - lag) if w >= lag else (n - 1, 1 - buf, w - lag + W)

        def place(pair, row, buffer):
            return strip_pieces(kit, buffer, pair, row, isinstance(row, int) and row == W - 1, shift)

        def strips(eng, slot):
            def two(pair, d, first, last):
                n = pair * W + 2 * d
                before = (pair - 1, W - 1) if isinstance(d, int) and d == 0 else (pair, 2 * d - 1)
                after = (pair + 1, 0) if isinstance(d, int) and d == D - 1 else (pair, 2 * d + 2)
                for w in range(W):
                    slot(n, 0, w, ((pair, 2 * d + 1), before), first, False)
                for w in range(W):
                    slot(n + 1, 1, w, (after, (pair, 2 * d)), False, last)

            def pair_of_batches(pair, first, last):
                two(pair, 0, first, False)
                with eng.Fori(1, D - 1) as d:
                    two(pair, d, False, False)
                two(pair, D - 1, False, last)

            pair_of_batches(0, True, False)
            with eng.Fori(1, PAIRS - 1) as pair:
                pair_of_batches(pair, False, False)
            pair_of_batches(PAIRS - 1, False, True)
            for w in range(W):
                slot(PAIRS * W, 0, w, (None, (PAIRS - 1, W - 1)), False, None)

        def before_first(first, w, lag):
            return first and w < lag

        @block.sync
        def _(sp):
            for dst, name in ((weights[:, :, :].rearrange("p a b -> p (a b)"), f"attn_w{layer}"),
                              (tables[:, :, :].rearrange("p a b -> p (a b)"), "amask"),
                              (relbias, f"relbias{layer}"), (headmask[:, :], "headmask"),
                              (fold[:, :], "fold"), (vmask[:, :], "vmask"), (vones[:, :], "vones")):
                sp.dma_start(dst, kit.d[name]).then_inc(weights_in, 16)

        @block.gpsimd
        def _(gp):
            open_all(gp, src_in, twice_out, shifted_pool, stream_out)
            nc.gpsimd.memset(qbd[:, :, :, :], 0.0).then_inc(cleared, 1)
            nc.gpsimd.memset(obd[:, :, :], 0.0).then_inc(cleared, 1)
            gp.wait_ge(weights_in, 7 * 16)

            def settled():
                gp.sem_inc(passed, 1)

            def ahead(n, w, where):
                if w == 0:
                    gp.wait_ge(cen_mm, at(n, 1, 0))
                    settled()
                    for part, img in place(*where, src):
                        done = nc.gpsimd.tensor_copy(part, img)
                    done.then_inc(src_in, 1)
                if w == 4:
                    gp.wait_ge(hn_out, at(n, 1, 1))
                    gp.wait_ge(v_mm, at(n, W, 0))
                    settled()
                    nc.gpsimd.tensor_copy(hn[:, :, 1, :], hn[:, :, 0, :]).then_inc(twice_out, 1)

            def slot(n, buf, w, where, first, last):
                after, before = where
                if last is False and w == 0:
                    ahead(n + 1, w, after)
                if last is not None and shifted(w)[0] is shifted_pool:
                    gp.wait_ge(max_out, at(n, W, w + 1))
                    settled()
                    nc.gpsimd.tensor_tensor(scores[:, w % 4, :, :], scores[:, w % 4, :, :],
                                            rmax[:, w % 4, :].unsqueeze(2).broadcast_to([P, NH, WIN]),
                                            ALU.subtract).then_inc(shifted_pool, 1)
                if last is False and w > 0:
                    ahead(n + 1, w, after)
                if w == W - 1 and not first:
                    gp.wait_ge(res_out, at(n - 1, 1, 1))
                    settled()
                    for new, img in place(*before, res):
                        done = nc.gpsimd.tensor_tensor(img, new, img, ALU.add)
                    done.then_inc(stream_out, 1)

            for w in range(W):
                ahead(0, w, (0, 0))
            strips(gp, slot)

        @block.tensor
        def _(pe):
            open_all(pe, cen_mm, var_mm, q_mm, k_mm, v_mm, score_mm, turn_mm, av_mm, fold_mm, proj_mm)
            pe.wait_ge(weights_in, 7 * 16)
            pe.wait_ge(cleared, 2)

            def values(n, g):
                pe.wait_ge(va_out, at(n, 2, g))
                for w in range(4 * g, 4 * g + 4):
                    nc.tensor.matmul(pv[0:2 * WIN, w % 4 * P:w % 4 * P + P],
                                     hn[:, w, :, :].rearrange("p a k -> p (a k)"), weights[:, 2, :],
                                     start=True, stop=True).then_inc(v_mm, 1)

            def ahead(n, w):
                if w == 1:
                    pe.wait_ge(src_in, at(n, 1, 1))
                    pe.wait_ge(q_out, at(n, 2, 0))
                    nc.tensor.matmul(pa[:, 0:N], kit.center[:, :], src[:, :, :].rearrange("p r c -> p (r c)"),
                                     start=True, stop=True).then_inc(cen_mm, 1)
                if w == 2:
                    pe.wait_ge(sq_out, at(n, 1, 1))
                    pe.wait_ge(keys_out, at(n, 1, 0))
                    nc.tensor.matmul(pb[:, 0:N], kit.average[:, :], sq[:, :], start=True, stop=True).then_inc(var_mm, 1)
                if w == 5:
                    pe.wait_ge(hn_out, at(n, 1, 1))
                    nc.tensor.matmul(pb[:, 0:N], weights[:, 1, :], hn[:, :, 0, :], start=True, stop=True).then_inc(k_mm, 1)
                    nc.tensor.matmul(pa[:, 0:N], weights[:, 0, :], hn[:, :, 0, :], start=True, stop=True).then_inc(q_mm, 1)
                if w == 6:
                    pe.wait_ge(twice_out, at(n, 1, 1))
                    values(n, 0)

            def slot(n, buf, w, where, first, last):
                if last is not None:
                    if w == 0:
                        pe.wait_ge(q_out, at(n, 2, 2))
                        pe.wait_ge(kx_act, at(n, ACT_HEADS, ACT_HEADS))
                        pe.wait_ge(kx_dve, at(n, NH - ACT_HEADS, NH - ACT_HEADS))
                    pe.wait_ge(biased_out, at(n, W, w - 1))
                    nc.tensor.matmul(pscore[:, w % 2, 0:NH * WIN], qbd[:, buf, w, :],
                                     kx[:, buf, w, :, :].rearrange("p h k -> p (h k)"),
                                     start=True, stop=True).then_inc(score_mm, 1)
                    if w == 2:
                        values(n, 1)
                if last is False:
                    ahead(n + 1, w)
                m, mbuf, v = lagged(n, buf, w, TURN_LAG)
                if not before_first(first, w, TURN_LAG) and (last is not None or m != n):
                    pe.wait_ge(probs_out, at(m, W, v + 1))
                    pe.wait_ge(pt_out, at(m, W, v))
                    for g in range(GROUPS):
                        done = nc.tensor.transpose(pt_ps[0:2 * WIN, g * P:(g + 1) * P],
                                                   scores[:, v % 4, 2 * g:2 * g + 2, :].rearrange("p h k -> p (h k)"),
                                                   kit.ident[:, :])
                    done.then_inc(turn_mm, 1)
                m, mbuf, v = lagged(n, buf, w, AV_LAG)
                if not before_first(first, w, AV_LAG) and (last is not None or m != n):
                    pe.wait_ge(pt_out, at(m, W, v + 1))
                    pe.wait_ge(va_out, at(m, 2, v // 4 + 1))
                    if v % 2 == 0:
                        pe.wait_ge(o_out, at(m, W, v))
                    for g in range(GROUPS):
                        o = (v % 2 * GROUPS + g) * 2 * VA
                        done = nc.tensor.matmul(po[:, o:o + 2 * VA], pt[:, v % 2, g, :],
                                                va[:, mbuf, v, 2 * g:2 * g + 2, :].rearrange("p b v -> p (b v)"),
                                                start=True, stop=True)
                    done.then_inc(av_mm, 1)
                m, mbuf, v = lagged(n, buf, w, FOLD_LAG)
                if not before_first(first, w, FOLD_LAG) and (last is not None or m != n) and v % 2 == 1:
                    pe.wait_ge(o_out, at(m, W, v + 1))
                    if v == 1:
                        pe.wait_ge(res_out, at(m, 1, 0))
                    for u in (v - 1, v):
                        nc.tensor.matmul(pf[:, u * WIN:(u + 1) * WIN], obd[:, u, :], fold[:, :],
                                         start=True, stop=True).then_inc(fold_mm, 1)
                if w == 6 and not first:
                    pe.wait_ge(ofm_out, at(n - 1, 1, 1))
                    nc.tensor.matmul(pf[:, 0:N], weights[:, 3, :], ofm[:, :], start=True, stop=True).then_inc(proj_mm, 1)

            for w in range(W):
                ahead(0, w)
            strips(pe, slot)

        @block.scalar
        def _(act):
            open_all(act, sq_out, logv_out, rstd_out, hn_out, q_out, keys_out, kx_act, probs_out, pt_out, ofm_out, res_out)
            act.preload_act_table_set(LN_EXP)
            act.wait_ge(tables_out, 1)
            act.wait_ge(weights_in, 7 * 16)

            def ahead(n, buf, w):
                if w == 1:
                    act.wait_ge(cen_mm, at(n, 1, 1))
                    act.wait_ge(var_mm, at(n, 1, 0))
                    nc.scalar.activation(sq[:, :], pa[:, 0:N], ACT.Square).then_inc(sq_out, 1)
                if w == 2:
                    act.wait_ge(var_mm, at(n, 1, 1))
                    nc.scalar.activation(logv[:, :], pb[:, 0:N], ACT.Ln, bias=kit.col("eps")).then_inc(logv_out, 1)
                    act.wait_ge(logv_out, at(n, 1, 1))
                    act.wait_ge(normed_out, at(n, 1, 0))
                    nc.scalar.activation(rstd[:, :], logv[:, :], ACT.Exp, scale=-0.5).then_inc(rstd_out, 1)
                if w == 3:
                    act.wait_ge(normed_out, at(n, 1, 1))
                    act.wait_ge(v_mm, at(n, W, 0))
                    nc.scalar.activation(hn[:, :, 0, :].rearrange("p w (r c) -> p r w c", c=WS),
                                         normed[:, :].rearrange("p (r w c) -> p r w c", r=WS, w=W), ACT.Identity,
                                         bias=kit.col(f"n1b{layer}"), scale=kit.col(f"n1g{layer}")).then_inc(hn_out, 1)
                if w == 5:
                    act.wait_ge(k_mm, at(n, 1, 1))
                    act.wait_ge(kx_dve, at(n, NH - ACT_HEADS, 0))
                    act.wait_ge(kx_act, at(n, ACT_HEADS, 0))
                    nc.scalar.activation(keys[:, :], pb[:, 0:N], ACT.Identity,
                                         bias=kit.col(f"bk{layer}")).then_inc(keys_out, 1)
                    act.wait_ge(q_mm, at(n, 1, 1))
                    act.wait_ge(score_mm, at(n, W, -W))
                    for b in (0, 1):
                        half = slice(C * b, C * b + C)
                        nc.scalar.activation(qbd[half, buf, :, QPAD * b:QPAD * b + WIN],
                                             pa[half, 0:N].rearrange("p (w k) -> p w k", w=W), ACT.Identity,
                                             bias=bq_scaled[half, :], scale=scale).then_inc(q_out, 1)
                if w >= W - ACT_HEADS:
                    head = w - (W - ACT_HEADS)
                    act.wait_ge(keys_out, at(n, 1, 1))
                    nc.scalar.activation(kx[:, buf, :, head, :], keys[:, :].rearrange("p (w k) -> p w k", w=W),
                                         ACT.Copy, scale=headmask[:, head:head + 1]).then_inc(kx_act, 1)

            def slot(n, buf, w, where, first, last):
                m, _, v = lagged(n, buf, w, EXP_LAG)
                if not before_first(first, w, EXP_LAG) and (last is not None or m != n):
                    sem, per, k = shifted(v)
                    act.wait_ge(sem, at(m, per, k))
                    e = scores[:, v % 4, :, :].rearrange("p h k -> p (h k)")
                    nc.scalar.activation(e, e, ACT.Exp).then_inc(probs_out, 1)
                m, _, v = lagged(n, buf, w, TURN_LAG)
                if not before_first(first, w, TURN_LAG) and (last is not None or m != n):
                    act.wait_ge(turn_mm, at(m, W, v + 1))
                    act.wait_ge(av_mm, at(m, W, v - 1))
                    nc.scalar.activation(pt[:, v % 2, :, :].rearrange("p g q -> p (g q)"),
                                         pt_ps[0:2 * WIN, :], ACT.Copy).then_inc(pt_out, 1)
                if last is False:
                    ahead(n + 1, 1 - buf, w)
                if not first and w == 5:
                    act.wait_ge(fold_mm, at(n - 1, W, W))
                    act.wait_ge(proj_mm, at(n - 1, 1, 0))
                    nc.scalar.activation(ofm[:, :], pf[:, 0:N], ACT.Identity,
                                         bias=kit.col(f"bv{layer}")).then_inc(ofm_out, 1)
                if not first and w == 6:
                    act.wait_ge(proj_mm, at(n - 1, 1, 1))
                    act.wait_ge(stream_out, at(n - 1, 1, 0))
                    nc.scalar.activation(res[:, :, :].rearrange("p r (w c) -> p r w c", w=W),
                                         pf[:, 0:N].rearrange("p (w r c) -> p r w c", w=W, r=WS), ACT.Identity,
                                         bias=kit.col(f"bp{layer}")).then_inc(res_out, 1)

            for w in range(W):
                ahead(0, 0, w)
            strips(act, slot)

        @block.vector
        def _(dve):
            open_all(dve, normed_out, kx_dve, va_out, biased_out, max_out, shifted_dve, rsum_out, o_out)
            dve.wait_ge(weights_in, 7 * 16)
            nc.vector.tensor_scalar(bq_scaled[:, :], kit.col(f"bq{layer}"), scale, None, ALU.mult).then_inc(tables_out, 1)
            nc.vector.tensor_tensor(tables[:, :, :], tables[:, :, :],
                                    relbias.unsqueeze(1).broadcast_to([P, 4, NH * WIN]),
                                    ALU.add).then_inc(tables_out, 1)
            for b in (0, 1):
                for w in range(W):
                    nc.vector.tensor_copy(va[:, b, w, :, 2 * HD:VA],
                                          vones[:, :].rearrange("p (g o) -> p g o", o=2)).then_inc(tables_out, 1)
            dve.wait_ge(tables_out, 2 + 2 * W)

            def values(n, buf, g):
                dve.wait_ge(v_mm, at(n, W, 4 * g + 4))
                dve.wait_ge(av_mm, at(n, W, -W))
                nc.vector.tensor_tensor(
                    va[:, buf, 4 * g:4 * g + 4, :, 0:2 * HD].rearrange("p w g v -> p (w g) v"),
                    pv[0:2 * WIN, :].rearrange("p (g v) -> p g v", v=2 * HD),
                    vmask[:, :].rearrange("p (g v) -> p g v", v=2 * HD), ALU.mult).then_inc(va_out, 1)

            def ahead(n, buf, w):
                if w == 3:
                    dve.wait_ge(rstd_out, at(n, 1, 1))
                    dve.wait_ge(hn_out, at(n, 1, 0))
                    nc.vector.tensor_tensor(normed[:, :], pa[:, 0:N], rstd[:, :], ALU.mult).then_inc(normed_out, 1)
                for head in {6: (3, 4), 7: (5, 6, 7)}.get(w, ()):
                    dve.wait_ge(keys_out, at(n, 1, 1))
                    dve.wait_ge(score_mm, at(n, W, -W))
                    nc.vector.tensor_scalar(kx[:, buf, :, head, :], keys[:, :].rearrange("p (w k) -> p w k", w=W),
                                            headmask[:, head:head + 1], None, ALU.mult).then_inc(kx_dve, 1)

            def outputs(n, g):
                dve.wait_ge(av_mm, at(n, W, 2 * g + 2))
                dve.wait_ge(fold_mm, at(n, W, 2 * g + 2 - W))
                o = po[:, 0:4 * GROUPS * VA].rearrange("p (w g b v) -> p w g b v", w=2, g=GROUPS, b=2)
                dve.wait_ge(o_out, at(n, W, 2 * g))
                nc.vector.reciprocal(rsum[:, :, :, :], o[:, :, :, 0, 2 * HD:VA]).then_inc(rsum_out, 1)
                dve.wait_ge(rsum_out, at(n, W // 2, g + 1))
                for k in (0, 1):
                    for b in (0, 1):
                        half = slice(QPAD * b, QPAD * b + QPAD)
                        done = nc.vector.tensor_tensor(
                            obd[half, 2 * g + k, C * b:C * b + C].rearrange("p (g o d) -> p g o d", o=2, d=HD),
                            o[half, k, :, b, 0:2 * HD].rearrange("p g (o d) -> p g o d", o=2),
                            rsum[half, k, :, :].unsqueeze(3).broadcast_to([QPAD, GROUPS, 2, HD]), ALU.mult)
                    done.then_inc(o_out, 1)

            def slot(n, buf, w, where, first, last):
                m, _, v = lagged(n, buf, w, OUT_LAG)
                if not before_first(first, w, OUT_LAG) and (last is not None or m != n) and v % 2 == 1:
                    outputs(m, v // 2)
                if last is not None:
                    after, _ = where
                    bottom = last or isinstance(after[1], int) and after[1] == 0
                    kind = (2 * bottom + (w == W - 1)) if shift else 0
                    dve.wait_ge(score_mm, at(n, W, w + 1))
                    dve.wait_ge(turn_mm, at(n, W, w - 3))
                    flat = scores[:, w % 4, :, :].rearrange("p h k -> p (h k)")
                    nc.vector.tensor_tensor(flat, pscore[:, w % 2, 0:NH * WIN], tables[:, kind, :],
                                            ALU.add).then_inc(biased_out, 1)
                    dve.wait_ge(biased_out, at(n, W, w + 1))
                    nc.vector.tensor_reduce(rmax[:, w % 4, :], scores[:, w % 4, :, :], AX_X,
                                            ALU.max).then_inc(max_out, 1)
                    if shifted(w)[0] is shifted_dve:
                        dve.wait_ge(max_out, at(n, W, w + 1))
                        nc.vector.tensor_tensor(scores[:, w % 4, :, :], scores[:, w % 4, :, :],
                                                rmax[:, w % 4, :].unsqueeze(2).broadcast_to([P, NH, WIN]),
                                                ALU.subtract).then_inc(shifted_dve, 1)
                if last is not None and w in (0, 3):
                    values(n, buf, w // 3)
                if last is False:
                    ahead(n + 1, 1 - buf, w)

            for w in range(W):
                ahead(0, 0, w)
            strips(dve, slot)


def mlp(kit, layer):
    nc = kit.nc
    N, K = STRIP, STRIPS
    with ExitStack() as ctx:
        sb = lambda name, shape, dt=F32: ctx.enter_context(nc.sbuf_tensor(f"{name}_m{layer}", shape, dt))
        ps = lambda name, *shape: ctx.enter_context(nc.psum_tensor(f"{name}_m{layer}", [P, *shape], F32))
        sem = lambda name: ctx.enter_context(kit.semaphore(f"{name}_m{layer}"))
        sems = lambda names: [sem(n) for n in names.split()]
        up = sb("up", [P, 4 * C])
        down = sb("down", [P, 2, 2, P])
        sq, logv, rstd, normed = (sb(n, [P, 2, N]) for n in ("sq", "logv", "rstd", "normed"))
        hn = sb("hn", [P, 2, N])
        parts = sb("parts", [P, K, 2, N], F32R)
        upparts = sb("upparts", [P, 2, 4 * C], F32R)
        gel = sb("gel", [P, 2, 4, N])
        pcen, pvar, pdown = ps("pcen", 4, 512), ps("pvar", 2, 512), ps("pdown", 512)
        pup = pcen
        uphi_out, uplo_out, hi_out, lo_out = sems("uphi_out uplo_out hi_out lo_out")
        weights_in, cen_mm, var_mm, up_mm, down_mm = sems("weights_in cen_mm var_mm up_mm down_mm")
        sq_out, logv_out, rstd_out, hn_out, gelu_out = sems("sq_out logv_out rstd_out hn_out gelu_out")
        normed_out, stream_out = sems("normed_out stream_out")
        block = ctx.enter_context(nc.Block())

        @block.sync
        def _(sp):
            sp.dma_start(up[:, :], kit.d[f"up{layer}"]).then_inc(weights_in, 16)
            sp.dma_start(down[:, :, :, :].rearrange("p h b m -> p (h b m)"), kit.d[f"down{layer}"]).then_inc(weights_in, 16)

        @block.tensor
        def _(pe):
            open_all(pe, cen_mm, var_mm, up_mm, down_mm)
            pe.wait_ge(weights_in, 32)
            pe.wait_ge(uplo_out, 1)
            with pe.Fori(0, PAIRS) as p:
                pe.wait_ge(stream_out, at(p, K, 0))
                for s in range(K + 1):
                    if s < K:
                        pe.wait_ge(normed_out, at(p, K, s - 3))
                        nc.tensor.matmul(pcen[:, s % 4, 0:N], kit.center[:, :],
                                         kit.stream[:, bass.ds(p, 1), s * N:(s + 1) * N].rearrange("p a n -> p (a n)"),
                                         start=True, stop=True).then_inc(cen_mm, 1)
                    c = s - 1
                    if 0 <= c:
                        pe.wait_ge(sq_out, at(p, K, c + 1))
                        pe.wait_ge(logv_out, at(p, K, c - 1))
                        nc.tensor.matmul(pvar[:, c % 2, 0:N], kit.average[:, :], sq[:, c % 2, :],
                                         start=True, stop=True).then_inc(var_mm, 1)
                pe.wait_ge(normed_out, at(p, K, K))
                for s in range(K + 1):
                    if s < K:
                        pe.wait_ge(hi_out, at(p, 2 * K, 2 * s + 2))
                        pe.wait_ge(lo_out, at(p, 2 * K, 2 * s + 2))
                        for b in (0, 1):
                            for half in (0, 1):
                                pe.wait_ge(gelu_out, at(p, 4 * K, 4 * (s - 1) + 2 * b + half + 1))
                                cols = slice(P * half, P * half + P)
                                nc.tensor.matmul(pup[:, 2 * b + half, 0:N], upparts[:, 0, cols], parts[:, s, b, :],
                                                 start=True, stop=False)
                                nc.tensor.matmul(pup[:, 2 * b + half, 0:N], upparts[:, 1, cols], parts[:, s, b, :],
                                                 start=False, stop=True).then_inc(up_mm, 1)
                    c = s - 1
                    if 0 <= c:
                        pe.wait_ge(stream_out, at(p, K, c))
                        for i in range(4):
                            pe.wait_ge(gelu_out, at(p, 4 * K, 4 * c + i + 1))
                            done = nc.tensor.matmul(pdown[:, 0:N], down[:, i % 2, i // 2, :], gel[:, c % 2, i, :],
                                                    start=(i == 0), stop=(i == 3))
                        done.then_inc(down_mm, 1)

        @block.scalar
        def _(act):
            open_all(act, sq_out, logv_out, rstd_out, hn_out, gelu_out)
            with act.Fori(0, PAIRS) as p:
                act.preload_act_table_set(LN_EXP)
                for s in range(K + 3):
                    if s < K:
                        act.wait_ge(cen_mm, at(p, K, s + 1))
                        act.wait_ge(var_mm, at(p, K, s - 1))
                        nc.scalar.activation(sq[:, s % 2, :], pcen[:, s % 4, 0:N], ACT.Square).then_inc(sq_out, 1)
                    c = s - 2
                    if 0 <= c < K:
                        act.wait_ge(var_mm, at(p, K, c + 1))
                        act.wait_ge(rstd_out, at(p, K, c - 1))
                        nc.scalar.activation(logv[:, c % 2, :], pvar[:, c % 2, 0:N], ACT.Ln,
                                             bias=kit.col("eps")).then_inc(logv_out, 1)
                        act.wait_ge(logv_out, at(p, K, c + 1))
                        act.wait_ge(normed_out, at(p, K, c - 1))
                        nc.scalar.activation(rstd[:, c % 2, :], logv[:, c % 2, :], ACT.Exp,
                                             scale=-0.5).then_inc(rstd_out, 1)
                    c = s - 3
                    if 0 <= c < K:
                        act.wait_ge(normed_out, at(p, K, c + 1))
                        act.wait_ge(lo_out, at(p, 2 * K, 2 * c - 2))
                        nc.scalar.activation(hn[:, c % 2, :], normed[:, c % 2, :], ACT.Identity,
                                             bias=kit.col(f"n2b{layer}"), scale=kit.col(f"n2g{layer}")).then_inc(hn_out, 1)
                for c in range(K):
                    act.wait_ge(down_mm, at(p, K, c - 1))
                    for i in range(4):
                        act.wait_ge(up_mm, at(p, 4 * K, 4 * c + i + 1))
                        nc.scalar.activation(gel[:, c % 2, i, :], pup[:, i, 0:N], ACT.Gelu,
                                             bias=kit.col(f"b1{('lo', 'hi')[i % 2]}{layer}")).then_inc(gelu_out, 1)

        @block.vector
        def _(dve):
            open_all(dve, normed_out, stream_out, hi_out, lo_out)
            dve.wait_ge(weights_in, 32)
            nc.vector.tensor_copy(upparts[:, 0, :], up[:, :]).then_inc(uphi_out, 1)
            dve.wait_ge(uphi_out, 1)
            nc.vector.tensor_tensor(upparts[:, 1, :], up[:, :], upparts[:, 0, :].bitcast(F32),
                                    ALU.subtract).then_inc(uplo_out, 1)
            with dve.Fori(0, PAIRS) as p:
                for s in range(K + 1):
                    c = s
                    if c < K:
                        dve.wait_ge(rstd_out, at(p, K, c + 1))
                        dve.wait_ge(hn_out, at(p, K, c - 1))
                        nc.vector.tensor_tensor(normed[:, c % 2, :], pcen[:, c % 4, 0:N], rstd[:, c % 2, :],
                                                ALU.mult).then_inc(normed_out, 1)
                    c = s - 1
                    if 0 <= c:
                        dve.wait_ge(hn_out, at(p, K, c + 1))
                        if c == 0:
                            dve.wait_ge(up_mm, at(p, 4 * K, 0))
                        for b in (0, 1):
                            half = slice(C * b, C * b + C)
                            nc.vector.tensor_copy(parts[half, c, b, :], hn[half, c % 2, :]).then_inc(hi_out, 1)
                        dve.wait_ge(hi_out, at(p, 2 * K, 2 * c + 2))
                        for b in (0, 1):
                            half, other = slice(C * b, C * b + C), slice(C - C * b, P - C * b)
                            nc.vector.tensor_tensor(parts[other, c, b, :], hn[half, c % 2, :],
                                                    parts[half, c, b, :].bitcast(F32), ALU.subtract).then_inc(lo_out, 1)
                for c in range(K):
                    x = kit.stream[:, bass.ds(p, 1), c * N:(c + 1) * N].rearrange("p a n -> p (a n)")
                    dve.wait_ge(down_mm, at(p, K, c + 1))
                    nc.vector.scalar_tensor_tensor(out=x, in0=pdown[:, 0:N], scalar=kit.col(f"b2{layer}"), in1=x,
                                                   op0=ALU.add, op1=ALU.add).then_inc(stream_out, 1)


def time_mix(kit):
    nc = kit.nc
    N, K = TCH, TCHS
    with ExitStack() as ctx:
        sb = lambda name, shape, dt=F32: ctx.enter_context(nc.sbuf_tensor(f"mix_{name}", shape, dt))
        sem = lambda name: ctx.enter_context(kit.semaphore(f"mix_{name}"))
        sems = lambda names: [sem(n) for n in names.split()]
        weights = sb("w", [P, 4, P])
        rates = sb("rates", [P, 2])
        decay, first = rates[:, 0:1], rates[:, 1:2]
        sq, logv, rstd, h, sq2, logv2, rstd2, yn, ya, gated, sr, bv, na, nb, da, best, numer, denom, recip = (
            sb(n, [P, N]) for n in ("sq logv rstd h sq2 logv2 rstd2 yn ya gated sr bv na nb da best "
                                    "numer denom recip").split())
        key, val, gate, y = sb("key", [P, 2, N]), sb("val", [P, 3, N]), sb("gate", [P, 4, N]), sb("y", [P, 2, N])
        top, num, den = (sb(n, [P, 2, N + 1]) for n in ("top", "num", "den"))
        ex = sb("ex", [P, 2, 4, N])
        pcen, pvar, pk, pv, pr, pcen2, pvar2, pout = (
            ctx.enter_context(nc.psum_tensor(f"mix_{n}", [P, 512], F32)) for n in
            "pcen pvar pk pv pr pcen2 pvar2 pout".split())
        weights_in, rates_out, passed = sems("weights_in rates_out passed")
        cen_mm, var_mm, k_mm, v_mm, r_mm, cen2_mm, var2_mm, out_mm = sems(
            "cen_mm var_mm k_mm v_mm r_mm cen2_mm var2_mm out_mm")
        sq_out, logv_out, rstd_out, key_out, val_out, er_out, gate_out, a2_out, b2_out, a1_out, b1_out = sems(
            "sq_out logv_out rstd_out key_out val_out er_out gate_out a2_out b2_out a1_out b1_out")
        sq2_out, logv2_out, rstd2_out, ya_out = sems("sq2_out logv2_out rstd2_out ya_out")
        h_out, topc_out, top_out, e2_out, best_out, numc_out, num_out, denc_out, den_out = sems(
            "h_out topc_out top_out e2_out best_out numc_out num_out denc_out den_out")
        numer_out, denom_out, recip_out, y_out, yn_out, sr_out, stream_out = sems(
            "numer_out denom_out recip_out y_out yn_out sr_out stream_out")
        d2_out, d1_out, e1_out, bv_out, na_out, nb_out, da_out, gated_out = sems(
            "d2_out d1_out e1_out bv_out na_out nb_out da_out gated_out")
        block = ctx.enter_context(nc.Block())

        def steps(eng, *stages):
            with eng.Fori(0, PAIRS) as p:
                def ready(sem, c):
                    eng.wait_ge(sem, at(p, K, c + 1))

                def free(sem, c, buffers):
                    eng.wait_ge(sem, at(p, K, max(c - buffers + 1, 0)))

                for s in range(K + 4):
                    for lag, stage in enumerate(stages):
                        if stage and 0 <= s - lag < K:
                            stage(p, s - lag, ready, free)

        def tokens(p, c):
            return kit.stream[:, bass.ds(p, 1), c * N:(c + 1) * N].rearrange("p a n -> p (a n)")

        @block.sync
        def _(sp):
            sp.dma_start(weights[:, :, :].rearrange("p a b -> p (a b)"), kit.d["mix_w"]).then_inc(weights_in, 16)

        @block.tensor
        def _(pe):
            open_all(pe, cen_mm, var_mm, k_mm, v_mm, r_mm, cen2_mm, var2_mm, out_mm)
            pe.wait_ge(weights_in, 16)

            def project(p, c, ready, free):
                free(h_out, c, 1)
                nc.tensor.matmul(pcen[:, 0:N], kit.center[:, :], tokens(p, c), start=True, stop=True).then_inc(cen_mm, 1)
                ready(sq_out, c)
                free(logv_out, c, 1)
                nc.tensor.matmul(pvar[:, 0:N], kit.average[:, :], sq[:, :], start=True, stop=True).then_inc(var_mm, 1)
                ready(h_out, c)
                for i, (bank, used, done) in enumerate(((pk, key_out, k_mm), (pv, val_out, v_mm), (pr, er_out, r_mm))):
                    free(used, c, 1)
                    nc.tensor.matmul(bank[:, 0:N], weights[:, i, :], h[:, :], start=True, stop=True).then_inc(done, 1)

            def norm(p, c, ready, free):
                ready(y_out, c)
                free(yn_out, c, 1)
                nc.tensor.matmul(pcen2[:, 0:N], kit.center[:, :], y[:, c % 2, :], start=True, stop=True).then_inc(cen2_mm, 1)
                ready(sq2_out, c)
                free(logv2_out, c, 1)
                nc.tensor.matmul(pvar2[:, 0:N], kit.average[:, :], sq2[:, :], start=True, stop=True).then_inc(var2_mm, 1)

            def output(p, c, ready, free):
                ready(gated_out, c)
                free(stream_out, c, 1)
                nc.tensor.matmul(pout[:, 0:N], weights[:, 3, :], gated[:, :], start=True, stop=True).then_inc(out_mm, 1)

            steps(pe, project, None, None, norm, output)

        @block.scalar
        def _(act):
            open_all(act, sq_out, logv_out, rstd_out, key_out, val_out, er_out, gate_out, a2_out, b2_out, a1_out,
                     b1_out, sq2_out, logv2_out, rstd2_out, ya_out)
            act.preload_act_table_set(LN_EXP)
            act.wait_ge(rates_out, 2)

            def project(p, c, ready, free):
                ready(cen_mm, c)
                free(var_mm, c, 1)
                nc.scalar.activation(sq[:, :], pcen[:, 0:N], ACT.Square).then_inc(sq_out, 1)
                ready(var_mm, c)
                free(rstd_out, c, 1)
                nc.scalar.activation(logv[:, :], pvar[:, 0:N], ACT.Ln, bias=kit.col("eps")).then_inc(logv_out, 1)
                ready(logv_out, c)
                free(h_out, c, 1)
                nc.scalar.activation(rstd[:, :], logv[:, :], ACT.Exp, scale=-0.5).then_inc(rstd_out, 1)
                ready(k_mm, c)
                free(e1_out, c, 2)
                nc.scalar.activation(key[:, c % 2, :], pk[:, 0:N], ACT.Copy).then_inc(key_out, 1)
                ready(v_mm, c)
                free(nb_out, c, 3)
                nc.scalar.activation(val[:, c % 3, :], pv[:, 0:N], ACT.Copy).then_inc(val_out, 1)
                ready(r_mm, c)
                free(sr_out, c, 4)
                nc.scalar.activation(gate[:, c % 4, :], pr[:, 0:N], ACT.Exp, scale=-1.0).then_inc(er_out, 1)
                ready(er_out, c)
                nc.scalar.activation(gate[:, c % 4, :], gate[:, c % 4, :], ACT.Copy, bias=1.0).then_inc(gate_out, 1)

            def exponentials(p, c, ready, free):
                e = ex[:, c % 2, :, :]
                ready(d2_out, c)
                nc.scalar.activation(e[:, 0, :], e[:, 0, :], ACT.Exp, bias=decay).then_inc(a2_out, 1)
                ready(e2_out, c)
                nc.scalar.activation(e[:, 1, :], e[:, 1, :], ACT.Exp).then_inc(b2_out, 1)
                ready(d1_out, c)
                nc.scalar.activation(e[:, 2, :], e[:, 2, :], ACT.Exp).then_inc(a1_out, 1)
                ready(e1_out, c)
                nc.scalar.activation(e[:, 3, :], e[:, 3, :], ACT.Exp, bias=first).then_inc(b1_out, 1)

            def norm(p, c, ready, free):
                ready(cen2_mm, c)
                free(var2_mm, c, 1)
                nc.scalar.activation(sq2[:, :], pcen2[:, 0:N], ACT.Square).then_inc(sq2_out, 1)
                ready(var2_mm, c)
                free(rstd2_out, c, 1)
                nc.scalar.activation(logv2[:, :], pvar2[:, 0:N], ACT.Ln, bias=kit.col("eps")).then_inc(logv2_out, 1)
                ready(logv2_out, c)
                free(yn_out, c, 1)
                nc.scalar.activation(rstd2[:, :], logv2[:, :], ACT.Exp, scale=-0.5).then_inc(rstd2_out, 1)
                ready(yn_out, c)
                free(gated_out, c, 1)
                nc.scalar.activation(ya[:, :], yn[:, :], ACT.Identity, bias=kit.col("ln_b"),
                                     scale=kit.col("ln_w")).then_inc(ya_out, 1)

            steps(act, project, exponentials, None, norm)

        @block.vector
        def _(dve):
            open_all(dve, h_out, topc_out, top_out, e2_out, best_out, numc_out, num_out, denc_out, den_out,
                     numer_out, denom_out, recip_out, y_out, yn_out, sr_out, stream_out)
            for i, name in enumerate(("decay", "first")):
                nc.vector.tensor_scalar(rates[:, i:i + 1], kit.col(name), 1.0 / T, None, ALU.mult).then_inc(rates_out, 1)
            dve.wait_ge(rates_out, 2)

            def carry(state, c, start, done):
                if c == 0:
                    nc.vector.memset(state[:, 0, 0:1], start).then_inc(done, 1)
                else:
                    nc.vector.tensor_copy(state[:, c % 2, 0:1], state[:, (c - 1) % 2, N:N + 1]).then_inc(done, 1)

            def project(p, c, ready, free):
                ready(rstd_out, c)
                free(r_mm, c, 1)
                nc.vector.tensor_tensor(h[:, :], pcen[:, 0:N], rstd[:, :], ALU.mult).then_inc(h_out, 1)

            def maxima(p, c, ready, free):
                free(d1_out, c, 2)
                free(e2_out, c, 1)
                carry(top, c, -1e38, topc_out)
                ready(topc_out, c)
                ready(key_out, c)
                nc.vector.tensor_tensor_scan(top[:, c % 2, 1:N + 1], decay.broadcast_to([P, N]), key[:, c % 2, :],
                                             top[:, c % 2, 0:1], ALU.add, ALU.max).then_inc(top_out, 1)
                ready(top_out, c)
                free(e1_out, c, 1)
                nc.vector.scalar_tensor_tensor(out=best[:, :], in0=key[:, c % 2, :], scalar=first,
                                               in1=top[:, c % 2, 0:N], op0=ALU.add, op1=ALU.max).then_inc(best_out, 1)
                free(y_out, c, 2)
                nc.vector.tensor_tensor(ex[:, c % 2, 1, :], key[:, c % 2, :], top[:, c % 2, 1:N + 1],
                                        ALU.subtract).then_inc(e2_out, 1)

            def states(p, c, ready, free):
                e = ex[:, c % 2, :, :]
                free(y_out, c, 1)
                carry(den, c, 0.0, denc_out)
                carry(num, c, 0.0, numc_out)
                ready(denc_out, c)
                ready(a2_out, c)
                ready(b2_out, c)
                nc.vector.tensor_tensor_scan(den[:, c % 2, 1:N + 1], e[:, 0, :], e[:, 1, :], den[:, c % 2, 0:1],
                                             ALU.mult, ALU.add).then_inc(den_out, 1)
                ready(numc_out, c)
                ready(bv_out, c)
                nc.vector.tensor_tensor_scan(num[:, c % 2, 1:N + 1], e[:, 0, :], bv[:, :], num[:, c % 2, 0:1],
                                             ALU.mult, ALU.add).then_inc(num_out, 1)
                ready(da_out, c)
                ready(b1_out, c)
                nc.vector.tensor_tensor(denom[:, :], da[:, :], e[:, 3, :], ALU.add).then_inc(denom_out, 1)
                ready(denom_out, c)
                nc.vector.reciprocal(recip[:, :], denom[:, :]).then_inc(recip_out, 1)
                ready(na_out, c)
                ready(nb_out, c)
                nc.vector.tensor_tensor(numer[:, :], na[:, :], nb[:, :], ALU.add).then_inc(numer_out, 1)
                ready(numer_out, c)
                ready(recip_out, c)
                free(cen2_mm, c, 2)
                nc.vector.tensor_tensor(y[:, c % 2, :], numer[:, :], recip[:, :], ALU.mult).then_inc(y_out, 1)

            def norm(p, c, ready, free):
                ready(gate_out, c)
                free(gated_out, c, 1)
                nc.vector.reciprocal(sr[:, :], gate[:, c % 4, :]).then_inc(sr_out, 1)
                ready(rstd2_out, c)
                free(ya_out, c, 1)
                nc.vector.tensor_tensor(yn[:, :], pcen2[:, 0:N], rstd2[:, :], ALU.mult).then_inc(yn_out, 1)

            def output(p, c, ready, free):
                ready(out_mm, c)
                nc.vector.tensor_tensor(tokens(p, c), pout[:, 0:N], tokens(p, c), ALU.add).then_inc(stream_out, 1)

            steps(dve, project, maxima, states, norm, output)

        @block.gpsimd
        def _(gp):
            open_all(gp, d2_out, d1_out, e1_out, bv_out, na_out, nb_out, da_out, gated_out)

            def then(out, in0, in1, op, done):
                gp.sem_inc(passed, 1)
                nc.gpsimd.tensor_tensor(out, in0, in1, op).then_inc(done, 1)

            def exponents(p, c, ready, free):
                old, new = top[:, c % 2, 0:N], top[:, c % 2, 1:N + 1]
                ready(top_out, c)
                free(y_out, c, 2)
                then(ex[:, c % 2, 0, :], old, new, ALU.subtract, d2_out)
                ready(best_out, c)
                then(ex[:, c % 2, 2, :], old, best[:, :], ALU.subtract, d1_out)
                then(ex[:, c % 2, 3, :], key[:, c % 2, :], best[:, :], ALU.subtract, e1_out)

            def states(p, c, ready, free):
                e = ex[:, c % 2, :, :]
                ready(b2_out, c)
                ready(val_out, c)
                free(num_out, c, 1)
                then(bv[:, :], e[:, 1, :], val[:, c % 3, :], ALU.mult, bv_out)
                ready(b1_out, c)
                free(numer_out, c, 1)
                then(nb[:, :], e[:, 3, :], val[:, c % 3, :], ALU.mult, nb_out)
                ready(den_out, c)
                ready(a1_out, c)
                free(denom_out, c, 1)
                then(da[:, :], e[:, 2, :], den[:, c % 2, 0:N], ALU.mult, da_out)
                ready(num_out, c)
                then(na[:, :], e[:, 2, :], num[:, c % 2, 0:N], ALU.mult, na_out)

            def norm(p, c, ready, free):
                ready(ya_out, c)
                ready(sr_out, c)
                free(out_mm, c, 1)
                then(gated[:, :], ya[:, :], sr[:, :], ALU.mult, gated_out)

            steps(gp, None, exponents, states, norm)


def experts(kit):
    nc = kit.nc
    N, G = CHUNK, 2 * NBLK
    with ExitStack() as ctx:
        sb = lambda name, shape, dt=F32: ctx.enter_context(nc.sbuf_tensor(f"moe_{name}", shape, dt))
        sem = lambda name: ctx.enter_context(kit.semaphore(f"moe_{name}"))
        sems = lambda names: [sem(n) for n in names.split()]
        w1, b1, w2 = sb("w1", [P, E, FF]), sb("b1", [P, E]), sb("w2", [P, E, C])
        w2b, gate_w, gate_b = sb("w2b", [2 * E, P]), sb("gate_w", [P, 2 * E]), sb("gate_b", [P, G * E])
        gamma, beta, iota = sb("gamma", [P, C]), sb("beta", [P, C]), sb("iota", [P, E])
        xs, sq, logv, rstd = (sb(n, [P, N]) for n in ("xs", "sq", "logv", "rstd"))
        h = sb("h", [P, 2, N])
        parts = sb("parts", [P, 2, 2, N], F32R)
        w1parts = sb("w1parts", [P, 2, E, FF], F32R)
        xt, acc = sb("xt", [BLK, 2, G, C]), sb("acc", [BLK, 2, G, C])
        logits = sb("logits", [BLK, G, E])
        best, place = sb("best", [BLK, G, 8]), sb("place", [BLK, G, 8], U32)
        placef = sb("placef", [BLK, G, 2])
        gap, egap, denom, wbest, wnext = (sb(n, [BLK, G]) for n in "gap egap denom wbest wnext".split())
        is_best, is_next, part_best, part_next = (sb(n, [BLK, G, E]) for n in "is_best is_next part_best part_next".split())
        wt = sb("wt", [BLK, 2, G, E])
        wtt = sb("wtt", [2 * E, N])
        hidden = sb("hidden", [P, 2, 2, N])
        scaled = sb("scaled", [BLK, 2, G, C])
        total, mean, sqsum, flogv, frstd = (sb(n, [BLK, G]) for n in "total mean sqsum flogv frstd".split())
        dev, devsq, fnorm, fgain, fshift = (sb(n, [BLK, G, C]) for n in "dev devsq fnorm fgain fshift".split())
        result = sb("result", [BLK, 2, G, C])
        ps = lambda name, *shape: ctx.enter_context(nc.psum_tensor(f"moe_{name}", [P, *shape], F32))
        pcen, pvar, pturn, phid, pout = ps("pcen", 512), ps("pvar", 512), ps("pturn", 512), ps("phid", 3, 512), ps("pout", 2, 512)
        weights_in, passed, w1hi_out, w1lo_out, hi_out, lo_out = sems("weights_in passed w1hi_out w1lo_out hi_out lo_out")
        cen_mm, var_mm, xt_mm, logit_mm, wtt_mm, h_mm, up_mm, down_mm = sems(
            "cen_mm var_mm xt_mm logit_mm wtt_mm h_mm up_mm down_mm")
        sq_out, logv_out, rstd_out, xt_out, egap_out, wtt_out, acc_in, hidden_act, devsq_out, flogv_out, frstd_out = sems(
            "sq_out logv_out rstd_out xt_out egap_out wtt_out acc_in hidden_act devsq_out flogv_out frstd_out")
        h_out, logits_out, best_out, place_out, placef_out, gap_out, denom_out, wbest_out, wnext_out = sems(
            "h_out logits_out best_out place_out placef_out gap_out denom_out wbest_out wnext_out")
        is_out, part_out, wt_out, hidden_dve, scaled_out, total_out, mean_out, sqsum_out, fnorm_out = sems(
            "is_out part_out wt_out hidden_dve scaled_out total_out mean_out sqsum_out fnorm_out")
        xs_in, acc_out, dev_out, fgain_out, fshift_out, result_out = sems(
            "xs_in acc_out dev_out fgain_out fshift_out result_out")
        stored = sems("stored0 stored1")
        block = ctx.enter_context(nc.Block())
        WEIGHTS = (("w1", w1), ("b1", b1), ("w2", w2), ("w2b", w2b), ("gate_w", gate_w), ("gate_b", gate_b),
                   ("gamma", gamma), ("beta", beta), ("iota", iota))

        def turns(eng, body):
            body(0, 0, True, 2, 0)
            with eng.Fori(0, (CHUNKS - 3) // 2) as t:
                body(2 * t + 1, 1, False, 2, t)
                body(2 * t + 2, 0, False, 2, t)
            body(CHUNKS - 2, 1, False, 1, (CHUNKS - 3) // 2)
            body(CHUNKS - 1, 0, False, 0, (CHUNKS - 3) // 2)

        @block.sync
        def _(sp):
            for sem in stored:
                sp.sem_inc(sem, 16)
            for name, t in WEIGHTS:
                dst = t[:, :] if len(t.shape) == 2 else t[:, :, :].rearrange("p a b -> p (a b)")
                sp.dma_start(dst, kit.d[name]).then_inc(weights_in, 16)

            def body(j, buf, first, left, stores):
                sp.wait_ge(result_out, at(j, 1, 1))
                sp.dma_start(kit.out[bass.ds(j, 1), :, :].rearrange("a t c -> (a t) c"),
                             result[:, buf, :, :].rearrange("p g c -> p (g c)")).then_inc(stored[buf], 16)

            turns(sp, body)
            sp.wait_ge(stored[0], 16 * ((CHUNKS + 1) // 2) + 16)
            sp.wait_ge(stored[1], 16 * (CHUNKS // 2) + 16)

        @block.tensor
        def _(pe):
            open_all(pe, cen_mm, var_mm, xt_mm, logit_mm, wtt_mm, h_mm, up_mm, down_mm)
            pe.wait_ge(weights_in, 16 * len(WEIGHTS))
            blocks = [slice(k * BLK, (k + 1) * BLK) for k in range(NBLK)]

            def center(j):
                pe.wait_ge(xs_in, at(j, 1, 1))
                pe.wait_ge(h_out, at(j, 1, 0))
                nc.tensor.matmul(pcen[:, 0:N], kit.center[:, :], xs[:, :], start=True, stop=True).then_inc(cen_mm, 1)
                pe.wait_ge(acc_in, at(j, 1, 0))
                for k, b in enumerate(blocks):
                    done = nc.tensor.transpose(pturn[0:BLK, k * P:(k + 1) * P], xs[:, b], kit.ident[:, :])
                done.then_inc(xt_mm, 1)

            def variance(j):
                pe.wait_ge(sq_out, at(j, 1, 1))
                pe.wait_ge(wtt_out, at(j, 1, 0))
                nc.tensor.matmul(pvar[:, 0:N], kit.average[:, :], sq[:, :], start=True, stop=True).then_inc(var_mm, 1)

            def gate(j, buf):
                pe.wait_ge(h_out, at(j, 1, 1))
                pe.wait_ge(logv_out, at(j, 1, 1))
                for k, b in enumerate(blocks):
                    done = nc.tensor.matmul(pvar[0:BLK, k * 2 * E:(k + 1) * 2 * E], h[:, buf, b], gate_w[:, :],
                                            start=True, stop=True)
                done.then_inc(logit_mm, 1)

            def turn_weights(j, buf):
                pe.wait_ge(wt_out, at(j, 1, 1))
                pe.wait_ge(logits_out, at(j, 1, 1))
                for k, b in enumerate(blocks):
                    done = nc.tensor.transpose(pvar[0:2 * E, b], wt[:, buf, 2 * k:2 * k + 2, :].rearrange("p g e -> p (g e)"),
                                               kit.ident[0:BLK, 0:BLK])
                done.then_inc(wtt_mm, 1)

            def start_sum(j, buf):
                pe.wait_ge(wtt_out, at(j, 1, 1))
                pe.wait_ge(xt_out, at(j, 1, 1))
                for k, b in enumerate(blocks):
                    dst = pturn[0:BLK, k * P:(k + 1) * P]
                    nc.tensor.matmul(dst, h[:, buf, b], kit.ident[:, :], start=True, stop=False)
                    done = nc.tensor.matmul(dst, wtt[:, b], w2b[:, :], start=False, stop=True)
                done.then_inc(h_mm, 1)

            def up(j, buf, e):
                if e == 0:
                    pe.wait_ge(hi_out, at(j, 2, 2))
                    pe.wait_ge(lo_out, at(j, 2, 2))
                for b in (0, 1):
                    i = 2 * e + b
                    if i < 3:
                        pe.wait_ge(hidden_act, at(j, E, 0))
                        pe.wait_ge(hidden_dve, at(j, E, 0))
                    else:
                        pe.wait_ge((hidden_act, hidden_dve)[(i - 3) % 2], at(j, E, (i - 3) // 2 + 1))
                    nc.tensor.matmul(phid[:, i % 3, 0:N], w1parts[:, 0, e, :], parts[:, buf, b, :], start=True, stop=False)
                    nc.tensor.matmul(phid[:, i % 3, 0:N], w1parts[:, 1, e, :], parts[:, buf, b, :],
                                     start=False, stop=True).then_inc(up_mm, 1)

            def down(j, e):
                pe.wait_ge(scaled_out, at(j, E, e - 1))
                for b in (0, 1):
                    pe.wait_ge((hidden_act, hidden_dve)[b], at(j, E, e + 1))
                    for k, blk in enumerate(blocks):
                        g = 2 * k + b
                        done = nc.tensor.matmul(pout[0:BLK, e % 2, g * C:(g + 1) * C], hidden[:, e % 2, b, blk],
                                                w2[:, e, :], start=True, stop=True)
                done.then_inc(down_mm, 1)

            def ahead(e, j, buf):
                if e == 0:
                    center(j)
                if e == 1:
                    variance(j)
                if e == 3:
                    gate(j, buf)
                if e == 11:
                    turn_weights(j, buf)
                if e == 14:
                    start_sum(j, buf)

            for e in range(E):
                ahead(e, 0, 0)
            pe.wait_ge(w1lo_out, 1)

            def body(j, buf, first, left, stores):
                for e in range(E + 1):
                    if e < E:
                        up(j, buf, e)
                        if left:
                            ahead(e, j + 1, 1 - buf)
                    if e > 0:
                        down(j, e - 1)

            turns(pe, body)

        @block.scalar
        def _(act):
            open_all(act, sq_out, logv_out, rstd_out, xt_out, egap_out, wtt_out, acc_in, hidden_act, devsq_out,
                     flogv_out, frstd_out, hi_out)
            act.preload_act_table_set(LN_EXP)
            act.wait_ge(weights_in, 16 * len(WEIGHTS))
            nc.scalar.activation(w1parts[:, 0, :, :], w1[:, :, :], ACT.Copy).then_inc(w1hi_out, 1)

            def ahead(e, j, buf):
                if e == 0:
                    act.wait_ge(cen_mm, at(j, 1, 1))
                    act.wait_ge(var_mm, at(j, 1, 0))
                    nc.scalar.activation(sq[:, :], pcen[:, 0:N], ACT.Square).then_inc(sq_out, 1)
                if e == 2:
                    act.wait_ge(var_mm, at(j, 1, 1))
                    act.wait_ge(rstd_out, at(j, 1, 0))
                    nc.scalar.activation(logv[:, :], pvar[:, 0:N], ACT.Ln, bias=kit.col("eps")).then_inc(logv_out, 1)
                    act.wait_ge(logv_out, at(j, 1, 1))
                    act.wait_ge(h_out, at(j, 1, 0))
                    nc.scalar.activation(rstd[:, :], logv[:, :], ACT.Exp, scale=-0.5).then_inc(rstd_out, 1)
                if e == 3:
                    act.wait_ge(h_out, at(j, 1, 1))
                    act.wait_ge(up_mm, at(j, 2 * E, -2 * E))
                    for b in (0, 1):
                        half = slice(C * b, C * b + C)
                        nc.scalar.activation(parts[half, buf, b, :], h[half, buf, :], ACT.Copy).then_inc(hi_out, 1)
                if e == 9:
                    act.wait_ge(gap_out, at(j, 1, 1))
                    act.wait_ge(wnext_out, at(j, 1, 0))
                    nc.scalar.activation(egap[:, :], gap[:, :], ACT.Exp).then_inc(egap_out, 1)
                if e == 12:
                    act.wait_ge(xt_mm, at(j, 1, 1))
                    act.wait_ge(result_out, at(j, 1, -1))
                    nc.scalar.activation(xt[:, buf, :, :].rearrange("p g c -> p (g c)"), pturn[0:BLK, :],
                                         ACT.Copy).then_inc(xt_out, 1)
                    act.wait_ge(wtt_mm, at(j, 1, 1))
                    act.wait_ge(h_mm, at(j, 1, 0))
                    nc.scalar.activation(wtt[:, :], pvar[0:2 * E, 0:N], ACT.Copy).then_inc(wtt_out, 1)
                if e == 15:
                    act.wait_ge(h_mm, at(j, 1, 1))
                    act.wait_ge(dev_out, at(j, 1, -1))
                    nc.scalar.activation(acc[:, buf, :, :].rearrange("p g c -> p (g c)"), pturn[0:BLK, :],
                                         ACT.Copy).then_inc(acc_in, 1)

            def finish(e, j):
                if e == 4:
                    act.wait_ge(dev_out, at(j, 1, 1))
                    act.wait_ge(sqsum_out, at(j, 1, 0))
                    nc.scalar.activation(devsq[:, :, :], dev[:, :, :], ACT.Square).then_inc(devsq_out, 1)
                if e == 6:
                    act.wait_ge(sqsum_out, at(j, 1, 1))
                    act.wait_ge(frstd_out, at(j, 1, 0))
                    nc.scalar.activation(flogv[:, :], sqsum[:, :], ACT.Ln, bias=kit.cols[0:BLK, CI["eps"]:CI["eps"] + 1],
                                         scale=1.0 / C).then_inc(flogv_out, 1)
                    act.wait_ge(flogv_out, at(j, 1, 1))
                    act.wait_ge(fnorm_out, at(j, 1, 0))
                    nc.scalar.activation(frstd[:, :], flogv[:, :], ACT.Exp, scale=-0.5).then_inc(frstd_out, 1)

            for e in range(E):
                ahead(e, 0, 0)

            def body(j, buf, first, left, stores):
                for e in range(E):
                    i = 2 * e
                    act.wait_ge(up_mm, at(j, 2 * E, i + 1))
                    act.wait_ge(down_mm, at(j, E, e - 1))
                    nc.scalar.activation(hidden[:, e % 2, 0, :], phid[:, i % 3, 0:N], ACT.Relu,
                                         bias=b1[:, e:e + 1]).then_inc(hidden_act, 1)
                    if left:
                        ahead(e, j + 1, 1 - buf)
                    if not first:
                        finish(e, j - 1)

            turns(act, body)
            for e in range(E):
                finish(e, CHUNKS - 1)

        @block.vector
        def _(dve):
            open_all(dve, h_out, logits_out, best_out, place_out, placef_out, gap_out, denom_out, wbest_out, wnext_out,
                     is_out, part_out, wt_out, hidden_dve, scaled_out, total_out, mean_out, sqsum_out, fnorm_out, lo_out)
            dve.wait_ge(weights_in, 16 * len(WEIGHTS))
            dve.wait_ge(w1hi_out, 1)
            nc.vector.tensor_tensor(w1parts[:, 1, :, :], w1[:, :, :], w1parts[:, 0, :, :].bitcast(F32),
                                    ALU.subtract).then_inc(w1lo_out, 1)
            wide = lambda t: t.unsqueeze(2).broadcast_to([BLK, G, E])

            def settled():
                dve.sem_inc(passed, 1)

            def ahead(e, j, buf):
                if e == 2:
                    dve.wait_ge(rstd_out, at(j, 1, 1))
                    dve.wait_ge(h_mm, at(j, 1, -1))
                    dve.wait_ge(up_mm, at(j, 2 * E, -2 * E))
                    nc.vector.tensor_tensor(h[:, buf, :], pcen[:, 0:N], rstd[:, :], ALU.mult).then_inc(h_out, 1)
                if e == 4:
                    dve.wait_ge(logit_mm, at(j, 1, 1))
                    dve.wait_ge(place_out, at(j, G, 0))
                    nc.vector.tensor_tensor(logits[:, :, :].rearrange("p g e -> p (g e)"), pvar[0:BLK, 0:G * E],
                                            gate_b[0:BLK, :], ALU.add).then_inc(logits_out, 1)
                    dve.wait_ge(logits_out, at(j, 1, 1))
                    dve.wait_ge(gap_out, at(j, 1, 0))
                    settled()
                    for g in range(G):
                        nc.vector.max(best[:, g, :], logits[:, g, :]).then_inc(best_out, 1)
                if e == 8:
                    dve.wait_ge(hi_out, at(j, 2, 2))
                    dve.wait_ge(up_mm, at(j, 2 * E, -2 * E))
                    for b in (0, 1):
                        half, other = slice(C * b, C * b + C), slice(C - C * b, P - C * b)
                        nc.vector.tensor_tensor(parts[other, buf, b, :], h[half, buf, :], parts[half, buf, b, :].bitcast(F32),
                                                ALU.subtract).then_inc(lo_out, 1)
                if e == 5:
                    dve.wait_ge(best_out, at(j, G, G))
                    dve.wait_ge(placef_out, at(j, 1, 0))
                    settled()
                    for g in range(G):
                        nc.vector.max_index(place[:, g, :], best[:, g, :], logits[:, g, :]).then_inc(place_out, 1)
                if e == 6:
                    dve.wait_ge(egap_out, at(j, 1, 0))
                    nc.vector.tensor_tensor(gap[:, :], best[:, :, 1], best[:, :, 0], ALU.subtract).then_inc(gap_out, 1)
                    dve.wait_ge(place_out, at(j, G, G))
                    dve.wait_ge(is_out, at(j, 2, 0))
                    nc.vector.tensor_copy(placef[:, :, :], place[:, :, 0:2]).then_inc(placef_out, 1)
                if e == 7:
                    dve.wait_ge(placef_out, at(j, 1, 1))
                    dve.wait_ge(part_out, at(j, 2, 0))
                    for which, t in enumerate((is_best, is_next)):
                        nc.vector.tensor_tensor(t[:, :, :], iota[0:BLK, :].unsqueeze(1).broadcast_to([BLK, G, E]),
                                                wide(placef[:, :, which]), ALU.is_equal).then_inc(is_out, 1)
                if e == 9:
                    dve.wait_ge(egap_out, at(j, 1, 1))
                    dve.wait_ge(wbest_out, at(j, 1, 0))
                    nc.vector.tensor_scalar(denom[:, :], egap[:, :], 1.0, None, ALU.add).then_inc(denom_out, 1)
                    dve.wait_ge(denom_out, at(j, 1, 1))
                    dve.wait_ge(part_out, at(j, 2, 0))
                    nc.vector.reciprocal(wbest[:, :], denom[:, :]).then_inc(wbest_out, 1)
                    dve.wait_ge(wbest_out, at(j, 1, 1))
                    nc.vector.tensor_tensor(wnext[:, :], egap[:, :], wbest[:, :], ALU.mult).then_inc(wnext_out, 1)
                if e == 10:
                    dve.wait_ge(wnext_out, at(j, 1, 1))
                    dve.wait_ge(is_out, at(j, 2, 2))
                    dve.wait_ge(wt_out, at(j, 1, 0))
                    nc.vector.tensor_tensor(part_best[:, :, :], is_best[:, :, :], wide(wbest[:, :]), ALU.mult).then_inc(part_out, 1)
                    nc.vector.tensor_tensor(part_next[:, :, :], is_next[:, :, :], wide(wnext[:, :]), ALU.mult).then_inc(part_out, 1)
                    dve.wait_ge(part_out, at(j, 2, 2))
                    dve.wait_ge(scaled_out, at(j, E, -E))
                    dve.wait_ge(wtt_mm, at(j, 1, -1))
                    nc.vector.tensor_tensor(wt[:, buf, :, :], part_best[:, :, :], part_next[:, :, :], ALU.add).then_inc(wt_out, 1)

            def finish(e, j, buf):
                if e == 1:
                    dve.wait_ge(acc_out, at(j, E, E))
                    dve.wait_ge(mean_out, at(j, 1, 0))
                    nc.vector.tensor_reduce(total[:, :], acc[:, buf, :, :], AX_X, ALU.add).then_inc(total_out, 1)
                    dve.wait_ge(total_out, at(j, 1, 1))
                    dve.wait_ge(dev_out, at(j, 1, 0))
                    nc.vector.tensor_scalar(mean[:, :], total[:, :], 1.0 / C, None, ALU.mult).then_inc(mean_out, 1)
                if e == 5:
                    dve.wait_ge(devsq_out, at(j, 1, 1))
                    dve.wait_ge(flogv_out, at(j, 1, 0))
                    nc.vector.tensor_reduce(sqsum[:, :], devsq[:, :, :], AX_X, ALU.add).then_inc(sqsum_out, 1)
                if e == 7:
                    dve.wait_ge(frstd_out, at(j, 1, 1))
                    dve.wait_ge(fgain_out, at(j, 1, 0))
                    nc.vector.tensor_tensor(fnorm[:, :, :], dev[:, :, :],
                                            frstd[:, :].unsqueeze(2).broadcast_to([BLK, G, C]), ALU.mult).then_inc(fnorm_out, 1)

            for e in range(E):
                ahead(e, 0, 0)

            def body(j, buf, first, left, stores):
                for e in range(E + 1):
                    if e < E:
                        i = 2 * e + 1
                        dve.wait_ge(up_mm, at(j, 2 * E, i + 1))
                        dve.wait_ge(down_mm, at(j, E, e - 1))
                        nc.vector.tensor_scalar(hidden[:, e % 2, 1, :], phid[:, i % 3, 0:N], b1[:, e:e + 1], 0.0,
                                                ALU.add, ALU.max).then_inc(hidden_dve, 1)
                    if e > 0:
                        f = e - 1
                        dve.wait_ge(down_mm, at(j, E, f + 1))
                        dve.wait_ge(acc_out, at(j, E, f - 1))
                        nc.vector.tensor_tensor(scaled[:, f % 2, :, :], pout[0:BLK, f % 2, :].rearrange("p (g c) -> p g c", c=C),
                                                wt[:, buf, :, f].unsqueeze(2).broadcast_to([BLK, G, C]),
                                                ALU.mult).then_inc(scaled_out, 1)
                    if e < E and left:
                        ahead(e, j + 1, 1 - buf)
                    if e < E and not first:
                        finish(e, j - 1, 1 - buf)

            turns(dve, body)
            for e in range(E):
                finish(e, CHUNKS - 1, 0)

        @block.gpsimd
        def _(gp):
            open_all(gp, xs_in, acc_out, dev_out, fgain_out, fshift_out, result_out)
            gp.wait_ge(weights_in, 16 * len(WEIGHTS))
            flat = kit.stream[:, :, :].rearrange("p n t -> p (n t)")

            def settled():
                gp.sem_inc(passed, 1)

            def copy_tokens(j):
                gp.wait_ge(xt_mm, at(j, 1, 0))
                settled()
                nc.gpsimd.tensor_copy(xs[:, :], flat[:, bass.ds(j * N, N)]).then_inc(xs_in, 1)

            def finish(e, j, buf, stores):
                if e == 1:
                    gp.wait_ge(mean_out, at(j, 1, 1))
                    gp.wait_ge(fnorm_out, at(j, 1, 0))
                    settled()
                    nc.gpsimd.tensor_tensor(dev[:, :, :], acc[:, buf, :, :],
                                            mean[:, :].unsqueeze(2).broadcast_to([BLK, G, C]), ALU.subtract).then_inc(dev_out, 1)
                if e == 8:
                    gp.wait_ge(fnorm_out, at(j, 1, 1))
                    gp.wait_ge(fshift_out, at(j, 1, 0))
                    settled()
                    nc.gpsimd.tensor_tensor(fgain[:, :, :], fnorm[:, :, :],
                                            gamma[0:BLK, :].unsqueeze(1).broadcast_to([BLK, G, C]), ALU.mult).then_inc(fgain_out, 1)
                if e == 9:
                    gp.wait_ge(fgain_out, at(j, 1, 1))
                    gp.wait_ge(result_out, at(j, 1, 0))
                    settled()
                    nc.gpsimd.tensor_tensor(fshift[:, :, :], fgain[:, :, :],
                                            beta[0:BLK, :].unsqueeze(1).broadcast_to([BLK, G, C]), ALU.add).then_inc(fshift_out, 1)
                if e == 10:
                    gp.wait_ge(fshift_out, at(j, 1, 1))
                    gp.wait_ge(stored[buf], 16 * stores + 16)
                    settled()
                    nc.gpsimd.tensor_tensor(result[:, buf, :, :], fshift[:, :, :], xt[:, buf, :, :], ALU.add).then_inc(result_out, 1)

            copy_tokens(0)
            copy_tokens(1)

            def body(j, buf, first, left, stores):
                for e in range(E):
                    if e == 5 and left == 2:
                        copy_tokens(j + 2)
                    gp.wait_ge(scaled_out, at(j, E, e + 1))
                    gp.wait_ge(acc_out, at(j, E, e))
                    if e == 0:
                        gp.wait_ge(acc_in, at(j, 1, 1))
                    settled()
                    nc.gpsimd.tensor_tensor(acc[:, buf, :, :], acc[:, buf, :, :], scaled[:, e % 2, :, :],
                                            ALU.add).then_inc(acc_out, 1)
                    if not first:
                        finish(e, j - 1, 1 - buf, stores)

            turns(gp, body)
            for e in range(E):
                finish(e, CHUNKS - 1, 0, CHUNKS // 2)


STAGES = [(embed,), (window_attention, 0), (mlp, 0), (window_attention, 1), (mlp, 1), (time_mix,), (experts,)]


def build(nc, d, out):
    with ExitStack() as ctx:
        kit = Kit(nc, ctx, d)
        kit.out = out
        setup(kit)
        kit.clear()
        for stage, *args in STAGES:
            stage(kit, *args)
            kit.clear()

def block_diag(m):
    z = np.zeros((2 * m.shape[0], 2 * m.shape[1]), m.dtype)
    z[:m.shape[0], :m.shape[1]] = m
    z[m.shape[0]:, m.shape[1]:] = m
    return z


def stack2(m):
    return np.concatenate([m, m], axis=0)


def shape_constants():
    f = np.float32
    average = block_diag(np.full((C, C), 1.0 / C, f))
    center = np.eye(P, dtype=f) - average
    row = np.arange(P)[:, None]
    fold = ((row % QPAD) == np.arange(WIN)[None, :]).astype(f)
    headmask = ((row % C) // HD == np.arange(NH)[None, :]).astype(f)
    dup = (np.arange(2 * WIN) // WIN)[:, None]
    vmask = (dup == (np.arange(4 * P)[None, :] // HD) % 2).astype(f)
    vones = np.tile((dup == np.arange(2)[None, :]).astype(f), (1, 2 * GROUPS))
    img = np.zeros((SIDE, SIDE), np.int32)
    n = 0
    for h in (slice(0, -WS), slice(-WS, -SHIFT), slice(-SHIFT, None)):
        for w in (slice(0, -WS), slice(-WS, -SHIFT), slice(-SHIFT, None)):
            n += 1
            img[h, w] = n
    mw = img.reshape(NWIN, WS, NWIN, WS).transpose(0, 2, 1, 3).reshape(NWIN, NWIN, WIN)
    amask = np.zeros((P, 4, NH, WIN), f)
    for kind in range(4):
        m = mw[NWIN - 1 if kind // 2 else 0, NWIN - 1 if kind % 2 else 0]
        a = np.where(m[None, :] != m[:, None], -100.0, 0.0).astype(f)
        for b in (0, 1):
            amask[QPAD * b:QPAD * b + WIN, kind] = a[:, None, :]
    iota = np.broadcast_to(np.arange(E, dtype=f), (P, E)).copy()
    power = np.array([pow(31, j, TBL) for j in range(HIST)], f)
    return dict(average=average, center=center, ident=np.eye(P, dtype=f), fold=fold, headmask=headmask,
                vmask=vmask, vones=vones, amask=amask.reshape(P, -1), iota=iota,
                hashes=np.broadcast_to(np.tile(power, TXT_COLS), (TXT_P, TXT_COLS * HIST)).copy(),
                fresh=np.broadcast_to(np.tile((np.arange(HIST) > 0).astype(f), TXT_COLS),
                                      (TXT_P, TXT_COLS * HIST)).copy(),
                tablebase=np.broadcast_to(np.tile(np.arange(SIZES, dtype=f) * (TBL + 1), TXT_COLS),
                                          (TXT_P, TXT_COLS * SIZES)).copy())


def lay_out(i):
    a = {k.replace("L0_", ""): np.asarray(v) for k, v in i.items()}
    f = np.float32
    d = shape_constants()
    d["patches"] = a["x"].reshape(PAIRS, 2, SIDE, 4, SIDE, 4).transpose(1, 3, 5, 0, 2, 4).reshape(32, PAIRS * NIMG)
    d["pe_w"] = block_diag(a["tok_pe_w"].reshape(C, 16).T)
    cols = {"pe_b": a["tok_pe_b"], "pe_ng": a["tok_pe_ng"], "pe_nb": a["tok_pe_nb"],
            "decay": a["attn_spatial_decay"], "first": a["attn_spatial_first"],
            "eps": np.full(C, EPS, f), "ln_w": a["attn_ln_w"], "ln_b": a["attn_ln_b"]}
    coords = np.stack(np.meshgrid(np.arange(WS), np.arange(WS), indexing="ij")).reshape(2, -1)
    rel = (coords[:, :, None] - coords[:, None, :]) + WS - 1
    rpi = rel[0] * (2 * WS - 1) + rel[1]
    for l in (0, 1):
        for n in ("n1g", "n1b", "n2g", "n2b", "b2"):
            cols[f"{n}{l}"] = a[f"tok_{n}"][l]
        qkvb = a["tok_qkv_b"][l].reshape(3, C)
        cols[f"bq{l}"], cols[f"bk{l}"], cols[f"bv{l}"] = qkvb
        cols[f"bp{l}"] = a["tok_proj_b"][l]
        cols[f"b1lo{l}"], cols[f"b1hi{l}"] = a["tok_b1"][l].reshape(2, P)
        qkvw = a["tok_qkv_w"][l].reshape(3, C, C)
        wq, wk, wv, wp = (block_diag(m.T) for m in (*qkvw, a["tok_proj_w"][l]))
        wv = wv.reshape(P, 2, GROUPS, 2 * HD).transpose(0, 2, 1, 3).reshape(P, P)
        d[f"attn_w{l}"] = np.concatenate([wq, wk, wv, wp], axis=1)
        bias = np.zeros((P, NH, WIN), f)
        table = a["tok_rpb"][l][rpi].transpose(0, 2, 1)
        for b in (0, 1):
            bias[QPAD * b:QPAD * b + WIN] = table
        d[f"relbias{l}"] = bias.reshape(P, -1)
        d[f"up{l}"] = stack2(a["tok_w1"][l].T)
        down = np.zeros((P, 2, 2, P), f)
        for half in (0, 1):
            for b in (0, 1):
                down[:, half, b, C * b:C * b + C] = a["tok_w2"][l][:, P * half:P * half + P].T
        d[f"down{l}"] = down.reshape(P, -1)
    d["cols"] = np.stack([v if v.shape[0] == P else np.concatenate([v, v]) for v in (cols[n] for n in COLS)], axis=1)
    d["mix_w"] = np.concatenate([block_diag(a[f"attn_W{n}"].T) for n in "kvro"], axis=1)
    d["gate_w"] = block_diag(a["ffn_gate_w"])
    d["gate_b"] = np.broadcast_to(np.tile(a["ffn_gate_b"], 2 * NBLK), (P, 2 * NBLK * E)).copy()
    d["w1"] = stack2(a["ffn_w1"].transpose(1, 0, 2).reshape(C, E * FF))
    d["b1"] = a["ffn_b1"].T
    d["w2"] = a["ffn_w2"].transpose(1, 0, 2).reshape(FF, E * C)
    d["w2b"] = block_diag(a["ffn_b2"])
    d["gamma"] = np.broadcast_to(a["ffn_gamma"], (P, C)).copy()
    d["beta"] = np.broadcast_to(a["ffn_beta"], (P, C)).copy()
    txt = a["x_txt"]
    padded = np.concatenate([np.zeros((B, HIST - 1), txt.dtype), txt], axis=1)
    history = np.stack([padded[:, HIST - 1 - j:HIST - 1 - j + NTXT] for j in range(HIST)], axis=2)
    d["history"] = history.reshape(TXT_COLS, TXT_P, HIST).transpose(1, 0, 2).reshape(TXT_P, TXT_COLS * HIST)
    d["tables"] = a["txt_tables"].reshape(SIZES * (TBL + 1), C)
    return {k: np.ascontiguousarray(v) for k, v in d.items()}


def kernel(**inputs):
    import concourse.bacc as bacc
    from concourse.bass_utils import run_bass_kernel_spmd

    data = lay_out(inputs)
    nc = bacc.Bacc("TRN2", target_bir_lowering=False, num_devices=1)
    d = {k: nc.dram_tensor("in_" + k, data[k].shape, mybir.dt.from_np(data[k].dtype), kind="ExternalInput").ap() for k in data}
    out = nc.dram_tensor("fused_out", [CHUNKS, BLK, NBLK * P], F32, kind="ExternalOutput").ap()
    build(nc, d, out)
    got = run_bass_kernel_spmd(nc, [{"in_" + k: data[k] for k in data}], core_ids=[0]).results[0]["fused_out"]
    y = got.reshape(CHUNKS, BLK, NBLK, 2, C).transpose(3, 0, 2, 1, 4).reshape(2, PAIRS, T, C)
    return np.ascontiguousarray(y.transpose(1, 0, 2, 3).reshape(B, T, C))
```
